# Optimizing a Trainium2 kernel written in Bass

```python
import numpy as np
import jax
import jax.numpy as jnp

def _softmax(x, axis=-1):
    return jax.nn.softmax(x, axis=axis)

def _gelu(x):
    return jax.nn.gelu(x, approximate=True)

def _silu(x):
    return jax.nn.silu(x)

def _sigmoid(x):
    return jax.nn.sigmoid(x)

def _layernorm(x, axis=-1, eps=1e-05):
    m = jnp.mean(x, axis=axis, keepdims=True)
    v = jnp.var(x, axis=axis, keepdims=True)
    return (x - m) / jnp.sqrt(v + eps)

def _scatter_add(tgt, idx, src, axis=0):
    return tgt.at[idx].add(src)

def _segment_sum(src, seg, n):
    return jax.ops.segment_sum(src, seg, n)
kernel_name = 'mk_cond_seq_d2_seqx_r8_2f1e09'

def setup_inputs(seed: int=0):
    np.random.seed(seed)
    _w = jnp.asarray

    def _rec_inputs():
        import jax
        import jax.numpy as jnp
        _rk = jax.random.key(seed)
        x = -0.0002928 + 1 * jax.random.normal(jax.random.fold_in(_rk, 1), (16, 128, 128), jnp.float32)
        _lenS = 128 - jax.random.randint(jax.random.fold_in(_rk, 7), (16,), 0, max(1, 128 // 4) + 1, jnp.int32)
        _lenS2 = 128 - jax.random.randint(jax.random.fold_in(_rk, 8), (16,), 0, max(1, 128 // 4) + 1, jnp.int32)
        cond_1024 = 0.000887014 + 1.03683 * jax.random.normal(jax.random.fold_in(_rk, 11), (16, 128), jnp.float32)
        _validS = jnp.arange(128)[None, :] < _lenS[:, None]
        _validS2 = jnp.arange(128)[None, :] < _lenS2[:, None]
        _causal = jnp.tril(jnp.ones((128, 128), dtype=bool))
        mask_BxS_bf0 = jnp.logical_not(jnp.ones((16, 128), dtype=bool))
        mask_BxSxSx11_ik0 = jnp.where(jnp.ones((16, 128, 128, 11), dtype=bool), 0, 1).astype(jnp.int32)
        return (x, cond_1024, mask_BxS_bf0, mask_BxSxSx11_ik0)
    x, cond_1024, mask_BxS_bf0, mask_BxSxSx11_ik0 = _rec_inputs()

    def _L0_cond_setup():
        import math
        import jax, jax.numpy as jnp
        import numpy as np
        H = 128
        NH = 16
        HD = H // NH
        CD = 128
        MLP = 512
        EPS = 1e-05

        def _layernorm(x):
            mu = jnp.mean(x, axis=-1, keepdims=True)
            var = jnp.var(x, axis=-1, keepdims=True)
            return (x - mu) * jax.lax.rsqrt(var + EPS)

        def _adaln(x, cond, W, b):
            ss = cond @ W.T + b
            scale, shift = jnp.split(ss, 2, axis=-1)
            return _layernorm(x) * (1.0 + scale[:, None, :]) + shift[:, None, :]
        key = jax.random.key(seed)
        ks = jax.random.split(key, 16)
        s = 0.02
        inp = {'x': jax.random.normal(ks[0], (2, 256, H), jnp.float32), 'cond': jax.random.normal(ks[1], (2, CD), jnp.float32), 'key_padding_mask': jnp.zeros((2, 256), dtype=bool), 'w_adaln1': jax.random.normal(ks[2], (2 * H, CD), jnp.float32) * s, 'b_adaln1': jnp.zeros((2 * H,), jnp.float32), 'w_adaln2': jax.random.normal(ks[3], (2 * H, CD), jnp.float32) * s, 'b_adaln2': jnp.zeros((2 * H,), jnp.float32), 'wq': jax.random.normal(ks[4], (H, H), jnp.float32) * s, 'bq': jnp.zeros((H,), jnp.float32), 'wk': jax.random.normal(ks[5], (H, H), jnp.float32) * s, 'bk': jnp.zeros((H,), jnp.float32), 'wv': jax.random.normal(ks[6], (H, H), jnp.float32) * s, 'bv': jnp.zeros((H,), jnp.float32), 'wo': jax.random.normal(ks[7], (H, H), jnp.float32) * s, 'bo': jnp.zeros((H,), jnp.float32), 'w1': jax.random.normal(ks[8], (MLP, H), jnp.float32) * s, 'b1': jnp.zeros((MLP,), jnp.float32), 'w2': jax.random.normal(ks[9], (H, MLP), jnp.float32) * s, 'b2': jnp.zeros((H,), jnp.float32)}
        return inp
    _L0_cond_all = _L0_cond_setup()
    _L0_cond_in = {k: v for k, v in _L0_cond_all.items() if k in ('w_adaln1', 'b_adaln1', 'w_adaln2', 'b_adaln2', 'wq', 'bq', 'wk', 'bk', 'wv', 'bv', 'wo', 'bo', 'w1', 'b1', 'w2', 'b2')}
    del _L0_cond_all

    def _L1_cond_setup():
        import jax, jax.numpy as jnp
        import numpy as np
        NONGT = 20
        H = 16
        NEG = -9000000000000000.0

        def _gat_attention(self_feat, cond_adj, label_bias, Wq, bq, Wk, bk, Wout, bout):
            B, N, F = self_feat.shape
            ng = min(NONGT, N)
            dh = F // H
            kv = self_feat[:, :ng]
            qh = (self_feat @ Wq.T + bq).reshape(B, N, H, dh)
            kh = (kv @ Wk.T + bk).reshape(B, ng, H, dh)
            aff = jnp.einsum('bnhd,bmhd->bnhm', qh, kh) * (1.0 / np.sqrt(dh))
            mask = cond_adj[:, :, None, :] > 0
            aff = jnp.where(mask, aff, NEG) + label_bias[:, :, None, :]
            w = jax.nn.softmax(aff, axis=-1)
            out_t = jnp.einsum('bnhm,bmf->bnhf', w, kv)
            out = jnp.einsum('bnhf,hgf->bnhg', out_t, Wout) + bout.reshape(H, F // H)
            return out.reshape(B, N, F)

        def _forward(v, q, adj, W_self, b_self, w_bias, b_bias, Wq, bq, Wk, bk, Wout, bout):
            adj_f = adj.astype(jnp.float32)
            exp_v = v
            row_zero = exp_v.sum(-1) == 0
            q_exp = jnp.where(row_zero[..., None], 0.0, q[:, None, :])
            vcq = jnp.concatenate([exp_v, q_exp], axis=-1)
            self_feat = vcq @ W_self.T + b_self
            output = self_feat
            for d in range(2):
                A = adj_f if d == 0 else jnp.swapaxes(adj_f, 1, 2)
                A = A[:, :, :NONGT, :]
                cond = A.sum(-1)
                vb = A @ w_bias + b_bias
                output = output + _gat_attention(self_feat, cond, vb, Wq[d], bq[d], Wk[d], bk[d], Wout[d], bout[d])
            rel = jax.nn.relu(output)
            return exp_v + rel
        key = jax.random.key(seed)
        ks = jax.random.split(key, 8)
        B, N, L, F, Q = (32, 36, 11, 128, 128)
        IN = F + Q
        s = 0.02
        return {'v': jax.random.normal(ks[0], (B, N, F), jnp.float32), 'q': jax.random.normal(ks[1], (B, Q), jnp.float32), 'adj': jax.random.randint(ks[2], (B, N, N, L), 0, 2, jnp.int32), 'W_self': jax.random.normal(ks[3], (F, IN), jnp.float32) * s, 'b_self': jnp.zeros((F,), jnp.float32), 'w_bias': jax.random.normal(ks[4], (L,), jnp.float32) * s, 'b_bias': jnp.zeros((), jnp.float32), 'Wq': jax.random.normal(ks[5], (2, F, F), jnp.float32) * s, 'bq': jnp.zeros((2, F), jnp.float32), 'Wk': jax.random.normal(ks[6], (2, F, F), jnp.float32) * s, 'bk': jnp.zeros((2, F), jnp.float32), 'Wout': jax.random.normal(ks[7], (2, H, F // H, F), jnp.float32) * s, 'bout': jnp.zeros((2, F), jnp.float32)}
    _L1_cond_all = _L1_cond_setup()
    _L1_cond_in = {k: v for k, v in _L1_cond_all.items() if k in ('W_self', 'b_self', 'w_bias', 'b_bias', 'Wq', 'bq', 'Wk', 'bk', 'Wout', 'bout')}
    del _L1_cond_all
    return {'x': x, 'cond_1024': cond_1024, 'mask_BxS_bf0': mask_BxS_bf0, 'mask_BxSxSx11_ik0': mask_BxSxSx11_ik0, 'L0_cond_w_adaln1': _L0_cond_in['w_adaln1'], 'L0_cond_b_adaln1': _L0_cond_in['b_adaln1'], 'L0_cond_w_adaln2': _L0_cond_in['w_adaln2'], 'L0_cond_b_adaln2': _L0_cond_in['b_adaln2'], 'L0_cond_wq': _L0_cond_in['wq'], 'L0_cond_bq': _L0_cond_in['bq'], 'L0_cond_wk': _L0_cond_in['wk'], 'L0_cond_bk': _L0_cond_in['bk'], 'L0_cond_wv': _L0_cond_in['wv'], 'L0_cond_bv': _L0_cond_in['bv'], 'L0_cond_wo': _L0_cond_in['wo'], 'L0_cond_bo': _L0_cond_in['bo'], 'L0_cond_w1': _L0_cond_in['w1'], 'L0_cond_b1': _L0_cond_in['b1'], 'L0_cond_w2': _L0_cond_in['w2'], 'L0_cond_b2': _L0_cond_in['b2'], 'L1_cond_W_self': _L1_cond_in['W_self'], 'L1_cond_b_self': _L1_cond_in['b_self'], 'L1_cond_w_bias': _L1_cond_in['w_bias'], 'L1_cond_b_bias': _L1_cond_in['b_bias'], 'L1_cond_Wq': _L1_cond_in['Wq'], 'L1_cond_bq': _L1_cond_in['bq'], 'L1_cond_Wk': _L1_cond_in['Wk'], 'L1_cond_bk': _L1_cond_in['bk'], 'L1_cond_Wout': _L1_cond_in['Wout'], 'L1_cond_bout': _L1_cond_in['bout']}

def reference(x, cond_1024, mask_BxS_bf0, mask_BxSxSx11_ik0, L0_cond_w_adaln1, L0_cond_b_adaln1, L0_cond_w_adaln2, L0_cond_b_adaln2, L0_cond_wq, L0_cond_bq, L0_cond_wk, L0_cond_bk, L0_cond_wv, L0_cond_bv, L0_cond_wo, L0_cond_bo, L0_cond_w1, L0_cond_b1, L0_cond_w2, L0_cond_b2, L1_cond_W_self, L1_cond_b_self, L1_cond_w_bias, L1_cond_b_bias, L1_cond_Wq, L1_cond_bq, L1_cond_Wk, L1_cond_bk, L1_cond_Wout, L1_cond_bout):
    import jax
    import jax.numpy as jnp

    def _L0_cond_ref(x, cond, key_padding_mask, w_adaln1, b_adaln1, w_adaln2, b_adaln2, wq, bq, wk, bk, wv, bv, wo, bo, w1, b1, w2, b2):
        import math
        import jax, jax.numpy as jnp
        import numpy as np
        H = 128
        NH = 16
        HD = H // NH
        CD = 128
        MLP = 512
        EPS = 1e-05

        def _layernorm(x):
            mu = jnp.mean(x, axis=-1, keepdims=True)
            var = jnp.var(x, axis=-1, keepdims=True)
            return (x - mu) * jax.lax.rsqrt(var + EPS)

        def _adaln(x, cond, W, b):
            ss = cond @ W.T + b
            scale, shift = jnp.split(ss, 2, axis=-1)
            return _layernorm(x) * (1.0 + scale[:, None, :]) + shift[:, None, :]
        B, L, D = x.shape
        normed = _adaln(x, cond, w_adaln1, b_adaln1)
        q = (normed @ wq.T + bq).reshape(B, L, NH, HD)
        k = (normed @ wk.T + bk).reshape(B, L, NH, HD)
        v = (normed @ wv.T + bv).reshape(B, L, NH, HD)
        scale = math.sqrt(HD)
        scores = jnp.einsum('blhd,bmhd->bhlm', q, k) / scale
        scores = jnp.where(key_padding_mask[:, None, None, :], -jnp.inf, scores)
        attn = jax.nn.softmax(scores, axis=-1)
        attn_out = jnp.einsum('bhlm,bmhd->blhd', attn, v).reshape(B, L, D)
        x = x + attn_out @ wo.T + bo
        normed = _adaln(x, cond, w_adaln2, b_adaln2)
        h = jax.nn.gelu(normed @ w1.T + b1, approximate=False)
        x = x + h @ w2.T + b2
        return x

    def _L1_cond_ref(v, q, adj, W_self, b_self, w_bias, b_bias, Wq, bq, Wk, bk, Wout, bout):
        import jax, jax.numpy as jnp
        import numpy as np
        NONGT = 20
        H = 16
        NEG = -9000000000000000.0

        def _gat_attention(self_feat, cond_adj, label_bias, Wq, bq, Wk, bk, Wout, bout):
            B, N, F = self_feat.shape
            ng = min(NONGT, N)
            dh = F // H
            kv = self_feat[:, :ng]
            qh = (self_feat @ Wq.T + bq).reshape(B, N, H, dh)
            kh = (kv @ Wk.T + bk).reshape(B, ng, H, dh)
            aff = jnp.einsum('bnhd,bmhd->bnhm', qh, kh) * (1.0 / np.sqrt(dh))
            mask = cond_adj[:, :, None, :] > 0
            aff = jnp.where(mask, aff, NEG) + label_bias[:, :, None, :]
            w = jax.nn.softmax(aff, axis=-1)
            out_t = jnp.einsum('bnhm,bmf->bnhf', w, kv)
            out = jnp.einsum('bnhf,hgf->bnhg', out_t, Wout) + bout.reshape(H, F // H)
            return out.reshape(B, N, F)

        def _forward(v, q, adj, W_self, b_self, w_bias, b_bias, Wq, bq, Wk, bk, Wout, bout):
            adj_f = adj.astype(jnp.float32)
            exp_v = v
            row_zero = exp_v.sum(-1) == 0
            q_exp = jnp.where(row_zero[..., None], 0.0, q[:, None, :])
            vcq = jnp.concatenate([exp_v, q_exp], axis=-1)
            self_feat = vcq @ W_self.T + b_self
            output = self_feat
            for d in range(2):
                A = adj_f if d == 0 else jnp.swapaxes(adj_f, 1, 2)
                A = A[:, :, :NONGT, :]
                cond = A.sum(-1)
                vb = A @ w_bias + b_bias
                output = output + _gat_attention(self_feat, cond, vb, Wq[d], bq[d], Wk[d], bk[d], Wout[d], bout[d])
            rel = jax.nn.relu(output)
            return exp_v + rel
        return _forward(v, q, adj, W_self, b_self, w_bias, b_bias, Wq, bq, Wk, bk, Wout, bout)
    x = _L0_cond_ref(x, cond_1024, mask_BxS_bf0, L0_cond_w_adaln1, L0_cond_b_adaln1, L0_cond_w_adaln2, L0_cond_b_adaln2, L0_cond_wq, L0_cond_bq, L0_cond_wk, L0_cond_bk, L0_cond_wv, L0_cond_bv, L0_cond_wo, L0_cond_bo, L0_cond_w1, L0_cond_b1, L0_cond_w2, L0_cond_b2)
    x = _L1_cond_ref(x, cond_1024, mask_BxSxSx11_ik0, L1_cond_W_self, L1_cond_b_self, L1_cond_w_bias, L1_cond_b_bias, L1_cond_Wq, L1_cond_bq, L1_cond_Wk, L1_cond_bk, L1_cond_Wout, L1_cond_bout)
    return x

_drawn_inputs = setup_inputs


def setup_inputs(seed=0):
    import zlib

    import numpy as np

    out = dict(_drawn_inputs(seed))
    spreads = {'L0_cond_b_adaln1': (0.0, 0.8),
     'L0_cond_b_adaln2': (0.0, 0.8),
     'L0_cond_bq': (0.0, 0.8),
     'L0_cond_bk': (0.0, 0.8),
     'L0_cond_bv': (0.0, 0.395),
     'L0_cond_bo': (0.0, 0.1),
     'L0_cond_b1': (0.0, 0.341),
     'L0_cond_b2': (0.0, 0.1),
     'L1_cond_b_self': (0.0, 0.1),
     'L1_cond_bq': (0.0, 0.1),
     'L1_cond_bk': (0.0, 0.1),
     'L1_cond_bout': (0.0, 0.1)}
    factors = {'L0_cond_w_adaln1': 4.967,
     'L0_cond_w_adaln2': 3.371,
     'L0_cond_wq': 8.0,
     'L0_cond_wk': 8.0,
     'L0_cond_wv': 4.218}
    for name, (base, spread) in spreads.items():
        noise = np.random.default_rng([zlib.crc32(name.encode()), seed]).standard_normal(out[name].shape)
        drawn = base * np.exp(spread * noise) if base else spread * noise
        out[name] = jnp.asarray(drawn.astype(out[name].dtype))
    for name, factor in factors.items():
        out[name] = (out[name] * factor).astype(out[name].dtype)
    return out
```

```python
from contextlib import ExitStack

import numpy as np

import concourse.bass as bass
from concourse import mybir

ALU = mybir.AluOpType
ACT = mybir.ActivationFunctionType
AX = mybir.AxisListType
F32 = mybir.dt.float32
BF16 = mybir.dt.bfloat16
I32 = mybir.dt.int32
U8 = mybir.dt.uint8

P = 128
B = 16
NH = 16
HD = 8
MC = 4
GB = 4
NG = B // GB
GT = GB * P
M = 20
L = 11
HC = 6
CHUNK_HEAD = (0, 6, 10)
CHUNK_NEW = (0, 0, 2)
ROWS = HC * M
QK_SCALE = float(1.0 / np.sqrt(HD))
EPS = 1e-5
NEG = -9000000000000000.0
MASKED = -1e30

Q_PARTS = (0, 0, 1, 1, 0, 2)
K_PARTS = (0, 1, 0, 1, 2, 0)
ROW_MASK = len(Q_PARTS) * HD
ROW_NEGMAX = ROW_MASK + 1
ROWS_S = ROW_NEGMAX
ROWS_ST = ROW_NEGMAX + 3
N_STACK = 2 * len(Q_PARTS) + 1

W_NAMES = (("wq", P), ("wk", P), ("wv", P), ("wa1", 2 * P), ("cond", B), ("wa2", 2 * P), ("ws", 2 * P),
           ("wo", P), ("w1", MC * P), ("w2", MC * P), ("gq", 2 * P), ("gk", 2 * P), ("gout", 2 * P))
W_AT = {}
_n = 0
for _name, _size in W_NAMES:
    W_AT[_name] = _n
    _n += _size
W_COLS = _n
W_FIRST = W_AT["wo"]
V_NAMES = (("bq", 1), ("bk", 1), ("bv", 1), ("bo", 0), ("ba1", 2), ("ba2", 2), ("bself", 1), ("b1", MC),
           ("b2", 1), ("gbq", 2), ("gbk", 2), ("gbout", 2))
V_AT = {}
_n = 0
for _name, _size in V_NAMES:
    V_AT[_name] = _n
    _n += _size
V_COLS = _n


def build(nc, x, wall, vecs, bo_row, edge_w, mask_cols, mask_row, adj, out):
    with ExitStack() as ctx:
        def sb(name, shape, dt=F32):
            return ctx.enter_context(nc.sbuf_tensor(name, shape, dt))

        def sem(name):
            return ctx.enter_context(nc.semaphore(name))

        psum = ctx.enter_context(nc.psum_tensor("psum", [P, 8, 512], F32))

        w = sb("w", [P, W_COLS])
        vec = sb("vec", [P, V_COLS])
        bo_all = sb("bo_all", [P, P])
        edge_all = sb("edge_all", [P, L + 1])
        mask_c = sb("mask_c", [P, B], U8)
        mask_r = sb("mask_r", [1, B * P], U8)
        mask_neg = sb("mask_neg", [1, B * P], BF16)
        keep = sb("keep", [P, B])
        ident = sb("ident", [P, P])
        ident_bf = sb("ident_bf", [P, P], BF16)
        ones_bf = sb("ones_bf", [4, B * P], BF16)
        ones_col = sb("ones_col", [P, B])
        head_mask = sb("head_mask", [P, NH])
        chunk_mask = sb("chunk_mask", [ROWS, HC * HD])
        batch_mask = sb("batch_mask", [B, B * P])
        minus_half = sb("minus_half", [P, GB])
        bq_scaled = sb("bq_scaled", [P, 1])
        gbq_scaled = sb("gbq_scaled", [P, 2])
        bself_bout = sb("bself_bout", [P, 1])
        ada = sb("ada", [P, 4, B])
        q_vec = sb("q_vec", [B, P])

        x_all = sb("x_all", [P, B, P])
        v_mem = sb("v_mem", [P, B * NH * (HD + 1)])
        v_aug = v_mem[:].rearrange("p (b h d) -> p b h d", b=B, h=NH)
        parts_mem = sb("parts_mem", [P, 3 * 2 * B * P], BF16)
        parts = parts_mem[:].rearrange("p (a s t) -> p a s t", a=3, s=2)
        attn_all = sb("attn_all", [P, B, P])
        x1T_all = parts_mem[:].bitcast(F32)[:, 0:B * P]
        feat_all = parts_mem[:].bitcast(F32)[:, B * P:3 * B * P].rearrange("p (a t) -> p a t", a=2)
        sfT_all = v_mem[:, 0:B * P]

        stats = sb("stats", [P, GB, 6])
        mean_var = sb("mean_var", [P, GB, 2])
        var_eps = sb("var_eps", [P, GB])
        carrier = sb("carrier", [P, 1])
        rstd = sb("rstd", [P, GB])
        norm_mem = sb("norm_mem", [P, 2 * GT])
        split_mem = sb("split_mem", [P, 4 * GT])
        xn = norm_mem[:, 0:GT].rearrange("p (b d) -> p b d", b=GB)
        nT = norm_mem[:, GT:2 * GT]
        qk32 = split_mem[:, 0:2 * GT].rearrange("p (s t) -> p s t", s=2)
        rest = split_mem[:, 2 * GT:4 * GT].rearrange("p (s t) -> p s t", s=2)
        stack_mem = sb("stack_mem", [P, 2 * GB * NH * P], BF16)
        q_stack, k_stack = (stack_mem[0:64, n * GB * NH * P:(n + 1) * GB * NH * P].rearrange(
            "p (b h t) -> p b h t", b=GB, h=NH) for n in range(2))
        row_max = sb("row_max", [P, NH])
        neg_all = sb("neg_all", [P, P], BF16)
        neg_parts = neg_all[:, 0:3 * NH].rearrange("p (a h) -> p a h", a=3)
        neg_rest = sb("neg_rest", [P, NH])
        neg_rows = sb("neg_rows", [3 * NH, 2, P], BF16)
        probs_mem = sb("probs_mem", [P, 4 * 512])
        probsT = probs_mem[:].rearrange("p (c t) -> p c t", c=4)
        den_inv = sb("den_inv", [P, NH])
        attn_g, x_bo, x1, xn2 = (split_mem[:, n * GT:(n + 1) * GT].rearrange("p (b d) -> p b d", b=GB)
                                 for n in range(4))
        attnT = norm_mem[:, 0:GT]
        n2T = norm_mem[:, GT:2 * GT]
        hT = probs_mem[:].rearrange("p (c t) -> p c t", c=MC)
        nonzero = sb("nonzero", [B, GT])
        adj_int = sb("adj_int", [P, B * M * L], I32)
        adj_f = sb("adj_f", [P, B * M * L])
        edge_bias = sb("edge_bias", [P, 2, B * M])
        edge_sum = sb("edge_sum", [P, 2, B * M])
        edge_keep = sb("edge_keep", [P, 2, B * M])
        feat = sb("feat", [P, GB, 2, P])
        key_feat = sb("key_feat", [P, GB, HC, M])
        gqT = sb("gqT", [P, 2, GT])
        HM = NH * M
        graph_mem = stack_mem[:].bitcast(F32)
        k_blocks = graph_mem[:, 0:8 * HM].rearrange("p (b d n) -> p b d n", b=GB, d=2)
        gw = graph_mem[:, 8 * HM:16 * HM].rearrange("p (b d n) -> p b d n", b=GB, d=2)
        aff = graph_mem[:, 16 * HM:20 * HM].rearrange("p (b d n) -> p b d n", b=2, d=2)
        aff_b = graph_mem[:, 20 * HM:24 * HM].rearrange("p (b d n) -> p b d n", b=2, d=2)
        aff_max = sb("aff_max", [P, 2, 2, NH])
        aff_c = sb("aff_c", [P, 2, 2, NH * M])
        gwT = sb("gwT", [ROWS, 6 * P])
        v_blocks = sb("v_blocks", [ROWS, GB, 6, HC, HD + 1])
        gden_inv = sb("gden_inv", [P, 2 * NH])
        gout_d = sb("gout_d", [P, 2, 2, P])
        gout_sum = sb("gout_sum", [P, 2, P])
        g_pre = sb("g_pre", [P, P])
        y_all = attn_all

        names = """x_loaded w_loaded wrest_loaded small_loaded ones_made ident_made ident_bf_made masks_made
            head_mask_a chunk_mask_a chunk_mask_b batch_mask_a batch_mask_b keep_made mask_neg_made bias_made condT_in ada_ready ada_done qvec_ready bank6_read
            stack_ones_in
            ln1_stats ln1_mv ln1_eps ln1_rstd xn_ready xT_ready nT_ready q_ready k_ready v_ready qk_copied v_done
            keep_col split_hi split_r split_mid split_done
            s_ready max_done neg_zeroed neg_hi neg_r neg_mid neg_done neg_turned neg_copied st_ready exp_done pv_done
            den_done norm_done
            attn_g_ready attn_turned attnT_ready wo_ready x_bo_ready x1_ready ln2_stats ln2_mv ln2_eps ln2_rstd
            xn2_ready x1_turned xn2_turned x1T_ready n2T_ready h_ready gelu_ready y_ready x2T_ready rowsum_ready
            nonzero_ready sf_ready sfT_done
            adj_loaded adj_cast edge_prod edge_bias_done edge_sum_done edge_keep_done edge_neg_done edge_mb_done
            gq_ready gk_ready gqT_done kblk_done aff_ready aff_masked aff_biased aff_maxed aff_centred gw_ready
            gw_turned gwT_done feat_copied key_feat_copied vb_ready vblk_done gpv_ready fT_ready gden_done
            gnorm_done gsum_done gpre_done y_done""".split()
        s = {n: sem(n) for n in names}
        stack_in = [sem(f"stack_in{j}") for j in range(GB)]
        negmax_in = [sem(f"negmax_in{j}") for j in range(GB)]
        out_done = [sem(f"out_done{j}") for j in range(GB)]

        def W(name, n=P, at=0):
            return w[:, W_AT[name] + at:W_AT[name] + at + n]

        def V(name, n=1, at=0):
            return vec[:, V_AT[name] + at:V_AT[name] + at + n]

        def bank(k):
            return psum[:, k, :]

        def group(t, g):
            return t[:, bass.ts(g, GT)]

        def known(b):
            return isinstance(b, int)

        def reuse(eng, semaphore, value, b, first):
            if not known(b) or b >= first:
                eng.wait_ge(semaphore, value)

        block = ctx.enter_context(nc.Block())

        @block.sync
        def _(sp):
            sp.dma_start(x_all[:, 0:GB, :], x[0:GB].rearrange("b t d -> t b d")).then_inc(s["x_loaded"], 16)
            sp.dma_start(w[:, 0:W_FIRST], wall[:, 0:W_FIRST]).then_inc(s["w_loaded"], 16)
            sp.dma_start(x_all[:, GB:, :], x[GB:].rearrange("b t d -> t b d")).then_inc(s["x_loaded"], 16)
            sp.dma_start(w[:, W_FIRST:], wall[:, W_FIRST:]).then_inc(s["wrest_loaded"], 16)
            sp.wait_ge(s["ones_made"], 1)
            for j in range(GB):
                sp.dma_start(q_stack[ROW_MASK:ROW_MASK + 1, j], ones_bf[0:1, :]).then_inc(s["stack_ones_in"], 16)
                sp.dma_start(k_stack[ROW_NEGMAX:ROW_NEGMAX + 3, j], ones_bf[0:3, :]).then_inc(s["stack_ones_in"], 16)
            sp.wait_ge(s["mask_neg_made"], 1)

            def stack(g, j):
                b = GB * g + j
                sp.wait_ge(s["split_done"], g + 1)
                reuse(sp, s["st_ready"], 4 * (b - GB) + 4, b, GB)
                for side, buf, which in ((0, q_stack, Q_PARTS), (1, k_stack, K_PARTS)):
                    for n, part in enumerate(which):
                        sp.dma_start(buf[n * HD:(n + 1) * HD, j], parts[:, part, side, bass.ts(b, P)]).then_inc(
                            stack_in[j], 16)
                sp.dma_start(k_stack[ROW_MASK:ROW_MASK + 1, j],
                             mask_neg[0:1, bass.ts(b, P)].unsqueeze(1).to_broadcast([1, NH, P])).then_inc(
                                 stack_in[j], 16)

            def negmax(g, j):
                b = GB * g + j
                sp.wait_ge(s["neg_copied"], b + 1)
                sp.dma_start(q_stack[ROW_NEGMAX:ROW_NEGMAX + 3, j], neg_rows[:, j % 2, :]).then_inc(negmax_in[j], 16)

            stack(0, 0)
            stack(0, 1)
            for j in range(GB):
                if j >= 1:
                    negmax(0, j - 1)
                stack((j + 2) // GB, (j + 2) % GB)
            with sp.Fori(1, NG - 1) as g:
                for j in range(GB):
                    negmax(g - (j == 0), (j - 1) % GB)
                    stack(g + (j + 2) // GB, (j + 2) % GB)
            for j in range(GB):
                negmax(NG - 1 - (j == 0), (j - 1) % GB)
                if j + 2 < GB:
                    stack(NG - 1, j + 2)
            negmax(NG - 1, GB - 1)

            with sp.Fori(0, NG) as g:
                for j in range(GB):
                    b = GB * g + j
                    sp.wait_ge(s["y_done"], b + 1)
                    sp.dma_start(out[bass.ds(b, 1)].rearrange("b t d -> t b d"), y_all[:, bass.ds(b, 1), :]).then_inc(out_done[j], 16)
            for j in range(GB):
                sp.wait_ge(out_done[j], 16 * NG)

        @block.gpsimd
        def _(pool):
            nc.gpsimd.memset(ones_bf[:], 1.0).then_inc(s["ones_made"], 1)
            nc.gpsimd.memset(ident[:], 0.0).then_inc(s["ident_made"], 1)
            pool.wait_ge(s["ident_made"], 1)
            nc.gpsimd.affine_select(out=ident[:], in_=ident[:], compare_op=ALU.not_equal, fill=1.0, base=0,
                                    pattern=[[-1, P]], channel_multiplier=1).then_inc(s["ident_made"], 1)
            nc.gpsimd.memset(minus_half[:], -0.5).then_inc(s["masks_made"], 1)
            pool.wait_ge(s["ident_made"], 2)
            nc.gpsimd.tensor_copy(ident_bf[:], ident[:]).then_inc(s["ident_bf_made"], 1)

            nc.gpsimd.memset(neg_all[:], 0.0).then_inc(s["neg_zeroed"], 1)
            pool.wait_ge(s["masks_made"], 1)

            def rstd_of(eps_sem, rstd_sem, g):
                pool.wait_ge(eps_sem, g + 1)
                nc.gpsimd.tensor_tensor(rstd[:], var_eps[:], minus_half[:], ALU.pow).then_inc(rstd_sem, 1)

            with pool.Fori(0, NG) as g:
                rstd_of(s["ln1_eps"], s["ln1_rstd"], g)

            pool.wait_ge(s["keep_made"], 1)
            nc.gpsimd.tensor_copy(v_aug[:, :, :, HD], keep[:].unsqueeze(2).to_broadcast([P, B, NH])).then_inc(
                s["keep_col"], 1)

            nc.gpsimd.memset(head_mask[:], 1.0).then_inc(s["head_mask_a"], 1)
            nc.gpsimd.memset(chunk_mask[:], 1.0).then_inc(s["chunk_mask_a"], 1)
            nc.gpsimd.memset(batch_mask[:], 1.0).then_inc(s["batch_mask_a"], 1)
            nc.gpsimd.memset(ones_col[:], 1.0).then_inc(s["masks_made"], 1)

            def band(t, sem_a, width, pattern):
                pool.wait_ge(sem_a, 1)
                lo = [[-width * n if n else 0, c] for n, c in pattern]
                nc.gpsimd.affine_select(out=t, in_=t, compare_op=ALU.is_ge, fill=0.0, base=0,
                                        pattern=lo, channel_multiplier=1).then_inc(sem_a, 1)
                pool.wait_ge(sem_a, 2)
                hi = [[width * n if n else 0, c] for n, c in pattern]
                nc.gpsimd.affine_select(out=t, in_=t, compare_op=ALU.is_ge, fill=0.0, base=width - 1,
                                        pattern=hi, channel_multiplier=-1).then_inc(s["masks_made"], 1)

            band(head_mask[:], s["head_mask_a"], HD, [[1, NH]])
            band(chunk_mask[:].rearrange("p (h d) -> p h d", h=HC), s["chunk_mask_a"], M, [[1, HC], [0, HD]])
            band(batch_mask[:].rearrange("p (b t) -> p b t", b=B), s["batch_mask_a"], 1, [[1, B], [0, P]])
            pool.wait_ge(s["masks_made"], 5)
            for j in range(GB):
                nc.gpsimd.tensor_copy(
                    v_blocks[:, j, :, :, HD],
                    chunk_mask[:].rearrange("p (h d) -> p h d", h=HC)[:, :, 0].unsqueeze(1).to_broadcast([ROWS, 6, HC])
                ).then_inc(s["masks_made"], 1)

            for d in range(2):
                if d:
                    pool.wait_ge(s["edge_bias_done"], d)
                pool.dma_start(adj_int[:], adj[d]).then_inc(s["adj_loaded"], 16)
                pool.wait_ge(s["adj_loaded"], 16 * (d + 1))
                if d:
                    pool.wait_ge(s["edge_sum_done"], d)
                nc.gpsimd.tensor_copy(adj_f[:], adj_int[:]).then_inc(s["adj_cast"], 1)
                pool.wait_ge(s["adj_cast"], d + 1)
                nc.gpsimd.tensor_tensor(
                    adj_int[:].bitcast(F32).rearrange("p (e l) -> p e l", l=L), adj_f[:].rearrange("p (e l) -> p e l", l=L),
                    edge_all[:, 0:L].unsqueeze(1).to_broadcast([P, B * M, L]), ALU.mult).then_inc(s["edge_prod"], 1)

            def fixed_copies(g):
                pool.wait_ge(s["norm_done"], GB * g + GB)
                reuse(pool, s["attn_turned"], g, g, 1)
                nc.gpsimd.tensor_copy(attn_g, attn_all[:, bass.ts(g, GB), :]).then_inc(s["attn_g_ready"], 1)
                reuse(pool, s["x1_ready"], g, g, 1)
                nc.gpsimd.tensor_tensor(x_bo, x_all[:, bass.ts(g, GB), :],
                                        bo_all[:].unsqueeze(1).to_broadcast([P, GB, P]), ALU.add).then_inc(s["x_bo_ready"], 1)
                rstd_of(s["ln2_eps"], s["ln2_rstd"], g)

            fixed_copies(0)
            with pool.Fori(1, NG) as g:
                fixed_copies(g)

            def copies(b, j):
                pool.wait_ge(s["bank6_read"], NG + 1)
                reuse(pool, s["fT_ready"], b - GB + 1, b, GB)
                nc.gpsimd.tensor_copy(feat[:, j], feat_all[:, :, bass.ts(b, P)]).then_inc(s["feat_copied"], 1)
                reuse(pool, s["vb_ready"], b - GB + 1, b, GB)
                nc.gpsimd.tensor_copy(key_feat[:, j], sfT_all[:, bass.ds(b * P, M)].unsqueeze(1).to_broadcast([P, HC, M])
                                      ).then_inc(s["key_feat_copied"], 1)

            def add_bias(b, j):
                pool.wait_ge(s["aff_masked"], b + 1)
                reuse(pool, s["aff_maxed"], b - 1, b, 2)
                mb = edge_bias[:, :, bass.ds(b * M, M)]
                for d in range(2):
                    nc.gpsimd.tensor_tensor(
                        aff_b[:, j % 2, d, :].rearrange("p (h m) -> p h m", h=NH), aff[:, j % 2, d, :].rearrange("p (h m) -> p h m", h=NH),
                        mb[:, d, :].unsqueeze(1).to_broadcast([P, NH, M]), ALU.add).then_inc(s["aff_biased"], 1)

            def centre(b, j):
                pool.wait_ge(s["aff_maxed"], b + 1)
                reuse(pool, s["gw_ready"], b - 1, b, 2)
                nc.gpsimd.tensor_tensor(
                    aff_c[:, j % 2].rearrange("p d (h m) -> p (d h) m", h=NH), aff_b[:, j % 2].rearrange("p d (h m) -> p (d h) m", h=NH),
                    aff_max[:, j % 2].rearrange("p d h -> p (d h)").unsqueeze(2).to_broadcast([P, 2 * NH, M]),
                    ALU.subtract).then_inc(s["aff_centred"], 1)

            def sum_directions(b, j):
                pool.wait_ge(s["gnorm_done"], b + 1)
                reuse(pool, s["gpre_done"], b - 1, b, 2)
                nc.gpsimd.tensor_tensor(gout_sum[:, j % 2], gout_d[:, j % 2, 0], gout_d[:, j % 2, 1], ALU.add).then_inc(s["gsum_done"], 1)

            def pool_step(g, j, n=None):
                b = GB * g + j
                if not known(g) or b < B:
                    copies(b, j)
                if not known(g) or 1 <= b <= B:
                    centre(b - 1, (j - 1) % GB)
                if not known(g) or b < B:
                    add_bias(b, j)
                if not known(g) or 3 <= b < B + 3:
                    sum_directions(b - 3, (j - 3) % GB)

            pool.wait_ge(s["edge_mb_done"], 1)
            for j in range(GB):
                pool_step(0, j)
            with pool.Fori(1, NG) as g:
                for j in range(GB):
                    pool_step(g, j)
            for j in range(GB):
                pool_step(NG, j)

        @block.scalar
        def _(act):
            act.dma_start(vec[:], vecs).then_inc(s["small_loaded"], 16)
            act.dma_start(mask_c[:], mask_cols).then_inc(s["small_loaded"], 16)
            act.dma_start(mask_r[:], mask_row).then_inc(s["small_loaded"], 16)
            act.dma_start(bo_all[:], bo_row.to_broadcast([P, P])).then_inc(s["small_loaded"], 16)
            act.dma_start(edge_all[:], edge_w.to_broadcast([P, L + 1])).then_inc(s["small_loaded"], 16)
            act.wait_ge(s["ada_done"], 4)
            act.wait_ge(s["bias_made"], 3)

            def project_in(g):
                act.wait_ge(s["xT_ready"], g + 1)
                for j in range(GB):
                    nc.scalar.activation(nT[:, bass.ts(j, P)], psum[:, 0, bass.ts(j, P)], ACT.Identity,
                                         scale=ada[:, 0, bass.ds(g * GB + j, 1)],
                                         bias=ada[:, 1, bass.ds(g * GB + j, 1)]).then_inc(s["nT_ready"], 1)
                act.wait_ge(s["q_ready"], g + 1)
                reuse(act, s["split_r"], g, g, 1)
                nc.scalar.activation(qk32[:, 0, :], bank(1), ACT.Identity, scale=QK_SCALE, bias=bq_scaled[:]).then_inc(s["qk_copied"], 1)
                act.wait_ge(s["k_ready"], g + 1)
                nc.scalar.activation(qk32[:, 1, :], bank(2), ACT.Identity, bias=V("bk")).then_inc(s["qk_copied"], 1)

            project_in(0)
            with act.Fori(1, NG) as g:
                project_in(g)

            def exp(b, c):
                quad = 4 * b + c
                act.wait_ge(s["st_ready"], quad + 1)
                reuse(act, s["pv_done"], quad - 3, b, 1)
                nc.scalar.activation(probsT[:, c, :], bank(6 + c % 2), ACT.Exp).then_inc(s["exp_done"], 1)

            def copy_negmax(b, j):
                act.wait_ge(s["neg_turned"], b + 1)
                if known(b):
                    if b >= 2:
                        act.wait_ge(negmax_in[(j - 2) % GB], 16 * ((b - 2) // GB + 1))
                nc.scalar.copy(neg_rows[:, j % 2, :], bank(1)[0:3 * NH, 0:P // 2].bitcast(BF16)).then_inc(s["neg_copied"], 1)

            def act_step(g, j):
                b = GB * g + j
                if not known(g) or 2 <= b < B + 2:
                    exp(b - 2, 0)
                    exp(b - 2, 1)
                if not known(g) or 1 <= b <= B:
                    if not known(g):
                        act.wait_ge(negmax_in[(j - 3) % GB], 16 * (g + (1 if j >= 3 else 0)))
                    copy_negmax(b - 1, (j - 1) % GB)
                if not known(g) or 2 <= b < B + 2:
                    exp(b - 2, 2)
                    exp(b - 2, 3)

            for j in range(GB):
                act_step(0, j)
            with act.Fori(1, NG) as g:
                for j in range(GB):
                    act_step(g, j)
            for j in range(2):
                act_step(NG, j)

            def attn_out(g):
                act.wait_ge(s["attn_turned"], g + 1)
                reuse(act, s["wo_ready"], g, g, 1)
                nc.scalar.activation(attnT, bank(0), ACT.Identity, bias=V("bv")).then_inc(s["attnT_ready"], 1)

            def modulate(g):
                act.wait_ge(s["xn2_turned"], g + 1)
                reuse(act, s["h_ready"], MC * g, g, 1)
                for j in range(GB):
                    nc.scalar.activation(n2T[:, bass.ts(j, P)], psum[:, 3, bass.ts(j, P)], ACT.Identity,
                                         scale=ada[:, 2, bass.ds(g * GB + j, 1)],
                                         bias=ada[:, 3, bass.ds(g * GB + j, 1)]).then_inc(s["n2T_ready"], 1)

            def gelu(g, c):
                act.wait_ge(s["h_ready"], MC * g + c + 1)
                nc.scalar.activation(hT[:, c, :], bank(4 + c % 2), ACT.Gelu, bias=V("b1", 1, c)).then_inc(s["gelu_ready"], 1)

            def self_features(g):
                act.wait_ge(s["sf_ready"], g + 1)
                nc.scalar.activation(group(sfT_all, g), bank(6), ACT.Identity, bias=V("bself")).then_inc(s["sfT_done"], 1)
                nc.scalar.activation(feat_all[:, 1, bass.ts(g, GT)], bank(6), ACT.Identity, bias=bself_bout[:]).then_inc(s["bank6_read"], 1)

            attn_out(0)
            modulate(0)
            with act.Fori(0, NG - 1) as g:
                attn_out(g + 1)
                for c in range(MC):
                    gelu(g, c)
                modulate(g + 1)
                self_features(g)
            for c in range(MC):
                gelu(NG - 1, c)
            self_features(NG - 1)

            def graph_queries(g):
                reuse(act, s["aff_ready"], GB * g, g, 1)
                for d in range(2):
                    act.wait_ge(s["gq_ready"], 2 * g + d + 1)
                    nc.scalar.activation(gqT[:, d, :], bank(d), ACT.Identity, scale=QK_SCALE,
                                         bias=gbq_scaled[:, d:d + 1]).then_inc(s["gqT_done"], 1)

            def graph_exp(b, j):
                act.wait_ge(s["aff_centred"], b + 1)
                reuse(act, s["gw_turned"], b - GB + 1, b, GB)
                nc.scalar.activation(gw[:, j], aff_c[:, j % 2], ACT.Exp).then_inc(s["gw_ready"], 1)

            def graph_weights(b, j):
                act.wait_ge(s["gw_turned"], b + 1)
                reuse(act, s["gpv_ready"], b, b, 1)
                nc.scalar.copy(gwT[:].rearrange("p (d t) -> p d t", d=2),
                               psum[0:ROWS, 3:5, 0:3 * P]).then_inc(s["gwT_done"], 1)

            def graph_act_step(g, j):
                b = GB * g + j
                if j == 0 and (not known(g) or g < NG):
                    graph_queries(g)
                if not known(g) or 1 <= b <= B:
                    graph_exp(b - 1, (j - 1) % GB)
                if not known(g) or 2 <= b < B + 2:
                    graph_weights(b - 2, (j - 2) % GB)

            for j in range(GB):
                graph_act_step(0, j)
            with act.Fori(1, NG) as g:
                for j in range(GB):
                    graph_act_step(g, j)
            for j in range(GB):
                graph_act_step(NG, j)

        @block.vector
        def _(dve):
            dve.wait_ge(s["small_loaded"], 16 * 5)
            nc.vector.tensor_scalar(keep[:], mask_c[:], -1.0, 1.0, ALU.mult, ALU.add).then_inc(s["keep_made"], 1)
            nc.vector.tensor_scalar(mask_neg[:], mask_r[:], MASKED, None, ALU.mult).then_inc(s["mask_neg_made"], 1)
            nc.vector.tensor_scalar(bq_scaled[:], V("bq"), QK_SCALE, None, ALU.mult).then_inc(s["bias_made"], 1)
            nc.vector.tensor_scalar(gbq_scaled[:], V("gbq", 2), QK_SCALE, None, ALU.mult).then_inc(s["bias_made"], 1)
            nc.vector.scalar_tensor_tensor(bself_bout[:], V("bself"), V("gbout", 1, 0), V("gbout", 1, 1),
                                           ALU.add, ALU.add).then_inc(s["bias_made"], 1)

            def layer_stats(src, stats_sem, mv_sem, eps_sem, g):
                for j in range(GB):
                    nc.vector.bn_stats(stats[:, j, :], src(j)).then_inc(stats_sem, 1)
                dve.wait_ge(stats_sem, GB * g + GB)
                nc.vector.memset(carrier[:], 0.0)
                for j in range(GB):
                    nc.vector.bn_aggr(mean_var[:, j, :], stats[:, j, :]).then_inc(mv_sem, 1)
                dve.wait_ge(mv_sem, GB * g + GB)
                nc.vector.tensor_scalar(var_eps[:], mean_var[:, :, 1], EPS, None, ALU.add).then_inc(eps_sem, 1)

            def normalise(dst, src, ready_sem):
                for j in range(GB):
                    nc.vector.tensor_scalar(dst[:, j, :], src(j), mean_var[:, j, 0:1], rstd[:, j:j + 1],
                                            ALU.subtract, ALU.mult).then_inc(ready_sem, 1)

            def batch_of_x(g, j):
                return x_all[:, bass.ds(g * GB + j, 1), :].rearrange("p b d -> p (b d)")

            def ln1(g):
                dve.wait_ge(s["x_loaded"], 32)
                layer_stats(lambda j: batch_of_x(g, j), s["ln1_stats"], s["ln1_mv"], s["ln1_eps"], g)
                dve.wait_ge(s["ln1_rstd"], g + 1)
                reuse(dve, s["xT_ready"], g, g, 1)
                normalise(xn, lambda j: batch_of_x(g, j), s["xn_ready"])

            def values_and_split(g):
                dve.wait_ge(s["v_ready"], g + 1)
                for j in range(GB):
                    b = g * GB + j
                    nc.vector.tensor_scalar(
                        v_aug[:, bass.ds(b, 1), :, 0:HD].rearrange("p b h d -> p (b h) d"),
                        bank(3)[:, bass.ts(j, P)].rearrange("p (h d) -> p h d", h=NH), keep[:, bass.ds(b, 1)], None, ALU.mult
                    ).then_inc(s["v_done"], 1)
                dve.wait_ge(s["qk_copied"], 2 * g + 2)
                part = [parts[:, n, :, bass.ts(g, GT)] for n in range(3)]
                nc.vector.tensor_copy(part[0], qk32).then_inc(s["split_hi"], 1)
                dve.wait_ge(s["split_hi"], g + 1)
                nc.vector.tensor_tensor(rest, qk32, part[0], ALU.subtract).then_inc(s["split_r"], 1)
                dve.wait_ge(s["split_r"], g + 1)
                nc.vector.tensor_copy(part[1], rest).then_inc(s["split_mid"], 1)
                dve.wait_ge(s["split_mid"], g + 1)
                nc.vector.tensor_tensor(part[2], rest, part[1], ALU.subtract).then_inc(s["split_done"], 1)

            dve.wait_ge(s["keep_made"], 1)
            ln1(0)
            dve.wait_ge(s["ada_ready"], 4)
            for n, name in enumerate(("ba1", "ba1", "ba2", "ba2")):
                nc.vector.tensor_scalar(ada[:, n, :], bank(7)[:, n * B:(n + 1) * B], V(name, 1, n % 2), 1.0 - n % 2,
                                        ALU.add, ALU.add).then_inc(s["ada_done"], 1)
            dve.wait_ge(s["qvec_ready"], 1)
            nc.vector.tensor_copy(q_vec[:], psum[0:B, 6, 0:P]).then_inc(s["bank6_read"], 1)
            with dve.Fori(0, NG - 1) as g:
                ln1(g + 1)
                values_and_split(g)
            values_and_split(NG - 1)

            def quad_max(b, c):
                dve.wait_ge(s["s_ready"], 4 * b + c + 1)
                nc.vector.tensor_reduce(row_max[:, 4 * c:4 * c + 4], bank(4 + c % 2).rearrange("p (h k) -> p h k", h=4),
                                        AX.X, ALU.max).then_inc(s["max_done"], 1)

            def split_negmax(b):
                dve.wait_ge(s["max_done"], 4 * b + 4)
                reuse(dve, s["neg_turned"], b, b, 1)
                nc.vector.tensor_scalar(neg_parts[:, 0, :], row_max[:], -1.0, None, ALU.mult).then_inc(s["neg_hi"], 1)
                dve.wait_ge(s["neg_hi"], b + 1)
                nc.vector.scalar_tensor_tensor(neg_rest[:], row_max[:], -1.0, neg_parts[:, 0, :], ALU.mult,
                                               ALU.subtract).then_inc(s["neg_r"], 1)
                dve.wait_ge(s["neg_r"], b + 1)
                nc.vector.tensor_copy(neg_parts[:, 1, :], neg_rest[:]).then_inc(s["neg_mid"], 1)
                dve.wait_ge(s["neg_mid"], b + 1)
                nc.vector.tensor_tensor(neg_parts[:, 2, :], neg_rest[:], neg_parts[:, 1, :], ALU.subtract).then_inc(
                    s["neg_done"], 1)

            def attn_normalise(b):
                dve.wait_ge(s["pv_done"], 4 * b + 4)
                o = bank(0)[:, 0:NH * (HD + 1)].rearrange("p (h d) -> p h d", h=NH)
                nc.vector.reciprocal(den_inv[:], o[:, :, HD]).then_inc(s["den_done"], 1)
                dve.wait_ge(s["den_done"], b + 1)
                nc.vector.tensor_tensor(attn_all[:, bass.ds(b, 1), :].rearrange("p b (h d) -> p (b h) d", h=NH), o[:, :, 0:HD],
                                        den_inv[:].unsqueeze(2).to_broadcast([P, NH, HD]), ALU.mult).then_inc(
                                            s["norm_done"], 1)

            def dve_step(g, j):
                b = GB * g + j
                for c in range(4):
                    if not known(g) or b < B:
                        quad_max(b, c)
                    if c == 1 and (not known(g) or 3 <= b < B + 3):
                        attn_normalise(b - 3)
                if not known(g) or b < B:
                    split_negmax(b)

            dve.wait_ge(s["neg_zeroed"], 1)
            for j in range(GB):
                dve_step(0, j)
            with dve.Fori(1, NG) as g:
                for j in range(GB):
                    dve_step(g, j)
            for j in range(3):
                dve_step(NG, j)

            def x1_and_norm(g):
                dve.wait_ge(s["wo_ready"], g + 1)
                dve.wait_ge(s["x_bo_ready"], g + 1)
                reuse(dve, s["x1_turned"], g, g, 1)
                nc.vector.tensor_tensor(x1.rearrange("p b d -> p (b d)"), bank(1), x_bo.rearrange("p b d -> p (b d)"),
                                        ALU.add).then_inc(s["x1_ready"], 1)
                dve.wait_ge(s["x1_ready"], g + 1)
                layer_stats(lambda j: x1[:, j, :], s["ln2_stats"], s["ln2_mv"], s["ln2_eps"], g)
                dve.wait_ge(s["ln2_rstd"], g + 1)
                reuse(dve, s["xn2_turned"], g, g, 1)
                normalise(xn2, lambda j: x1[:, j, :], s["xn2_ready"])
                dve.wait_ge(s["x1_turned"], g + 1)
                nc.vector.tensor_scalar(group(x1T_all, g), bank(2), V("b2"), None, ALU.add).then_inc(s["x1T_ready"], 1)

            def x2_and_rows(g):
                dve.wait_ge(s["y_ready"], g + 1)
                dve.wait_ge(s["x1T_ready"], g + 1)
                nc.vector.tensor_tensor(feat_all[:, 0, bass.ts(g, GT)], bank(6), group(x1T_all, g), ALU.add).then_inc(
                    s["x2T_ready"], 1)
                dve.wait_ge(s["rowsum_ready"], g + 1)
                nc.vector.scalar_tensor_tensor(nonzero[:], psum[0:B, 7, :], 0.0, group(batch_mask, g), ALU.not_equal,
                                               ALU.mult).then_inc(s["nonzero_ready"], 1)

            for d in range(2):
                dve.wait_ge(s["edge_prod"], d + 1)
                nc.vector.tensor_reduce(edge_bias[:, d, :], adj_int[:].bitcast(F32).rearrange("p (e l) -> p e l", l=L),
                                        AX.X, ALU.add).then_inc(s["edge_bias_done"], 1)
                nc.vector.tensor_reduce(edge_sum[:, d, :], adj_f[:].rearrange("p (e l) -> p e l", l=L),
                                        AX.X, ALU.add).then_inc(s["edge_sum_done"], 1)
            dve.wait_ge(s["edge_sum_done"], 2)
            nc.vector.tensor_scalar(edge_keep[:], edge_sum[:], 0.0, None, ALU.is_gt).then_inc(s["edge_keep_done"], 1)
            dve.wait_ge(s["edge_keep_done"], 1)
            nc.vector.tensor_scalar(edge_sum[:], edge_keep[:], -NEG, NEG, ALU.mult, ALU.add).then_inc(s["edge_neg_done"], 1)
            dve.wait_ge(s["edge_neg_done"], 1)
            dve.wait_ge(s["edge_bias_done"], 2)
            nc.vector.scalar_tensor_tensor(edge_bias[:], edge_bias[:], edge_all[:, L:L + 1], edge_sum[:], ALU.add,
                                           ALU.add).then_inc(s["edge_mb_done"], 1)

            x1_and_norm(0)
            with dve.Fori(0, NG - 1) as g:
                x1_and_norm(g + 1)
                x2_and_rows(g)
            x2_and_rows(NG - 1)

            def key_blocks(g, j):
                b = GB * g + j
                if j == 0:
                    dve.wait_ge(s["gk_ready"], g + 1)
                reuse(dve, s["aff_ready"], b - GB + 1, b, GB)
                for d in range(2):
                    keys = bank(2)[:, d * GB * M + j * M:d * GB * M + (j + 1) * M]
                    nc.vector.scalar_tensor_tensor(
                        k_blocks[:, j, d, :].rearrange("p (h m) -> p h m", h=NH), keys.unsqueeze(1).to_broadcast([P, NH, M]),
                        V("gbk", 1, d), head_mask[:].unsqueeze(2).to_broadcast([P, NH, M]), ALU.add, ALU.mult
                    ).then_inc(s["kblk_done"], 1)

            def mask_aff(b, j):
                dve.wait_ge(s["aff_ready"], b + 1)
                reuse(dve, s["aff_biased"], 2 * (b - 2) + 2, b, 2)
                nc.vector.tensor_tensor(
                    aff[:, j % 2].rearrange("p d (h m) -> p d h m", h=NH),
                    psum[:, 6:8, 0:NH * M].rearrange("p d (h m) -> p d h m", h=NH),
                    edge_keep[:, :, bass.ds(b * M, M)].unsqueeze(2).to_broadcast([P, 2, NH, M]), ALU.mult
                ).then_inc(s["aff_masked"], 1)

            def max_aff(b, j):
                dve.wait_ge(s["aff_biased"], 2 * b + 2)
                reuse(dve, s["aff_centred"], b - 1, b, 2)
                nc.vector.tensor_reduce(aff_max[:, j % 2].rearrange("p d h -> p (d h)"),
                                        aff_b[:, j % 2].rearrange("p d (h m) -> p (d h) m", h=NH), AX.X, ALU.max).then_inc(s["aff_maxed"], 1)

            def value_blocks(b, j):
                dve.wait_ge(s["vb_ready"], b + 1)
                reuse(dve, s["gpv_ready"], b - GB + 1, b, GB)
                nc.vector.tensor_tensor(
                    v_blocks[:, j, :, :, 0:HD], psum[0:ROWS, 0, 0:6 * HC * HD].rearrange("p (k h d) -> p k h d", k=6, h=HC),
                    chunk_mask[:].rearrange("p (h d) -> p h d", h=HC).unsqueeze(1).to_broadcast([ROWS, 6, HC, HD]), ALU.mult
                ).then_inc(s["vblk_done"], 1)

            def graph_normalise(b, j):
                dve.wait_ge(s["gpv_ready"], b + 1)
                o = bank(5)[:, 0:2 * NH * (HD + 1)].rearrange("p (h d) -> p h d", h=2 * NH)
                nc.vector.reciprocal(gden_inv[:], o[:, :, HD]).then_inc(s["gden_done"], 1)
                dve.wait_ge(s["gden_done"], b + 1)
                reuse(dve, s["gsum_done"], b - 1, b, 2)
                nc.vector.tensor_tensor(gout_d[:, j % 2].rearrange("p d (h e) -> p (d h) e", h=NH), o[:, :, 0:HD],
                                        gden_inv[:].unsqueeze(2).to_broadcast([P, 2 * NH, HD]), ALU.mult).then_inc(
                                            s["gnorm_done"], 1)

            def finish(b, j):
                dve.wait_ge(s["gsum_done"], b + 1)
                dve.wait_ge(s["fT_ready"], b + 1)
                nc.vector.tensor_tensor(g_pre[:], bank(1)[:, P:2 * P], gout_sum[:, j % 2], ALU.add).then_inc(s["gpre_done"], 1)
                dve.wait_ge(s["gpre_done"], b + 1)
                nc.vector.scalar_tensor_tensor(y_all[:, bass.ds(b, 1), :].rearrange("p b d -> p (b d)"), g_pre[:], 0.0, bank(1)[:, 0:P], ALU.max, ALU.add).then_inc(
                    s["y_done"], 1)

            def graph_dve_step(g, j):
                b = GB * g + j
                if not known(g) or 1 <= b <= B:
                    max_aff(b - 1, (j - 1) % GB)
                    value_blocks(b - 1, (j - 1) % GB)
                if not known(g) or 4 <= b < B + 4:
                    finish(b - 4, j)
                if not known(g) or b < B:
                    key_blocks(g, j)
                if not known(g) or 3 <= b < B + 3:
                    graph_normalise(b - 3, (j - 3) % GB)
                if not known(g) or b < B:
                    mask_aff(b, j)

            dve.wait_ge(s["masks_made"], 5 + GB)
            for j in range(GB):
                graph_dve_step(0, j)
            with dve.Fori(1, NG) as g:
                for j in range(GB):
                    graph_dve_step(g, j)
            for j in range(GB):
                graph_dve_step(NG, j)

        @block.tensor
        def _(pe):
            def mm(dst, lhsT, rhs, start=True, stop=True):
                return nc.tensor.matmul(dst, lhsT, rhs, start=start, stop=stop)

            pe.wait_ge(s["w_loaded"], 16)
            for n in range(4):
                mm(bank(7)[:, n * B:(n + 1) * B], W(("wa1", "wa2")[n // 2], P, n % 2 * P), W("cond", B)).then_inc(s["ada_ready"], 1)
            mm(psum[0:B, 6, 0:P], W("cond", B), W("ws", P, P)).then_inc(s["qvec_ready"], 1)
            pe.wait_ge(s["ident_made"], 2)
            def project_in(g):
                pe.wait_ge(s["xn_ready"], GB * g + GB)
                for j in range(GB):
                    t = nc.tensor.transpose(bank(0)[:, j * P:(j + 1) * P], xn[:, j, :], ident[:])
                t.then_inc(s["xT_ready"], 1)
                pe.wait_ge(s["nT_ready"], GB * g + GB)
                reuse(pe, s["qk_copied"], 2 * g, g, 1)
                mm(bank(1), W("wq"), nT).then_inc(s["q_ready"], 1)
                mm(bank(2), W("wk"), nT).then_inc(s["k_ready"], 1)
                reuse(pe, s["v_done"], GB * g, g, 1)
                for j in range(GB):
                    t = mm(bank(3)[:, j * P:(j + 1) * P], nT[:, j * P:(j + 1) * P], W("wv"))
                t.then_inc(s["v_ready"], 1)

            project_in(0)
            with pe.Fori(1, NG) as g:
                project_in(g)

            def scores(g, j, c):
                quad = 4 * (GB * g + j) + c
                if c == 0:
                    pe.wait_ge(stack_in[j], 16 * N_STACK * (g + 1))
                reuse(pe, s["max_done"], quad - 1, quad, 2)
                for n in range(4):
                    h = 4 * c + n
                    t = mm(bank(4 + c % 2)[:, n * P:(n + 1) * P], q_stack[0:ROWS_S, j, h, :], k_stack[0:ROWS_S, j, h, :])
                t.then_inc(s["s_ready"], 1)

            def turn_negmax(b):
                pe.wait_ge(s["neg_done"], b + 1)
                reuse(pe, s["neg_copied"], b, b, 1)
                nc.tensor.transpose(bank(1)[:, 0:P // 2].bitcast(BF16), neg_all[:], ident_bf[:]).then_inc(s["neg_turned"], 1)

            def scores_T(g, j, c):
                quad = 4 * (GB * g + j) + c
                if c == 0:
                    pe.wait_ge(negmax_in[j], 16 * (g + 1))
                reuse(pe, s["exp_done"], quad - 1, quad, 2)
                for n in range(4):
                    h = 4 * c + n
                    t = mm(bank(6 + c % 2)[:, n * P:(n + 1) * P], k_stack[0:ROWS_ST, j, h, :], q_stack[0:ROWS_ST, j, h, :])
                t.then_inc(s["st_ready"], 1)

            def weighted_values(b, c):
                pe.wait_ge(s["exp_done"], 4 * b + c + 1)
                if c == 0:
                    reuse(pe, s["norm_done"], b, b, 1)
                for n in range(4):
                    h = 4 * c + n
                    t = mm(bank(0)[:, h * (HD + 1):(h + 1) * (HD + 1)], probsT[:, c, n * P:(n + 1) * P],
                           v_aug[:, bass.ds(b, 1), h, :].rearrange("p b d -> p (b d)"))
                t.then_inc(s["pv_done"], 1)

            def pe_step(g, j):
                b = GB * g + j
                for c in range(4):
                    if not known(g) or b < B:
                        scores(g, j, c)
                    if c == 1 and (not known(g) or 1 <= b <= B):
                        turn_negmax(b - 1)
                    if not known(g) or 2 <= b < B + 2:
                        scores_T(g - (j < 2), (j - 2) % GB, c)
                    if c == 0:
                        if not known(g) or 3 <= b < B + 3:
                            weighted_values(b - 3, 3)
                    elif not known(g) or 2 <= b < B + 2:
                        weighted_values(b - 2, c - 1)

            pe.wait_ge(s["stack_ones_in"], 16 * 2 * GB)
            pe.wait_ge(s["ident_bf_made"], 1)
            pe.wait_ge(s["keep_col"], 1)
            pe.wait_ge(s["v_done"], B)
            for j in range(GB):
                pe_step(0, j)
            with pe.Fori(1, NG) as g:
                for j in range(GB):
                    pe_step(g, j)
            for j in range(3):
                pe_step(NG, j)

            pe.wait_ge(s["wrest_loaded"], 16)
            pe.wait_ge(s["norm_done"], B)
            pe.wait_ge(s["neg_copied"], B)
            pe.wait_ge(s["max_done"], 4 * B)
            pe.wait_ge(s["exp_done"], 4 * B)
            pe.wait_ge(s["masks_made"], 5 + GB)

            def turn_attn(g):
                pe.wait_ge(s["attn_g_ready"], g + 1)
                reuse(pe, s["attnT_ready"], g, g, 1)
                for j in range(GB):
                    t = nc.tensor.transpose(bank(0)[:, j * P:(j + 1) * P], attn_g[:, j, :], ident[:])
                t.then_inc(s["attn_turned"], 1)

            def project(g):
                pe.wait_ge(s["attnT_ready"], g + 1)
                reuse(pe, s["x1_ready"], g, g, 1)
                for j in range(GB):
                    t = mm(bank(1)[:, j * P:(j + 1) * P], attnT[:, j * P:(j + 1) * P], W("wo"))
                t.then_inc(s["wo_ready"], 1)

            def turn_x1(g):
                pe.wait_ge(s["x1_ready"], g + 1)
                reuse(pe, s["x1T_ready"], g, g, 1)
                for j in range(GB):
                    t = nc.tensor.transpose(bank(2)[:, j * P:(j + 1) * P], x1[:, j, :], ident[:])
                t.then_inc(s["x1_turned"], 1)

            def turn_xn2(g):
                pe.wait_ge(s["xn2_ready"], GB * g + GB)
                reuse(pe, s["n2T_ready"], GB * g, g, 1)
                for j in range(GB):
                    t = nc.tensor.transpose(bank(3)[:, j * P:(j + 1) * P], xn2[:, j, :], ident[:])
                t.then_inc(s["xn2_turned"], 1)

            def hidden(g, c):
                if c == 0:
                    pe.wait_ge(s["n2T_ready"], GB * g + GB)
                elif c >= 2:
                    pe.wait_ge(s["gelu_ready"], MC * g + c - 1)
                mm(bank(4 + c % 2), W("w1", P, c * P), n2T).then_inc(s["h_ready"], 1)

            def mlp_out(g):
                pe.wait_ge(s["bank6_read"], g + 1)
                for c in range(MC):
                    pe.wait_ge(s["gelu_ready"], MC * g + c + 1)
                    t = mm(bank(6), W("w2", P, c * P), hT[:, c, :], start=(c == 0), stop=(c == MC - 1))
                t.then_inc(s["y_ready"], 1)

            def self_features(g):
                pe.wait_ge(s["x2T_ready"], g + 1)
                mm(psum[0:B, 7, :], ones_col[:], feat_all[:, 0, bass.ts(g, GT)]).then_inc(s["rowsum_ready"], 1)
                mm(bank(6), W("ws"), feat_all[:, 0, bass.ts(g, GT)], stop=False)
                pe.wait_ge(s["nonzero_ready"], g + 1)
                mm(bank(6), q_vec[:], nonzero[:], start=False).then_inc(s["sf_ready"], 1)

            turn_attn(0)
            project(0)
            turn_x1(0)
            turn_xn2(0)
            with pe.Fori(0, NG - 1) as g:
                turn_attn(g + 1)
                hidden(g, 0)
                hidden(g, 1)
                project(g + 1)
                hidden(g, 2)
                hidden(g, 3)
                mlp_out(g)
                turn_x1(g + 1)
                turn_xn2(g + 1)
                self_features(g)
            for c in range(MC):
                hidden(NG - 1, c)
            mlp_out(NG - 1)
            self_features(NG - 1)

            pe.wait_ge(s["attnT_ready"], NG)
            pe.wait_ge(s["x1_ready"], NG)
            pe.wait_ge(s["x1T_ready"], NG)
            pe.wait_ge(s["n2T_ready"], B)
            pe.wait_ge(s["gelu_ready"], MC * NG)
            pe.wait_ge(s["bank6_read"], NG + 1)
            pe.wait_ge(s["nonzero_ready"], NG)

            def queries_and_keys(g):
                reuse(pe, s["vblk_done"], GB * g, g, 1)
                reuse(pe, s["y_done"], GB * g - 3, g, 1)
                mm(bank(0), W("gq", P, 0), group(sfT_all, g)).then_inc(s["gq_ready"], 1)
                mm(bank(1), W("gq", P, P), group(sfT_all, g)).then_inc(s["gq_ready"], 1)
                keys = group(sfT_all, g).rearrange("p (b t) -> p b t", b=GB)[:, :, 0:M]
                reuse(pe, s["kblk_done"], 2 * GB * g, g, 1)
                for d in range(2):
                    t = mm(bank(2)[:, d * GB * M:(d + 1) * GB * M].rearrange("p (b m) -> p b m", b=GB), W("gk", P, d * P), keys)
                t.then_inc(s["gk_ready"], 1)

            def turn_weights(b, j):
                pe.wait_ge(s["gw_ready"], b + 1)
                reuse(pe, s["gwT_done"], b, b, 1)
                for d in range(2):
                    for c in range(3):
                        h = CHUNK_HEAD[c]
                        t = nc.tensor.transpose(psum[0:ROWS, 3 + d, c * P:(c + 1) * P], gw[:, j, d, h * M:h * M + ROWS], ident[:])
                t.then_inc(s["gw_turned"], 1)

            def graph_values(b, j):
                pe.wait_ge(s["gwT_done"], b + 1)
                pe.wait_ge(s["vblk_done"], b + 1)
                reuse(pe, s["gnorm_done"], b, b, 1)
                for d in range(2):
                    for c in range(3):
                        first = CHUNK_NEW[c]
                        at = (d * NH + CHUNK_HEAD[c] + first) * (HD + 1)
                        n = (HC - first) * (HD + 1)
                        t = mm(bank(5)[:, at:at + n], gwT[:, (d * 3 + c) * P:(d * 3 + c + 1) * P],
                               v_blocks[:, j, 3 * d + c, first:, :].rearrange("p h d -> p (h d)"))
                t.then_inc(s["gpv_ready"], 1)

            def turn_features(g, j, b):
                pe.wait_ge(s["feat_copied"], b + 1)
                pe.wait_ge(s["gqT_done"], 2 * NG if known(g) and g >= NG else 2 * g + 2)
                reuse(pe, s["y_done"], b, b, 1)
                for n in range(2):
                    t = nc.tensor.transpose(bank(1)[:, n * P:(n + 1) * P], feat[:, j, n, :], ident[:])
                t.then_inc(s["fT_ready"], 1)

            def affinities(g, j):
                b = GB * g + j
                pe.wait_ge(s["gqT_done"], 2 * g + 2)
                pe.wait_ge(s["kblk_done"], 2 * b + 2)
                reuse(pe, s["aff_masked"], b, b, 1)
                for d in range(2):
                    t = mm(bank(6 + d)[:, 0:NH * M], gqT[:, d, j * P:(j + 1) * P], k_blocks[:, j, d, :])
                t.then_inc(s["aff_ready"], 1)

            def value_projection(b, j):
                pe.wait_ge(s["key_feat_copied"], b + 1)
                reuse(pe, s["vblk_done"], b, b, 1)
                for d in range(2):
                    for c in range(3):
                        n = (d * 3 + c) * HC * HD
                        t = mm(psum[0:ROWS, 0, n:n + HC * HD], key_feat[:, j].rearrange("p h m -> p (h m)"),
                               W("gout", HC * HD, d * P + CHUNK_HEAD[c] * HD))
                t.then_inc(s["vb_ready"], 1)

            def graph_pe_step(g, j):
                b = GB * g + j
                if j == 0 and (not known(g) or g < NG):
                    queries_and_keys(g)
                if not known(g) or 2 <= b < B + 2:
                    turn_weights(b - 2, (j - 2) % GB)
                if not known(g) or b < B:
                    affinities(g, j)
                    value_projection(b, j)
                if not known(g) or 3 <= b < B + 3:
                    turn_features(g, (j - 3) % GB, b - 3)
                    graph_values(b - 3, (j - 3) % GB)

            for j in range(GB):
                graph_pe_step(0, j)
            with pe.Fori(1, NG) as g:
                for j in range(GB):
                    graph_pe_step(g, j)
            for j in range(GB):
                graph_pe_step(NG, j)


def kernel(**inputs):
    import concourse.bacc as bacc
    from concourse.bass_utils import run_bass_kernel_spmd

    def a(name):
        return np.asarray(inputs[name])

    def dh(v):
        return v.reshape(NH, HD, *v.shape[1:]).swapaxes(0, 1).reshape(v.shape)

    adj = a("mask_BxSxSx11_ik0")
    columns = {
        "wq": dh(a("L0_cond_wq")).T, "wk": dh(a("L0_cond_wk")).T, "wv": a("L0_cond_wv").T,
        "wa1": a("L0_cond_w_adaln1").T, "cond": a("cond_1024").T, "wa2": a("L0_cond_w_adaln2").T,
        "ws": np.concatenate([a("L1_cond_W_self")[:, :P].T, a("L1_cond_W_self")[:, P:].T], axis=1),
        "wo": a("L0_cond_wo").T, "w1": a("L0_cond_w1").T,
        "w2": a("L0_cond_w2").T.reshape(MC, P, P).transpose(1, 0, 2).reshape(P, MC * P),
        "gq": np.concatenate([m.T for m in a("L1_cond_Wq")], axis=1),
        "gk": np.concatenate([m.T for m in a("L1_cond_Wk")], axis=1),
        "gout": np.concatenate([m.reshape(P, P).T for m in a("L1_cond_Wout")], axis=1),
    }
    vectors = {
        "bq": dh(a("L0_cond_bq"))[:, None], "bk": dh(a("L0_cond_bk"))[:, None], "bv": a("L0_cond_bv")[:, None],
        "ba1": a("L0_cond_b_adaln1").reshape(2, P).T, "ba2": a("L0_cond_b_adaln2").reshape(2, P).T,
        "bself": a("L1_cond_b_self")[:, None], "b1": a("L0_cond_b1").reshape(MC, P).T, "b2": a("L0_cond_b2")[:, None],
        "gbq": a("L1_cond_bq").T, "gbk": a("L1_cond_bk").T, "gbout": a("L1_cond_bout").T,
    }
    arrays = {
        "x": a("x"),
        "wall": np.concatenate([columns[n] for n, _ in W_NAMES], axis=1),
        "vecs": np.concatenate([vectors[n] for n, size in V_NAMES if size], axis=1),
        "bo_row": a("L0_cond_bo").reshape(1, P),
        "edge_w": np.concatenate([a("L1_cond_w_bias").reshape(1, L), a("L1_cond_b_bias").reshape(1, 1)], axis=1),
        "mask_cols": np.ascontiguousarray(a("mask_BxS_bf0").T),
        "mask_row": np.ascontiguousarray(a("mask_BxS_bf0").reshape(1, B * P)),
        "adj": np.stack([adj[:, :, :M].transpose(1, 0, 2, 3).reshape(P, B * M * L),
                         adj[:, :M].transpose(2, 0, 1, 3).reshape(P, B * M * L)]),
    }
    nc = bacc.Bacc("TRN2", target_bir_lowering=False, num_devices=1)
    args = []
    for name in arrays:
        v = arrays[name] = np.ascontiguousarray(arrays[name])
        args.append(nc.dram_tensor(f"in_{name}", v.shape, mybir.dt.from_np(v.dtype), kind="ExternalInput").ap())
    out = nc.dram_tensor("out_y", (B, P, P), F32, kind="ExternalOutput").ap()
    build(nc, *args, out)
    r = run_bass_kernel_spmd(nc, [{f"in_{n}": v for n, v in arrays.items()}], core_ids=[0])
    return r.results[0]["out_y"]
```

```python
from contextlib import ExitStack

import numpy as np

import concourse.bass as bass
from concourse import mybir

ALU = mybir.AluOpType
ACT = mybir.ActivationFunctionType
AX = mybir.AxisListType
F32 = mybir.dt.float32
BF16 = mybir.dt.bfloat16
I32 = mybir.dt.int32
U8 = mybir.dt.uint8

P = 128
B = 16
NH = 16
HD = 8
MC = 4
GB = 4
NG = B // GB
GT = GB * P
M = 20
L = 11
HC = 6
CHUNK_HEAD = (0, 6, 10)
CHUNK_NEW = (0, 0, 2)
ROWS = HC * M
QK_SCALE = float(1.0 / np.sqrt(HD))
EPS = 1e-5
NEG = -9000000000000000.0
MASKED = -1e30

Q_PARTS = (0, 0, 1, 1, 0, 2)
K_PARTS = (0, 1, 0, 1, 2, 0)
ROW_MASK = len(Q_PARTS) * HD
ROW_NEGMAX = ROW_MASK + 1
ROWS_S = ROW_NEGMAX
ROWS_ST = ROW_NEGMAX + 3
N_STACK = 2 * len(Q_PARTS) + 1

W_NAMES = (("wq", P), ("wk", P), ("wv", P), ("wa1", 2 * P), ("cond", B), ("wa2", 2 * P), ("ws", 2 * P),
           ("wo", P), ("w1", MC * P), ("w2", MC * P), ("gq", 2 * P), ("gk", 2 * P), ("gout", 6 * HC * HD))
W_AT = {}
_n = 0
for _name, _size in W_NAMES:
    W_AT[_name] = _n
    _n += _size
W_COLS = _n
W_FIRST = W_AT["wo"]
V_NAMES = (("bq", 1), ("bk", 1), ("bv", 1), ("bo", 0), ("ba1", 2), ("ba2", 2), ("bself", 1), ("b1", MC),
           ("b2", 1), ("gbq", 2), ("gbk", 2), ("gbout", 2))
V_AT = {}
_n = 0
for _name, _size in V_NAMES:
    V_AT[_name] = _n
    _n += _size
V_COLS = _n


def build(nc, x, wall, vecs, bo_row, edge_w, mask_cols, mask_row, adj, out):
    with ExitStack() as ctx:
        def sb(name, shape, dt=F32):
            return ctx.enter_context(nc.sbuf_tensor(name, shape, dt))

        def sem(name):
            return ctx.enter_context(nc.semaphore(name))

        psum = ctx.enter_context(nc.psum_tensor("psum", [P, 8, 512], F32))

        w = sb("w", [P, W_COLS])
        vec = sb("vec", [P, V_COLS])
        bo_all = sb("bo_all", [P, P])
        edge_all = sb("edge_all", [P, L + 1])
        mask_c = sb("mask_c", [P, B], U8)
        mask_r = sb("mask_r", [1, B * P], U8)
        mask_neg = sb("mask_neg", [1, B * P], BF16)
        keep = sb("keep", [P, B])
        ident = sb("ident", [P, P])
        ident_bf = sb("ident_bf", [P, P], BF16)
        ones_col = sb("ones_col", [P, B])
        head_mask = sb("head_mask", [P, NH])
        chunk_mask = sb("chunk_mask", [ROWS, HC * HD])
        batch_mask = sb("batch_mask", [B, B * P])
        ones_bf = batch_mask[0:3, 0:NH * P // 2].bitcast(BF16)
        minus_half = sb("minus_half", [P, GB])
        bq_scaled = sb("bq_scaled", [P, 1])
        gbq_scaled = sb("gbq_scaled", [P, 2])
        bself_bout = sb("bself_bout", [P, 1])
        ada = sb("ada", [P, 4, B])
        q_vec = sb("q_vec", [B, P])

        x_all = sb("x_all", [P, B, P])
        v_mem = sb("v_mem", [P, B * NH * (HD + 1)])
        v_aug = v_mem[:].rearrange("p (b h d) -> p b h d", b=B, h=NH)
        parts = sb("parts", [P, 3, 2, B * P], BF16)
        attn_all = sb("attn_all", [P, B, P])
        sfT_all = v_mem[:, 0:B * P]

        stats = sb("stats", [P, GB, 6])
        mean_var = sb("mean_var", [P, GB, 2])
        var_eps = sb("var_eps", [P, GB])
        carrier = sb("carrier", [P, 1])
        rstd = sb("rstd", [P, GB])
        norm_mem = sb("norm_mem", [P, 2 * GT])
        split_mem = sb("split_mem", [P, 4 * GT])
        xn = norm_mem[:, 0:GT].rearrange("p (b d) -> p b d", b=GB)
        nT = norm_mem[:, GT:2 * GT]
        qk32 = split_mem[:, 0:2 * GT].rearrange("p (s t) -> p s t", s=2)
        rest = split_mem[:, 2 * GT:4 * GT].rearrange("p (s t) -> p s t", s=2)
        SIDE = 2 * NH * GT
        stack_mem = sb("stack_mem", [P, 2 * SIDE], BF16)
        q_all, k_all = stack_mem[0:ROWS_ST, 0:SIDE], stack_mem[0:ROWS_ST, SIDE:2 * SIDE]
        q_stack, k_stack = (t.rearrange("p (g h j t) -> p g h j t", g=2, h=NH, j=GB) for t in (q_all, k_all))
        late_mem = stack_mem[:].bitcast(F32)
        row_max = sb("row_max", [P, NH])
        neg_all = sb("neg_all", [P, P], BF16)
        neg_parts = neg_all[:, 0:3 * NH].rearrange("p (a h) -> p a h", a=3)
        neg_rest = sb("neg_rest", [P, NH])
        neg_rows = sb("neg_rows", [3 * NH, 2, P], BF16)
        probs_mem = sb("probs_mem", [P, 4 * 512])
        probsT = probs_mem[:].rearrange("p (c t) -> p c t", c=4)
        v_fixed = sb("v_fixed", [P, GB, NH, HD + 1])
        o_rows = norm_mem[:].rearrange("p (j t) -> p j t", j=2)
        den_inv = sb("den_inv", [P, NH])
        attn_g, x_bo, x1, xn2 = (split_mem[:, n * GT:(n + 1) * GT].rearrange("p (b d) -> p b d", b=GB)
                                 for n in range(4))
        attnT = norm_mem[:, 0:GT]
        n2T = norm_mem[:, GT:2 * GT]
        x1T_all = late_mem[:, 0:B * P]
        feat_all = late_mem[:, B * P:3 * B * P].rearrange("p (a t) -> p a t", a=2)
        hT = probs_mem[:].rearrange("p (c t) -> p c t", c=MC)
        nonzero = sb("nonzero", [B, GT])
        adj_int = sb("adj_int", [P, B * M * L], I32)
        adj_f = sb("adj_f", [P, B * M * L])
        edge_bias = sb("edge_bias", [P, 2, B * M])
        edge_sum = sb("edge_sum", [P, 2, B * M])
        edge_keep = sb("edge_keep", [P, 2, B * M])
        HM = NH * M
        graph_mem = late_mem[:, 3 * B * P:]
        k_blocks = graph_mem[:, 0:8 * HM].rearrange("p (b d n) -> p b d n", b=GB, d=2)
        gw = graph_mem[:, 8 * HM:12 * HM].rearrange("p (b d n) -> p b d n", b=2, d=2)
        aff = graph_mem[:, 12 * HM:16 * HM].rearrange("p (b d n) -> p b d n", b=2, d=2)
        aff_b = graph_mem[:, 16 * HM:20 * HM].rearrange("p (b d n) -> p b d n", b=2, d=2)
        aff_c = graph_mem[:, 20 * HM:24 * HM].rearrange("p (b d n) -> p b d n", b=2, d=2)
        feat = graph_mem[:, 24 * HM:24 * HM + GB * 2 * P].rearrange("p (b n t) -> p b n t", b=GB, n=2)
        at = 24 * HM + GB * 2 * P
        gqT = graph_mem[:, at:at + GB * 2 * P].rearrange("p (b d t) -> p b d t", b=GB, d=2)
        gkT = graph_mem[:, at + GB * 2 * P:at + GB * 2 * (P + M)].rearrange("p (b d m) -> p b d m", b=GB, d=2)
        key_feat = split_mem[:, 0:GB * HC * M].rearrange("p (b h m) -> p b h m", b=GB, h=HC)
        aff_max = sb("aff_max", [P, 2, 2, NH])
        gwT = probs_mem[0:ROWS, 0:6 * P]
        v_blocks = sb("v_blocks", [ROWS, 2, 6, HC, HD + 1])
        gden_inv = sb("gden_inv", [P, 2 * NH])
        gout_d = probs_mem[:, 6 * P:10 * P].rearrange("p (b d f) -> p b d f", b=2, d=2)
        gout_sum = split_mem[:, 4 * P:6 * P].rearrange("p (b f) -> p b f", b=2)
        g_pre = sb("g_pre", [P, P])
        y_all = attn_all

        names = """x_loaded w_loaded wrest_loaded small_loaded ones_made ident_made ident_bf_made masks_made
            head_mask_a chunk_mask_a chunk_mask_b batch_mask_a batch_mask_b keep_made mask_neg_made bias_made condT_in ada_ready ada_done qvec_ready bank6_read
            stack_in stack_ones_in v_fixed_in
            ln1_stats ln1_mv ln1_eps ln1_rstd xn_ready xT_ready nT_ready q_ready k_ready v_ready qk_copied v_done
            keep_col split_hi split_r split_mid split_done
            s_ready max_done neg_zeroed neg_hi neg_r neg_mid neg_done neg_turned neg_copied st_ready exp_done pv_done
            o_zeroed o_copied o_turned den_done norm_done
            attn_g_ready attn_turned attnT_ready wo_ready x_bo_ready x1_ready ln2_stats ln2_mv ln2_eps ln2_rstd
            xn2_ready x1_turned xn2_turned x1T_ready n2T_ready h_ready gelu_ready y_ready x2T_ready rowsum_ready
            nonzero_ready sf_ready sfT_done
            adj_loaded adj_cast edge_prod edge_bias_done edge_sum_done edge_keep_done edge_neg_done edge_mb_done
            gq_ready gk_ready gqT_done kblk_done aff_ready aff_masked aff_biased aff_maxed aff_centred gw_ready
            gw_turned gwT_done feat_copied key_feat_copied vb_ready vblk_done gpv_ready fT_ready gden_done
            gnorm_done gsum_done gpre_done y_done""".split()
        s = {n: sem(n) for n in names}
        negmax_in = [sem(f"negmax_in{j}") for j in range(GB)]
        out_done = [sem(f"out_done{j}") for j in range(GB)]

        def W(name, n=P, at=0):
            return w[:, W_AT[name] + at:W_AT[name] + at + n]

        def V(name, n=1, at=0):
            return vec[:, V_AT[name] + at:V_AT[name] + at + n]

        def bank(k):
            return psum[:, k, :]

        def group(t, g):
            return t[:, bass.ts(g, GT)]

        def known(b):
            return isinstance(b, int)

        def reuse(eng, semaphore, value, b, first):
            if not known(b) or b >= first:
                eng.wait_ge(semaphore, value)

        block = ctx.enter_context(nc.Block())

        @block.sync
        def _(sp):
            sp.dma_start(x_all[:, 0:GB, :], x[0:GB].rearrange("b t d -> t b d")).then_inc(s["x_loaded"], 16)
            sp.dma_start(w[:, 0:W_FIRST], wall[:, 0:W_FIRST]).then_inc(s["w_loaded"], 16)
            sp.dma_start(x_all[:, GB:, :], x[GB:].rearrange("b t d -> t b d")).then_inc(s["x_loaded"], 16)
            sp.dma_start(w[:, W_FIRST:], wall[:, W_FIRST:]).then_inc(s["wrest_loaded"], 16)
            sp.wait_ge(s["ones_made"], 1)
            for t, row, n in ((q_all, ROW_MASK, 1), (k_all, ROW_NEGMAX, 3)):
                sp.dma_start(t[row:row + n].rearrange("r (a t) -> r a t", t=NH * P),
                             ones_bf[0:n].unsqueeze(1).to_broadcast([n, SIDE // (NH * P), NH * P])).then_inc(
                                 s["stack_ones_in"], 16)
            sp.wait_ge(s["mask_neg_made"], 1)

            def stack(g, turn):
                reuse(sp, s["stack_in"], 16 * N_STACK * g, g, 1)
                sp.wait_ge(s["split_done"], g + 1)
                reuse(sp, s["st_ready"], 4 * GB * (g - 1), g, 2)
                for buf, side, which in ((q_stack, 0, Q_PARTS), (k_stack, 1, K_PARTS)):
                    for n, part in enumerate(which):
                        sp.dma_start(buf[n * HD:(n + 1) * HD, turn].rearrange("r h j t -> r h (j t)"),
                                     parts[:, part, side, bass.ts(g, GT)]).then_inc(s["stack_in"], 16)
                sp.dma_start(k_stack[ROW_MASK:ROW_MASK + 1, turn].rearrange("r h j t -> r h (j t)"),
                             group(mask_neg, g).unsqueeze(1).to_broadcast([1, NH, GT])).then_inc(
                                 s["stack_in"], 16)

            stack(0, 0)
            stack(1, 1)
            with sp.Fori(1, NG // 2) as pair:
                stack(2 * pair, 0)
                stack(2 * pair + 1, 1)

            with sp.Fori(0, NG) as g:
                for j in range(GB):
                    b = GB * g + j
                    sp.wait_ge(s["y_done"], b + 1)
                    sp.dma_start(out[bass.ds(b, 1)].rearrange("b t d -> t b d"), y_all[:, bass.ds(b, 1), :]).then_inc(out_done[j], 16)
            for j in range(GB):
                sp.wait_ge(out_done[j], 16 * NG)

        @block.gpsimd
        def _(pool):
            nc.gpsimd.memset(ones_bf, 1.0).then_inc(s["ones_made"], 1)
            nc.gpsimd.memset(ident[:], 0.0).then_inc(s["ident_made"], 1)
            pool.wait_ge(s["ident_made"], 1)
            nc.gpsimd.affine_select(out=ident[:], in_=ident[:], compare_op=ALU.not_equal, fill=1.0, base=0,
                                    pattern=[[-1, P]], channel_multiplier=1).then_inc(s["ident_made"], 1)
            nc.gpsimd.memset(minus_half[:], -0.5).then_inc(s["masks_made"], 1)
            pool.wait_ge(s["ident_made"], 2)
            nc.gpsimd.tensor_copy(ident_bf[:], ident[:]).then_inc(s["ident_bf_made"], 1)

            nc.gpsimd.memset(neg_all[:], 0.0).then_inc(s["neg_zeroed"], 1)
            pool.wait_ge(s["masks_made"], 1)

            def rstd_of(eps_sem, rstd_sem, g):
                pool.wait_ge(eps_sem, g + 1)
                nc.gpsimd.tensor_tensor(rstd[:], var_eps[:], minus_half[:], ALU.pow).then_inc(rstd_sem, 1)

            with pool.Fori(0, NG) as g:
                rstd_of(s["ln1_eps"], s["ln1_rstd"], g)

            pool.wait_ge(s["keep_made"], 1)
            nc.gpsimd.tensor_copy(v_aug[:, :, :, HD], keep[:].unsqueeze(2).to_broadcast([P, B, NH])).then_inc(
                s["keep_col"], 1)

            nc.gpsimd.memset(head_mask[:], 1.0).then_inc(s["head_mask_a"], 1)
            nc.gpsimd.memset(chunk_mask[:], 1.0).then_inc(s["chunk_mask_a"], 1)
            pool.wait_ge(s["stack_ones_in"], 16 * 2)
            nc.gpsimd.memset(batch_mask[:], 1.0).then_inc(s["batch_mask_a"], 1)
            nc.gpsimd.memset(ones_col[:], 1.0).then_inc(s["masks_made"], 1)

            def band(t, sem_a, width, pattern):
                pool.wait_ge(sem_a, 1)
                lo = [[-width * n if n else 0, c] for n, c in pattern]
                nc.gpsimd.affine_select(out=t, in_=t, compare_op=ALU.is_ge, fill=0.0, base=0,
                                        pattern=lo, channel_multiplier=1).then_inc(sem_a, 1)
                pool.wait_ge(sem_a, 2)
                hi = [[width * n if n else 0, c] for n, c in pattern]
                nc.gpsimd.affine_select(out=t, in_=t, compare_op=ALU.is_ge, fill=0.0, base=width - 1,
                                        pattern=hi, channel_multiplier=-1).then_inc(s["masks_made"], 1)

            band(head_mask[:], s["head_mask_a"], HD, [[1, NH]])
            band(chunk_mask[:].rearrange("p (h d) -> p h d", h=HC), s["chunk_mask_a"], M, [[1, HC], [0, HD]])
            band(batch_mask[:].rearrange("p (b t) -> p b t", b=B), s["batch_mask_a"], 1, [[1, B], [0, P]])
            pool.wait_ge(s["masks_made"], 5)
            for j in range(2):
                nc.gpsimd.tensor_copy(
                    v_blocks[:, j, :, :, HD],
                    chunk_mask[:].rearrange("p (h d) -> p h d", h=HC)[:, :, 0].unsqueeze(1).to_broadcast([ROWS, 6, HC])
                ).then_inc(s["masks_made"], 1)

            for d in range(2):
                if d:
                    pool.wait_ge(s["edge_bias_done"], d)
                pool.dma_start(adj_int[:], adj[d]).then_inc(s["adj_loaded"], 16)
                pool.wait_ge(s["adj_loaded"], 16 * (d + 1))
                if d:
                    pool.wait_ge(s["edge_sum_done"], d)
                nc.gpsimd.tensor_copy(adj_f[:], adj_int[:]).then_inc(s["adj_cast"], 1)
                pool.wait_ge(s["adj_cast"], d + 1)
                nc.gpsimd.tensor_tensor(
                    adj_int[:].bitcast(F32).rearrange("p (e l) -> p e l", l=L), adj_f[:].rearrange("p (e l) -> p e l", l=L),
                    edge_all[:, 0:L].unsqueeze(1).to_broadcast([P, B * M, L]), ALU.mult).then_inc(s["edge_prod"], 1)

            def fixed_copies(g):
                pool.wait_ge(s["norm_done"], GB * g + GB)
                reuse(pool, s["attn_turned"], g, g, 1)
                nc.gpsimd.tensor_copy(attn_g, attn_all[:, bass.ts(g, GB), :]).then_inc(s["attn_g_ready"], 1)
                reuse(pool, s["x1_ready"], g, g, 1)
                nc.gpsimd.tensor_tensor(x_bo, x_all[:, bass.ts(g, GB), :],
                                        bo_all[:].unsqueeze(1).to_broadcast([P, GB, P]), ALU.add).then_inc(s["x_bo_ready"], 1)
                rstd_of(s["ln2_eps"], s["ln2_rstd"], g)

            fixed_copies(0)
            with pool.Fori(1, NG) as g:
                fixed_copies(g)

            def add_bias(b, j):
                pool.wait_ge(s["aff_masked"], b + 1)
                reuse(pool, s["aff_maxed"], b - 1, b, 2)
                mb = edge_bias[:, :, bass.ds(b * M, M)]
                for d in range(2):
                    nc.gpsimd.tensor_tensor(
                        aff_b[:, j % 2, d, :].rearrange("p (h m) -> p h m", h=NH), aff[:, j % 2, d, :].rearrange("p (h m) -> p h m", h=NH),
                        mb[:, d, :].unsqueeze(1).to_broadcast([P, NH, M]), ALU.add).then_inc(s["aff_biased"], 1)

            def centre(b, j):
                pool.wait_ge(s["aff_maxed"], b + 1)
                reuse(pool, s["gw_ready"], b - 1, b, 2)
                nc.gpsimd.tensor_tensor(
                    aff_c[:, j % 2].rearrange("p d (h m) -> p (d h) m", h=NH), aff_b[:, j % 2].rearrange("p d (h m) -> p (d h) m", h=NH),
                    aff_max[:, j % 2].rearrange("p d h -> p (d h)").unsqueeze(2).to_broadcast([P, 2 * NH, M]),
                    ALU.subtract).then_inc(s["aff_centred"], 1)

            def sum_directions(b, j):
                pool.wait_ge(s["gnorm_done"], b + 1)
                reuse(pool, s["gpre_done"], b - 1, b, 2)
                nc.gpsimd.tensor_tensor(gout_sum[:, j % 2], gout_d[:, j % 2, 0], gout_d[:, j % 2, 1], ALU.add).then_inc(s["gsum_done"], 1)

            def pool_step(g, j, n=None):
                b = GB * g + j
                if not known(g) or 1 <= b <= B:
                    add_bias(b - 1, (j - 1) % GB)
                if not known(g) or 4 <= b < B + 4:
                    sum_directions(b - 4, j)
                if not known(g) or 1 <= b <= B:
                    centre(b - 1, (j - 1) % GB)

            pool.wait_ge(s["edge_mb_done"], 1)
            for j in range(2 * GB):
                pool_step(j // GB, j % GB)
            with pool.Fori(2, NG) as g:
                for j in range(GB):
                    pool_step(g, j)
            for j in range(GB):
                pool_step(NG, j)

        @block.scalar
        def _(act):
            act.dma_start(vec[:], vecs).then_inc(s["small_loaded"], 16)
            act.dma_start(mask_c[:], mask_cols).then_inc(s["small_loaded"], 16)
            act.dma_start(mask_r[:], mask_row).then_inc(s["small_loaded"], 16)
            act.dma_start(bo_all[:], bo_row.to_broadcast([P, P])).then_inc(s["small_loaded"], 16)
            act.dma_start(edge_all[:], edge_w.to_broadcast([P, L + 1])).then_inc(s["small_loaded"], 16)
            act.wait_ge(s["ada_done"], 4)
            act.wait_ge(s["bias_made"], 3)

            def project_in(g):
                act.wait_ge(s["xT_ready"], g + 1)
                for j in range(GB):
                    nc.scalar.activation(nT[:, bass.ts(j, P)], psum[:, 0, bass.ts(j, P)], ACT.Identity,
                                         scale=ada[:, 0, bass.ds(g * GB + j, 1)],
                                         bias=ada[:, 1, bass.ds(g * GB + j, 1)]).then_inc(s["nT_ready"], 1)
                act.wait_ge(s["q_ready"], g + 1)
                reuse(act, s["split_r"], g, g, 1)
                nc.scalar.activation(qk32[:, 0, :], bank(1), ACT.Identity, scale=QK_SCALE, bias=bq_scaled[:]).then_inc(s["qk_copied"], 1)
                act.wait_ge(s["k_ready"], g + 1)
                nc.scalar.activation(qk32[:, 1, :], bank(2), ACT.Identity, bias=V("bk")).then_inc(s["qk_copied"], 1)

            project_in(0)
            with act.Fori(1, NG) as g:
                project_in(g)

            def fix_values(b, j):
                reuse(act, s["pv_done"], 4 * (b - GB) + 4, b, GB)
                act.wait_ge(s["v_done"], B)
                act.wait_ge(s["keep_col"], 1)
                nc.scalar.copy(v_fixed[:, j], v_aug[:, bass.ds(b, 1)].rearrange("p b h d -> p (b h) d")).then_inc(
                    s["v_fixed_in"], 1)

            def exp(b, c):
                quad = 4 * b + c
                act.wait_ge(s["st_ready"], quad + 1)
                reuse(act, s["pv_done"], quad - 3, b, 1)
                nc.scalar.activation(probsT[:, c, :], bank(6 + c % 2), ACT.Exp).then_inc(s["exp_done"], 1)

            def copy_negmax(g, j):
                b = GB * g + j
                act.wait_ge(s["neg_turned"], b + 1)
                if not known(g) or b >= 2:
                    act.wait_ge(negmax_in[(j - 2) % GB], 16 * (g + (j >= 2)))
                nc.scalar.copy(neg_rows[:, j % 2, :], bank(1)[0:3 * NH, 0:P // 2].bitcast(BF16)).then_inc(s["neg_copied"], 1)
                act.wait_ge(s["neg_copied"], b + 1)
                act.dma_start(q_stack[ROW_NEGMAX:ROW_NEGMAX + 3, bass.ds(g & 1, 1), :, j, :].rearrange("r g h t -> r (g h) t"), neg_rows[:, j % 2, :]).then_inc(negmax_in[j], 16)

            def copy_values(b, j):
                act.wait_ge(s["pv_done"], 4 * b + 4)
                reuse(act, s["o_turned"], b - 1, b, 2)
                nc.scalar.copy(o_rows[:, j % 2, :], bank(3 * (j % 2))).then_inc(s["o_copied"], 1)

            def act_step(g, j):
                b = GB * g + j
                if not known(g) or 2 <= b < B + 2:
                    exp(b - 2, 0)
                    exp(b - 2, 1)
                if not known(g) or 3 <= b < B + 3:
                    copy_values(b - 3, (j - 3) % GB)
                if not known(g) or 1 <= b <= B:
                    fix_values(b - 1, (j - 1) % GB)
                    copy_negmax(g - (j == 0), (j - 1) % GB)
                if not known(g) or 2 <= b < B + 2:
                    exp(b - 2, 2)
                    exp(b - 2, 3)

            for j in range(GB):
                act_step(0, j)
            with act.Fori(1, NG) as g:
                for j in range(GB):
                    act_step(g, j)
            for j in range(3):
                act_step(NG, j)

            def attn_out(g):
                act.wait_ge(s["attn_turned"], g + 1)
                reuse(act, s["wo_ready"], g, g, 1)
                nc.scalar.activation(attnT, bank(0), ACT.Identity, bias=V("bv")).then_inc(s["attnT_ready"], 1)

            def modulate(g):
                act.wait_ge(s["xn2_turned"], g + 1)
                reuse(act, s["h_ready"], MC * g, g, 1)
                for j in range(GB):
                    nc.scalar.activation(n2T[:, bass.ts(j, P)], psum[:, 3, bass.ts(j, P)], ACT.Identity,
                                         scale=ada[:, 2, bass.ds(g * GB + j, 1)],
                                         bias=ada[:, 3, bass.ds(g * GB + j, 1)]).then_inc(s["n2T_ready"], 1)

            def gelu(g, c):
                act.wait_ge(s["h_ready"], MC * g + c + 1)
                nc.scalar.activation(hT[:, c, :], bank(4 + c % 2), ACT.Gelu, bias=V("b1", 1, c)).then_inc(s["gelu_ready"], 1)

            def self_features(g):
                act.wait_ge(s["sf_ready"], g + 1)
                nc.scalar.activation(group(sfT_all, g), bank(6), ACT.Identity, bias=V("bself")).then_inc(s["sfT_done"], 1)
                nc.scalar.activation(feat_all[:, 1, bass.ts(g, GT)], bank(6), ACT.Identity, bias=bself_bout[:]).then_inc(s["bank6_read"], 1)

            attn_out(0)
            modulate(0)
            with act.Fori(0, NG - 1) as g:
                attn_out(g + 1)
                for c in range(MC):
                    gelu(g, c)
                modulate(g + 1)
                self_features(g)
            for c in range(MC):
                gelu(NG - 1, c)
            self_features(NG - 1)

            def queries_and_keys(b, j):
                act.wait_ge(s["gq_ready"], b + 1)
                reuse(act, s["aff_ready"], b - GB + 1, b, GB)
                for d in range(2):
                    nc.scalar.activation(gqT[:, j, d, :], bank(0)[:, d * P:(d + 1) * P], ACT.Identity, scale=QK_SCALE,
                                         bias=gbq_scaled[:, d:d + 1]).then_inc(s["gqT_done"], 1)
                for d in range(2):
                    nc.scalar.activation(gkT[:, j, d, :], bank(0)[:, 2 * P + d * M:2 * P + (d + 1) * M], ACT.Identity,
                                         bias=V("gbk", 1, d)).then_inc(s["gqT_done"], 1)

            def copies(b, j):
                reuse(act, s["fT_ready"], b - GB + 1, b, GB)
                nc.scalar.copy(feat[:, j], feat_all[:, :, bass.ts(b, P)]).then_inc(s["feat_copied"], 1)
                reuse(act, s["vb_ready"], b - GB + 1, b, GB)
                nc.scalar.copy(key_feat[:, j], sfT_all[:, bass.ds(b * P, M)].unsqueeze(1).to_broadcast([P, HC, M])
                                      ).then_inc(s["key_feat_copied"], 1)

            def graph_exp(b, j):
                act.wait_ge(s["aff_centred"], b + 1)
                reuse(act, s["gw_turned"], b - 1, b, 2)
                nc.scalar.activation(gw[:, j % 2], aff_c[:, j % 2], ACT.Exp).then_inc(s["gw_ready"], 1)

            def graph_weights(b, j):
                act.wait_ge(s["gw_turned"], b + 1)
                reuse(act, s["gpv_ready"], b, b, 1)
                nc.scalar.copy(gwT.rearrange("p (d t) -> p d t", d=2),
                               psum[0:ROWS, 3:5, 0:3 * P]).then_inc(s["gwT_done"], 1)

            def graph_act_step(g, j):
                b = GB * g + j
                if not known(g) or 2 <= b < B + 2:
                    graph_exp(b - 2, (j - 2) % GB)
                if not known(g) or b < B:
                    copies(b, j)
                if not known(g) or 2 <= b < B + 2:
                    graph_weights(b - 2, (j - 2) % GB)
                if not known(g) or b + 2 < B:
                    queries_and_keys(b + 2, (j + 2) % GB)

            act.wait_ge(s["bank6_read"], NG + 1)
            queries_and_keys(0, 0)
            queries_and_keys(1, 1)
            for j in range(GB):
                graph_act_step(0, j)
            with act.Fori(1, NG - 1) as g:
                for j in range(GB):
                    graph_act_step(g, j)
            for j in range(2 * GB):
                graph_act_step(NG - 1 + j // GB, j % GB)

        @block.vector
        def _(dve):
            dve.wait_ge(s["small_loaded"], 16 * 5)
            nc.vector.tensor_scalar(keep[:], mask_c[:], -1.0, 1.0, ALU.mult, ALU.add).then_inc(s["keep_made"], 1)
            nc.vector.tensor_scalar(mask_neg[:], mask_r[:], MASKED, None, ALU.mult).then_inc(s["mask_neg_made"], 1)
            nc.vector.tensor_scalar(bq_scaled[:], V("bq"), QK_SCALE, None, ALU.mult).then_inc(s["bias_made"], 1)
            nc.vector.tensor_scalar(gbq_scaled[:], V("gbq", 2), QK_SCALE, None, ALU.mult).then_inc(s["bias_made"], 1)
            nc.vector.scalar_tensor_tensor(bself_bout[:], V("bself"), V("gbout", 1, 0), V("gbout", 1, 1),
                                           ALU.add, ALU.add).then_inc(s["bias_made"], 1)

            def layer_stats(src, stats_sem, mv_sem, eps_sem, g):
                for j in range(GB):
                    nc.vector.bn_stats(stats[:, j, :], src(j)).then_inc(stats_sem, 1)
                dve.wait_ge(stats_sem, GB * g + GB)
                nc.vector.memset(carrier[:], 0.0)
                for j in range(GB):
                    nc.vector.bn_aggr(mean_var[:, j, :], stats[:, j, :]).then_inc(mv_sem, 1)
                dve.wait_ge(mv_sem, GB * g + GB)
                nc.vector.tensor_scalar(var_eps[:], mean_var[:, :, 1], EPS, None, ALU.add).then_inc(eps_sem, 1)

            def normalise(dst, src, ready_sem):
                for j in range(GB):
                    nc.vector.tensor_scalar(dst[:, j, :], src(j), mean_var[:, j, 0:1], rstd[:, j:j + 1],
                                            ALU.subtract, ALU.mult).then_inc(ready_sem, 1)

            def batch_of_x(g, j):
                return x_all[:, bass.ds(g * GB + j, 1), :].rearrange("p b d -> p (b d)")

            def ln1(g):
                dve.wait_ge(s["x_loaded"], 32)
                layer_stats(lambda j: batch_of_x(g, j), s["ln1_stats"], s["ln1_mv"], s["ln1_eps"], g)
                dve.wait_ge(s["ln1_rstd"], g + 1)
                reuse(dve, s["xT_ready"], g, g, 1)
                normalise(xn, lambda j: batch_of_x(g, j), s["xn_ready"])

            def values_and_split(g):
                dve.wait_ge(s["v_ready"], g + 1)
                for j in range(GB):
                    b = g * GB + j
                    nc.vector.tensor_scalar(
                        v_aug[:, bass.ds(b, 1), :, 0:HD].rearrange("p b h d -> p (b h) d"),
                        bank(3)[:, bass.ts(j, P)].rearrange("p (h d) -> p h d", h=NH), keep[:, bass.ds(b, 1)], None, ALU.mult
                    ).then_inc(s["v_done"], 1)
                dve.wait_ge(s["qk_copied"], 2 * g + 2)
                part = [parts[:, n, :, bass.ts(g, GT)] for n in range(3)]
                nc.vector.tensor_copy(part[0], qk32).then_inc(s["split_hi"], 1)
                dve.wait_ge(s["split_hi"], g + 1)
                nc.vector.tensor_tensor(rest, qk32, part[0], ALU.subtract).then_inc(s["split_r"], 1)
                dve.wait_ge(s["split_r"], g + 1)
                nc.vector.tensor_copy(part[1], rest).then_inc(s["split_mid"], 1)
                dve.wait_ge(s["split_mid"], g + 1)
                nc.vector.tensor_tensor(part[2], rest, part[1], ALU.subtract).then_inc(s["split_done"], 1)

            dve.wait_ge(s["keep_made"], 1)
            ln1(0)
            dve.wait_ge(s["ada_ready"], 4)
            for n, name in enumerate(("ba1", "ba1", "ba2", "ba2")):
                nc.vector.tensor_scalar(ada[:, n, :], bank(7)[:, n * B:(n + 1) * B], V(name, 1, n % 2), 1.0 - n % 2,
                                        ALU.add, ALU.add).then_inc(s["ada_done"], 1)
            dve.wait_ge(s["qvec_ready"], 1)
            nc.vector.tensor_copy(q_vec[:], psum[0:B, 6, 0:P]).then_inc(s["bank6_read"], 1)
            with dve.Fori(0, NG - 1) as g:
                ln1(g + 1)
                values_and_split(g)
            values_and_split(NG - 1)

            def quad_max(b, c):
                dve.wait_ge(s["s_ready"], 4 * b + c + 1)
                nc.vector.tensor_reduce(row_max[:, 4 * c:4 * c + 4], bank(4 + c % 2).rearrange("p (h k) -> p h k", h=4),
                                        AX.X, ALU.max).then_inc(s["max_done"], 1)

            def split_negmax(b):
                dve.wait_ge(s["max_done"], 4 * b + 4)
                reuse(dve, s["neg_turned"], b, b, 1)
                nc.vector.tensor_scalar(neg_parts[:, 0, :], row_max[:], -1.0, None, ALU.mult).then_inc(s["neg_hi"], 1)
                dve.wait_ge(s["neg_hi"], b + 1)
                nc.vector.scalar_tensor_tensor(neg_rest[:], row_max[:], -1.0, neg_parts[:, 0, :], ALU.mult,
                                               ALU.subtract).then_inc(s["neg_r"], 1)
                dve.wait_ge(s["neg_r"], b + 1)
                nc.vector.tensor_copy(neg_parts[:, 1, :], neg_rest[:]).then_inc(s["neg_mid"], 1)
                dve.wait_ge(s["neg_mid"], b + 1)
                nc.vector.tensor_tensor(neg_parts[:, 2, :], neg_rest[:], neg_parts[:, 1, :], ALU.subtract).then_inc(
                    s["neg_done"], 1)

            def attn_normalise(b):
                dve.wait_ge(s["o_turned"], b + 1)
                o = bank(2).rearrange("p (h d) -> p h d", h=NH)
                nc.vector.reciprocal(den_inv[:], o[:, :, HD]).then_inc(s["den_done"], 1)
                dve.wait_ge(s["den_done"], b + 1)
                nc.vector.tensor_tensor(attn_all[:, bass.ds(b, 1), :].rearrange("p b (h d) -> p (b h) d", h=NH), o[:, :, 0:HD],
                                        den_inv[:].unsqueeze(2).to_broadcast([P, NH, HD]), ALU.mult).then_inc(
                                            s["norm_done"], 1)

            def edge_total(d):
                dve.wait_ge(s["adj_cast"], d + 1)
                nc.vector.tensor_reduce(edge_sum[:, d, :], adj_f[:].rearrange("p (e l) -> p e l", l=L),
                                        AX.X, ALU.add).then_inc(s["edge_sum_done"], 1)

            def edge_weighted(d):
                dve.wait_ge(s["edge_prod"], d + 1)
                nc.vector.tensor_reduce(edge_bias[:, d, :], adj_int[:].bitcast(F32).rearrange("p (e l) -> p e l", l=L),
                                        AX.X, ALU.add).then_inc(s["edge_bias_done"], 1)

            def dve_step(g, j):
                b = GB * g + j
                for c in range(4):
                    if not known(g) or b < B:
                        quad_max(b, c)
                    if c == 1 and (not known(g) or 4 <= b < B + 4):
                        attn_normalise(b - 4)
                if not known(g) or b < B:
                    split_negmax(b)

            dve.wait_ge(s["nT_ready"], B)
            for k in (0, 3):
                nc.vector.memset(bank(k), 0.0).then_inc(s["o_zeroed"], 1)
            dve.wait_ge(s["neg_zeroed"], 1)
            for j in range(GB):
                dve_step(0, j)
                if j == 1:
                    edge_total(0)
                if j == 2:
                    edge_weighted(0)
            with dve.Fori(1, NG) as g:
                for j in range(GB):
                    dve_step(g, j)
            for j in range(GB):
                if j == 0:
                    edge_total(1)
                if j == 1:
                    edge_weighted(1)
                dve_step(NG, j)

            def x1_and_norm(g):
                dve.wait_ge(s["wo_ready"], g + 1)
                dve.wait_ge(s["x_bo_ready"], g + 1)
                reuse(dve, s["x1_turned"], g, g, 1)
                nc.vector.tensor_tensor(x1.rearrange("p b d -> p (b d)"), bank(1), x_bo.rearrange("p b d -> p (b d)"),
                                        ALU.add).then_inc(s["x1_ready"], 1)
                dve.wait_ge(s["x1_ready"], g + 1)
                layer_stats(lambda j: x1[:, j, :], s["ln2_stats"], s["ln2_mv"], s["ln2_eps"], g)
                dve.wait_ge(s["ln2_rstd"], g + 1)
                reuse(dve, s["xn2_turned"], g, g, 1)
                normalise(xn2, lambda j: x1[:, j, :], s["xn2_ready"])
                dve.wait_ge(s["x1_turned"], g + 1)
                nc.vector.tensor_scalar(group(x1T_all, g), bank(2), V("b2"), None, ALU.add).then_inc(s["x1T_ready"], 1)

            def x2_and_rows(g):
                dve.wait_ge(s["y_ready"], g + 1)
                dve.wait_ge(s["x1T_ready"], g + 1)
                nc.vector.tensor_tensor(feat_all[:, 0, bass.ts(g, GT)], bank(6), group(x1T_all, g), ALU.add).then_inc(
                    s["x2T_ready"], 1)
                dve.wait_ge(s["rowsum_ready"], g + 1)
                nc.vector.scalar_tensor_tensor(nonzero[:], psum[0:B, 7, :], 0.0, group(batch_mask, g), ALU.not_equal,
                                               ALU.mult).then_inc(s["nonzero_ready"], 1)

            x1_and_norm(0)
            with dve.Fori(0, NG - 1) as g:
                x1_and_norm(g + 1)
                x2_and_rows(g)
            dve.wait_ge(s["edge_sum_done"], 2)
            nc.vector.tensor_scalar(edge_keep[:], edge_sum[:], 0.0, None, ALU.is_gt).then_inc(s["edge_keep_done"], 1)
            dve.wait_ge(s["edge_keep_done"], 1)
            nc.vector.tensor_scalar(edge_sum[:], edge_keep[:], -NEG, NEG, ALU.mult, ALU.add).then_inc(s["edge_neg_done"], 1)
            dve.wait_ge(s["edge_neg_done"], 1)
            dve.wait_ge(s["edge_bias_done"], 2)
            nc.vector.scalar_tensor_tensor(edge_bias[:], edge_bias[:], edge_all[:, L:L + 1], edge_sum[:], ALU.add,
                                           ALU.add).then_inc(s["edge_mb_done"], 1)

            x2_and_rows(NG - 1)

            def key_blocks(b, j):
                dve.wait_ge(s["gqT_done"], 4 * b + 4)
                reuse(dve, s["aff_ready"], b - GB + 1, b, GB)
                nc.vector.tensor_tensor(
                    k_blocks[:, j].rearrange("p d (h m) -> p d h m", h=NH),
                    gkT[:, j].unsqueeze(2).to_broadcast([P, 2, NH, M]),
                    head_mask[:].unsqueeze(1).unsqueeze(3).to_broadcast([P, 2, NH, M]), ALU.mult).then_inc(s["kblk_done"], 1)

            def mask_aff(b, j):
                dve.wait_ge(s["aff_ready"], b + 1)
                reuse(dve, s["aff_biased"], 2 * (b - 2) + 2, b, 2)
                nc.vector.tensor_tensor(
                    aff[:, j % 2].rearrange("p d (h m) -> p d h m", h=NH),
                    psum[:, 6:8, 0:NH * M].rearrange("p d (h m) -> p d h m", h=NH),
                    edge_keep[:, :, bass.ds(b * M, M)].unsqueeze(2).to_broadcast([P, 2, NH, M]), ALU.mult
                ).then_inc(s["aff_masked"], 1)

            def max_aff(b, j):
                dve.wait_ge(s["aff_biased"], 2 * b + 2)
                reuse(dve, s["aff_centred"], b - 1, b, 2)
                nc.vector.tensor_reduce(aff_max[:, j % 2].rearrange("p d h -> p (d h)"),
                                        aff_b[:, j % 2].rearrange("p d (h m) -> p (d h) m", h=NH), AX.X, ALU.max).then_inc(s["aff_maxed"], 1)

            def value_blocks(b, j):
                dve.wait_ge(s["vb_ready"], b + 1)
                reuse(dve, s["gpv_ready"], b - 1, b, 2)
                nc.vector.tensor_tensor(
                    v_blocks[:, j % 2, :, :, 0:HD], psum[0:ROWS, 2, 0:6 * HC * HD].rearrange("p (k h d) -> p k h d", k=6, h=HC),
                    chunk_mask[:].rearrange("p (h d) -> p h d", h=HC).unsqueeze(1).to_broadcast([ROWS, 6, HC, HD]), ALU.mult
                ).then_inc(s["vblk_done"], 1)

            def graph_normalise(b, j):
                dve.wait_ge(s["gpv_ready"], b + 1)
                o = bank(5)[:, 0:2 * NH * (HD + 1)].rearrange("p (h d) -> p h d", h=2 * NH)
                nc.vector.reciprocal(gden_inv[:], o[:, :, HD]).then_inc(s["gden_done"], 1)
                dve.wait_ge(s["gden_done"], b + 1)
                reuse(dve, s["gsum_done"], b - 1, b, 2)
                nc.vector.tensor_tensor(gout_d[:, j % 2].rearrange("p d (h e) -> p (d h) e", h=NH), o[:, :, 0:HD],
                                        gden_inv[:].unsqueeze(2).to_broadcast([P, 2 * NH, HD]), ALU.mult).then_inc(
                                            s["gnorm_done"], 1)

            def finish(b, j):
                dve.wait_ge(s["gsum_done"], b + 1)
                dve.wait_ge(s["fT_ready"], b + 1)
                nc.vector.tensor_tensor(g_pre[:], bank(1)[:, P:2 * P], gout_sum[:, j % 2], ALU.add).then_inc(s["gpre_done"], 1)
                dve.wait_ge(s["gpre_done"], b + 1)
                nc.vector.scalar_tensor_tensor(y_all[:, bass.ds(b, 1), :].rearrange("p b d -> p (b d)"), g_pre[:], 0.0, bank(1)[:, 0:P], ALU.max, ALU.add).then_inc(
                    s["y_done"], 1)

            def graph_dve_step(g, j):
                b = GB * g + j
                if not known(g) or 1 <= b <= B:
                    mask_aff(b - 1, (j - 1) % GB)
                if not known(g) or 4 <= b < B + 4:
                    graph_normalise(b - 4, j)
                if not known(g) or b + 1 < B:
                    key_blocks(b + 1, (j + 1) % GB)
                if not known(g) or 1 <= b <= B:
                    max_aff(b - 1, (j - 1) % GB)
                if not known(g) or 2 <= b < B + 2:
                    value_blocks(b - 2, (j - 2) % GB)
                if not known(g) or 5 <= b < B + 5:
                    finish(b - 5, (j - 5) % GB)

            dve.wait_ge(s["masks_made"], 5 + 2)
            key_blocks(0, 0)
            for j in range(2 * GB):
                graph_dve_step(j // GB, j % GB)
            with dve.Fori(2, NG - 1) as g:
                for j in range(GB):
                    graph_dve_step(g, j)
            for j in range(2 * GB + 1):
                graph_dve_step(NG - 1 + j // GB, j % GB)

        @block.tensor
        def _(pe):
            def mm(dst, lhsT, rhs, start=True, stop=True):
                return nc.tensor.matmul(dst, lhsT, rhs, start=start, stop=stop)

            pe.wait_ge(s["w_loaded"], 16)
            for n in range(4):
                mm(bank(7)[:, n * B:(n + 1) * B], W(("wa1", "wa2")[n // 2], P, n % 2 * P), W("cond", B)).then_inc(s["ada_ready"], 1)
            mm(psum[0:B, 6, 0:P], W("cond", B), W("ws", P, P)).then_inc(s["qvec_ready"], 1)
            pe.wait_ge(s["ident_made"], 2)
            def project_in(g):
                pe.wait_ge(s["xn_ready"], GB * g + GB)
                for j in range(GB):
                    t = nc.tensor.transpose(bank(0)[:, j * P:(j + 1) * P], xn[:, j, :], ident[:])
                t.then_inc(s["xT_ready"], 1)
                pe.wait_ge(s["nT_ready"], GB * g + GB)
                reuse(pe, s["qk_copied"], 2 * g, g, 1)
                mm(bank(1), W("wq"), nT).then_inc(s["q_ready"], 1)
                mm(bank(2), W("wk"), nT).then_inc(s["k_ready"], 1)
                reuse(pe, s["v_done"], GB * g, g, 1)
                for j in range(GB):
                    t = mm(bank(3)[:, j * P:(j + 1) * P], nT[:, j * P:(j + 1) * P], W("wv"))
                t.then_inc(s["v_ready"], 1)

            project_in(0)
            with pe.Fori(1, NG) as g:
                project_in(g)

            def stacked(t, rows, g, j, h, slot=None):
                return t[0:rows, bass.ds(g % 2 if rows == ROWS_ST else g & 1, 1), h, j, :].rearrange("r g t -> r (g t)")

            def scores(g, j, c):
                quad = 4 * (GB * g + j) + c
                if c == 0 and j == 0:
                    pe.wait_ge(s["stack_in"], 16 * N_STACK * (g + 1))
                reuse(pe, s["max_done"], quad - 1, quad, 2)
                for n in range(4):
                    h = 4 * c + n
                    t = mm(bank(4 + c % 2)[:, n * P:(n + 1) * P], stacked(q_stack, ROWS_S, g, j, h), stacked(k_stack, ROWS_S, g, j, h))
                t.then_inc(s["s_ready"], 1)

            def turn_negmax(b):
                pe.wait_ge(s["neg_done"], b + 1)
                reuse(pe, s["neg_copied"], b, b, 1)
                nc.tensor.transpose(bank(1)[:, 0:P // 2].bitcast(BF16), neg_all[:], ident_bf[:]).then_inc(s["neg_turned"], 1)

            def scores_T(g, j, c):
                quad = 4 * (GB * g + j) + c
                if c == 0:
                    pe.wait_ge(negmax_in[j], 16 * (g + 1))
                reuse(pe, s["exp_done"], quad - 1, quad, 2)
                for n in range(4):
                    h = 4 * c + n
                    t = mm(bank(6 + c % 2)[:, n * P:(n + 1) * P], stacked(k_stack, ROWS_ST, g, j, h), stacked(q_stack, ROWS_ST, g, j, h))
                t.then_inc(s["st_ready"], 1)

            def weighted_values(b, j, c):
                pe.wait_ge(s["exp_done"], 4 * b + c + 1)
                if c == 0:
                    pe.wait_ge(s["v_fixed_in"], b + 1)
                    reuse(pe, s["o_copied"], b - 1, b, 2)
                for n in range(4):
                    t = mm(psum[32 * n:32 * n + HD + 1, 3 * (j % 2), c * P:(c + 1) * P], v_fixed[:, j, 4 * c + n, :],
                           probsT[:, c, n * P:(n + 1) * P])
                t.then_inc(s["pv_done"], 1)

            def turn_values(b, j):
                pe.wait_ge(s["o_copied"], b + 1)
                reuse(pe, s["norm_done"], b, b, 1)
                for c in range(4):
                    t = nc.tensor.transpose(bank(2)[:, c * P:(c + 1) * P], o_rows[:, j % 2, c * P:(c + 1) * P], ident[:])
                t.then_inc(s["o_turned"], 1)

            def pe_step(g, j):
                b = GB * g + j
                for c in range(4):
                    if not known(g) or b < B:
                        scores(g, j, c)
                    if c == 1 and (not known(g) or 1 <= b <= B):
                        turn_negmax(b - 1)
                    if not known(g) or 2 <= b < B + 2:
                        scores_T(g - (j < 2), (j - 2) % GB, c)
                    if c == 0:
                        if not known(g) or 3 <= b < B + 3:
                            weighted_values(b - 3, (j - 3) % GB, 3)
                    elif not known(g) or 2 <= b < B + 2:
                        weighted_values(b - 2, (j - 2) % GB, c - 1)
                if not known(g) or 3 <= b < B + 3:
                    turn_values(b - 3, (j - 3) % GB)

            pe.wait_ge(s["stack_ones_in"], 16 * 2)
            pe.wait_ge(s["ident_bf_made"], 1)
            pe.wait_ge(s["o_zeroed"], 2)
            for j in range(GB):
                pe_step(0, j)
            with pe.Fori(1, NG) as g:
                for j in range(GB):
                    pe_step(g, j)
            for j in range(3):
                pe_step(NG, j)

            pe.wait_ge(s["wrest_loaded"], 16)
            pe.wait_ge(s["norm_done"], B)
            pe.wait_ge(s["neg_copied"], B)
            pe.wait_ge(s["max_done"], 4 * B)
            pe.wait_ge(s["exp_done"], 4 * B)
            pe.wait_ge(s["masks_made"], 5 + 2)

            def turn_attn(g):
                pe.wait_ge(s["attn_g_ready"], g + 1)
                reuse(pe, s["attnT_ready"], g, g, 1)
                for j in range(GB):
                    t = nc.tensor.transpose(bank(0)[:, j * P:(j + 1) * P], attn_g[:, j, :], ident[:])
                t.then_inc(s["attn_turned"], 1)

            def project(g):
                pe.wait_ge(s["attnT_ready"], g + 1)
                reuse(pe, s["x1_ready"], g, g, 1)
                for j in range(GB):
                    t = mm(bank(1)[:, j * P:(j + 1) * P], attnT[:, j * P:(j + 1) * P], W("wo"))
                t.then_inc(s["wo_ready"], 1)

            def turn_x1(g):
                pe.wait_ge(s["x1_ready"], g + 1)
                reuse(pe, s["x1T_ready"], g, g, 1)
                for j in range(GB):
                    t = nc.tensor.transpose(bank(2)[:, j * P:(j + 1) * P], x1[:, j, :], ident[:])
                t.then_inc(s["x1_turned"], 1)

            def turn_xn2(g):
                pe.wait_ge(s["xn2_ready"], GB * g + GB)
                reuse(pe, s["n2T_ready"], GB * g, g, 1)
                for j in range(GB):
                    t = nc.tensor.transpose(bank(3)[:, j * P:(j + 1) * P], xn2[:, j, :], ident[:])
                t.then_inc(s["xn2_turned"], 1)

            def hidden(g, c):
                if c == 0:
                    pe.wait_ge(s["n2T_ready"], GB * g + GB)
                elif c >= 2:
                    pe.wait_ge(s["gelu_ready"], MC * g + c - 1)
                mm(bank(4 + c % 2), W("w1", P, c * P), n2T).then_inc(s["h_ready"], 1)

            def mlp_out(g):
                pe.wait_ge(s["bank6_read"], g + 1)
                for c in range(MC):
                    pe.wait_ge(s["gelu_ready"], MC * g + c + 1)
                    t = mm(bank(6), W("w2", P, c * P), hT[:, c, :], start=(c == 0), stop=(c == MC - 1))
                t.then_inc(s["y_ready"], 1)

            def self_features(g):
                pe.wait_ge(s["x2T_ready"], g + 1)
                mm(psum[0:B, 7, :], ones_col[:], feat_all[:, 0, bass.ts(g, GT)]).then_inc(s["rowsum_ready"], 1)
                mm(bank(6), W("ws"), feat_all[:, 0, bass.ts(g, GT)], stop=False)
                pe.wait_ge(s["nonzero_ready"], g + 1)
                mm(bank(6), q_vec[:], nonzero[:], start=False).then_inc(s["sf_ready"], 1)

            turn_attn(0)
            project(0)
            turn_x1(0)
            turn_xn2(0)
            with pe.Fori(0, NG - 1) as g:
                turn_attn(g + 1)
                hidden(g, 0)
                hidden(g, 1)
                project(g + 1)
                hidden(g, 2)
                hidden(g, 3)
                mlp_out(g)
                turn_x1(g + 1)
                turn_xn2(g + 1)
                self_features(g)
            for c in range(MC):
                hidden(NG - 1, c)
            mlp_out(NG - 1)
            self_features(NG - 1)

            pe.wait_ge(s["attnT_ready"], NG)
            pe.wait_ge(s["x1_ready"], NG)
            pe.wait_ge(s["x1T_ready"], NG)
            pe.wait_ge(s["n2T_ready"], B)
            pe.wait_ge(s["gelu_ready"], MC * NG)
            pe.wait_ge(s["bank6_read"], NG + 1)
            pe.wait_ge(s["nonzero_ready"], NG)

            def queries_and_keys(b):
                reuse(pe, s["gqT_done"], 4 * b, b, 1)
                for d in range(2):
                    mm(bank(0)[:, d * P:(d + 1) * P], W("gq", P, d * P), sfT_all[:, bass.ts(b, P)])
                for d in range(2):
                    t = mm(bank(0)[:, 2 * P + d * M:2 * P + (d + 1) * M], W("gk", P, d * P), sfT_all[:, bass.ds(b * P, M)])
                t.then_inc(s["gq_ready"], 1)

            def turn_weights(b, j):
                pe.wait_ge(s["gw_ready"], b + 1)
                reuse(pe, s["gwT_done"], b, b, 1)
                for d in range(2):
                    for c in range(3):
                        h = CHUNK_HEAD[c]
                        t = nc.tensor.transpose(psum[0:ROWS, 3 + d, c * P:(c + 1) * P], gw[:, j % 2, d, h * M:h * M + ROWS], ident[:])
                t.then_inc(s["gw_turned"], 1)

            def graph_values(b, j):
                pe.wait_ge(s["gwT_done"], b + 1)
                pe.wait_ge(s["vblk_done"], b + 1)
                reuse(pe, s["gnorm_done"], b, b, 1)
                for d in range(2):
                    for c in range(3):
                        first = CHUNK_NEW[c]
                        at = (d * NH + CHUNK_HEAD[c] + first) * (HD + 1)
                        n = (HC - first) * (HD + 1)
                        t = mm(bank(5)[:, at:at + n], gwT[:, (d * 3 + c) * P:(d * 3 + c + 1) * P],
                               v_blocks[:, j % 2, 3 * d + c, first:, :].rearrange("p h d -> p (h d)"))
                t.then_inc(s["gpv_ready"], 1)

            def turn_features(b, j):
                pe.wait_ge(s["feat_copied"], b + 1)
                reuse(pe, s["y_done"], b, b, 1)
                for n in range(2):
                    t = nc.tensor.transpose(bank(1)[:, n * P:(n + 1) * P], feat[:, j, n, :], ident[:])
                t.then_inc(s["fT_ready"], 1)

            def affinities(g, j):
                b = GB * g + j
                pe.wait_ge(s["gqT_done"], 4 * b + 4)
                pe.wait_ge(s["kblk_done"], b + 1)
                reuse(pe, s["aff_masked"], b, b, 1)
                for d in range(2):
                    t = mm(bank(6 + d)[:, 0:NH * M], gqT[:, j, d, :], k_blocks[:, j, d, :])
                t.then_inc(s["aff_ready"], 1)

            def value_projection(b, j):
                pe.wait_ge(s["key_feat_copied"], b + 1)
                reuse(pe, s["vblk_done"], b, b, 1)
                mm(psum[0:ROWS, 2, 0:6 * HC * HD], key_feat[:, j].rearrange("p h m -> p (h m)"),
                   W("gout", 6 * HC * HD)).then_inc(s["vb_ready"], 1)

            def graph_pe_step(g, j):
                b = GB * g + j
                if not known(g) or b < B:
                    affinities(g, j)
                if not known(g) or 1 <= b <= B:
                    value_projection(b - 1, (j - 1) % GB)
                if not known(g) or 3 <= b < B + 3:
                    graph_values(b - 3, (j - 3) % GB)
                if not known(g) or 4 <= b < B + 4:
                    turn_features(b - 4, j)
                if not known(g) or 2 <= b < B + 2:
                    turn_weights(b - 2, (j - 2) % GB)
                if not known(g) or b + 2 < B:
                    queries_and_keys(b + 2)

            queries_and_keys(0)
            queries_and_keys(1)
            for j in range(GB):
                graph_pe_step(0, j)
            with pe.Fori(1, NG - 1) as g:
                for j in range(GB):
                    graph_pe_step(g, j)
            for j in range(2 * GB):
                graph_pe_step(NG - 1 + j // GB, j % GB)


def kernel(**inputs):
    import concourse.bacc as bacc
    from concourse.bass_utils import run_bass_kernel_spmd

    def a(name):
        return np.asarray(inputs[name])

    def dh(v):
        return v.reshape(NH, HD, *v.shape[1:]).swapaxes(0, 1).reshape(v.shape)

    adj = a("mask_BxSxSx11_ik0")
    columns = {
        "wq": dh(a("L0_cond_wq")).T, "wk": dh(a("L0_cond_wk")).T, "wv": a("L0_cond_wv").T,
        "wa1": a("L0_cond_w_adaln1").T, "cond": a("cond_1024").T, "wa2": a("L0_cond_w_adaln2").T,
        "ws": np.concatenate([a("L1_cond_W_self")[:, :P].T, a("L1_cond_W_self")[:, P:].T], axis=1),
        "wo": a("L0_cond_wo").T, "w1": a("L0_cond_w1").T,
        "w2": a("L0_cond_w2").T.reshape(MC, P, P).transpose(1, 0, 2).reshape(P, MC * P),
        "gq": np.concatenate([m.T for m in a("L1_cond_Wq")], axis=1),
        "gk": np.concatenate([m.T for m in a("L1_cond_Wk")], axis=1),
        "gout": np.concatenate([m[h:h + HC].reshape(HC * HD, P).T for m in a("L1_cond_Wout") for h in CHUNK_HEAD], axis=1),
    }
    vectors = {
        "bq": dh(a("L0_cond_bq"))[:, None], "bk": dh(a("L0_cond_bk"))[:, None], "bv": a("L0_cond_bv")[:, None],
        "ba1": a("L0_cond_b_adaln1").reshape(2, P).T, "ba2": a("L0_cond_b_adaln2").reshape(2, P).T,
        "bself": a("L1_cond_b_self")[:, None], "b1": a("L0_cond_b1").reshape(MC, P).T, "b2": a("L0_cond_b2")[:, None],
        "gbq": a("L1_cond_bq").T, "gbk": a("L1_cond_bk").T, "gbout": a("L1_cond_bout").T,
    }
    arrays = {
        "x": a("x"),
        "wall": np.concatenate([columns[n] for n, _ in W_NAMES], axis=1),
        "vecs": np.concatenate([vectors[n] for n, size in V_NAMES if size], axis=1),
        "bo_row": a("L0_cond_bo").reshape(1, P),
        "edge_w": np.concatenate([a("L1_cond_w_bias").reshape(1, L), a("L1_cond_b_bias").reshape(1, 1)], axis=1),
        "mask_cols": np.ascontiguousarray(a("mask_BxS_bf0").T),
        "mask_row": np.ascontiguousarray(a("mask_BxS_bf0").reshape(1, B * P)),
        "adj": np.stack([adj[:, :, :M].transpose(1, 0, 2, 3).reshape(P, B * M * L),
                         adj[:, :M].transpose(2, 0, 1, 3).reshape(P, B * M * L)]),
    }
    nc = bacc.Bacc("TRN2", target_bir_lowering=False, num_devices=1)
    args = []
    for name in arrays:
        v = arrays[name] = np.ascontiguousarray(arrays[name])
        args.append(nc.dram_tensor(f"in_{name}", v.shape, mybir.dt.from_np(v.dtype), kind="ExternalInput").ap())
    out = nc.dram_tensor("out_y", (B, P, P), F32, kind="ExternalOutput").ap()
    build(nc, *args, out)
    r = run_bass_kernel_spmd(nc, [{f"in_{n}": v for n, v in arrays.items()}], core_ids=[0])
    return r.results[0]["out_y"]
```

```python
from contextlib import ExitStack

import numpy as np

import concourse.bass as bass
from concourse import mybir

ALU = mybir.AluOpType
ACT = mybir.ActivationFunctionType
AX = mybir.AxisListType
F32 = mybir.dt.float32
BF16 = mybir.dt.bfloat16
I32 = mybir.dt.int32
U8 = mybir.dt.uint8

P = 128
B = 16
NH = 16
HD = 8
MC = 4
GB = 4
NG = B // GB
GT = GB * P
M = 20
L = 11
HC = 6
CHUNK_HEAD = (0, 6, 10)
CHUNK_NEW = (0, 0, 2)
ROWS = HC * M
QK_SCALE = float(1.0 / np.sqrt(HD))
EPS = 1e-5
NEG = -9000000000000000.0
MASKED = -1e30

NP = NH // 2
Q_PARTS = (0, 0, 1, 1, 0, 2)
K_PARTS = (0, 1, 0, 1, 2, 0)
ROW_MASK = len(Q_PARTS) * 2 * HD
ROW_NEGMAX = ROW_MASK + 1
ROWS_S = ROW_NEGMAX
ROWS_ST = ROW_NEGMAX + 6
N_STACK_Q = len(Q_PARTS)
N_STACK_K = len(K_PARTS) + 1

W_NAMES = (("wq", P), ("wk", P), ("wv", P), ("wa1", 2 * P), ("cond", B), ("wa2", 2 * P), ("ws", 2 * P),
           ("wo", P), ("w1", MC * P), ("w2", MC * P), ("gq", 2 * P), ("gk", 2 * P), ("gout", 6 * HC * HD))
W_AT = {}
_n = 0
for _name, _size in W_NAMES:
    W_AT[_name] = _n
    _n += _size
W_COLS = _n
W_FIRST = W_AT["wo"]
V_NAMES = (("bq", 1), ("bk", 1), ("bv", 1), ("bo", 0), ("ba1", 2), ("ba2", 2), ("bself", 1), ("b1", MC),
           ("b2", 1), ("gbq", 2), ("gbk", 2), ("gbout", 2))
V_AT = {}
_n = 0
for _name, _size in V_NAMES:
    V_AT[_name] = _n
    _n += _size
V_COLS = _n


def build(nc, x, wall, vecs, bo_row, edge_w, row_of_head, mask_cols, mask_row, adj, out):
    with ExitStack() as ctx:
        def sb(name, shape, dt=F32):
            return ctx.enter_context(nc.sbuf_tensor(name, shape, dt))

        def sem(name):
            return ctx.enter_context(nc.semaphore(name))

        psum = ctx.enter_context(nc.psum_tensor("psum", [P, 8, 512], F32))

        w = sb("w", [P, W_COLS])
        vec = sb("vec", [P, V_COLS])
        bo_all = sb("bo_all", [P, P])
        edge_all = sb("edge_all", [P, L + 1])
        mask_c = sb("mask_c", [P, B], U8)
        mask_r = sb("mask_r", [1, B * P], U8)
        mask_neg = sb("mask_neg", [1, B * P], BF16)
        keep = sb("keep", [P, B])
        ident = sb("ident", [P, P])
        ident_bf = sb("ident_bf", [P, P], BF16)
        ones_col = sb("ones_col", [P, B])
        head_mask = sb("head_mask", [P, NH])
        chunk_mask = sb("chunk_mask", [ROWS, HC * HD])
        batch_mask = sb("batch_mask", [B, B * P])
        ones_bf = batch_mask[0:6, 0:B * P // 2].bitcast(BF16)
        minus_half = sb("minus_half", [P, B])
        bq_scaled = sb("bq_scaled", [P, 1])
        gbq_scaled = sb("gbq_scaled", [P, 2])
        bout_sum = sb("bout_sum", [P, 1])
        ada = sb("ada", [P, 4, B])
        q_vec = sb("q_vec", [B, P])

        x_all = sb("x_all", [P, B, P])
        v_mem = sb("v_mem", [P, B * NH * (HD + 1)])
        v_aug = v_mem[:].rearrange("p (b h d) -> p b h d", b=B, h=NH)
        parts = sb("parts", [P, 3, 2, B * P], BF16)
        attn_all = sb("attn_all", [P, B, P])
        sfT_all = v_mem[:, 0:B * P]

        stats = sb("stats", [P, B, 6])
        mean_var = sb("mean_var", [P, B, 2])
        var_eps = sb("var_eps", [P, B])
        carrier = sb("carrier", [P, 1])
        rstd = sb("rstd", [P, B])
        norm_mem = sb("norm_mem", [P, 2 * GT])
        split_mem = sb("split_mem", [P, 4 * GT])
        xn = norm_mem[:, 0:GT].rearrange("p (b d) -> p b d", b=GB)
        nT = norm_mem[:, GT:2 * GT]
        qk32 = split_mem[:, 0:2 * GT].rearrange("p (s t) -> p s t", s=2)
        rest = split_mem[:, 2 * GT:4 * GT].rearrange("p (s t) -> p s t", s=2)
        QSIDE, KSIDE = 2 * NP * GT, 2 * NH * GT
        stack_mem = sb("stack_mem", [P, QSIDE + KSIDE], BF16)
        q_all, k_all = stack_mem[:, 0:QSIDE], stack_mem[:, QSIDE:QSIDE + KSIDE]
        q_stack = q_all.rearrange("r (g p j t) -> r g p j t", g=2, p=NP, j=GB)
        k_mem = sb("k_mem", [P, NP * GT], BF16)
        k_rows = k_mem[0:ROWS_ST, :]
        head_rows = sb("head_rows", [P, 2])
        k_stack = k_all.rearrange("r (g p s j t) -> r g p s j t", g=2, p=NP, s=2, j=GB)
        late_mem = stack_mem[:].bitcast(F32)
        row_max = sb("row_max", [P, NH])
        neg_all = sb("neg_all", [P, P], BF16)
        neg_parts = neg_all[:, 0:3 * NH].rearrange("q (s a p) -> q a p s", s=2, a=3)
        neg_rest = sb("neg_rest", [P, NH])
        pair_max, pair_rest = (t[:].rearrange("q (p s) -> q p s", s=2) for t in (row_max, neg_rest))
        neg_rows = sb("neg_rows", [3 * NH, 2, P], BF16)
        probs_mem = sb("probs_mem", [P, 4 * 512])
        probsT = probs_mem[:].rearrange("p (c t) -> p c t", c=4)
        v_fixed = sb("v_fixed", [P, GB, NH, HD + 1])
        o_rows = norm_mem[:].rearrange("p (j t) -> p j t", j=2)
        den_inv = sb("den_inv", [P, NH])
        attn_g, x_bo, x1, xn2 = (split_mem[:, n * GT:(n + 1) * GT].rearrange("p (b d) -> p b d", b=GB)
                                 for n in range(4))
        attnT = k_mem[:, 0:2 * GT].bitcast(F32)
        n2T = norm_mem[:, GT:2 * GT]
        x1T_all = late_mem[:, 0:B * P]
        feat_all = late_mem[:, B * P:3 * B * P].rearrange("p (a t) -> p a t", a=2)
        hT = probs_mem[:].rearrange("p (c t) -> p c t", c=MC)
        nonzero = sb("nonzero", [B, GT])
        adj_int = sb("adj_int", [P, B * M * L], I32)
        adj_f = sb("adj_f", [P, B * M * L])
        edge_bias = sb("edge_bias", [P, 2, B * M])
        edge_sum = sb("edge_sum", [P, 2, B * M])
        edge_keep = sb("edge_keep", [P, 2, B * M])
        HM = NH * M
        graph_mem = late_mem[:, 3 * B * P:]
        k_blocks = graph_mem[:, 0:8 * HM].rearrange("p (b d n) -> p b d n", b=GB, d=2)
        gw = graph_mem[:, 8 * HM:12 * HM].rearrange("p (b d n) -> p b d n", b=2, d=2)
        aff_b = graph_mem[:, 12 * HM:16 * HM].rearrange("p (b d n) -> p b d n", b=2, d=2)
        feat = graph_mem[:, 16 * HM:16 * HM + GB * 2 * P].rearrange("p (b n t) -> p b n t", b=GB, n=2)
        aff = late_mem[:, 0:4 * HM].rearrange("p (b d n) -> p b d n", b=2, d=2)
        gkT = late_mem[:, 4 * HM:4 * HM + GB * 2 * M].rearrange("p (b d m) -> p b d m", b=GB, d=2)
        aff_c = sb("aff_c", [P, 2, 2, HM])
        gqT = sb("gqT", [P, GB, 2, P])
        key_feat = split_mem[:, 0:GB * HC * M].rearrange("p (b h m) -> p b h m", b=GB, h=HC)
        aff_max = sb("aff_max", [P, 2, 2, NH])
        gwT = probs_mem[0:ROWS, 0:6 * P]
        v_blocks = sb("v_blocks", [ROWS, 2, 6, HC, HD + 1])
        gden_inv = sb("gden_inv", [P, 2 * NH])
        gout_d = probs_mem[:, 6 * P:10 * P].rearrange("p (b d f) -> p b d f", b=2, d=2)
        gout_sum = split_mem[:, 4 * P:6 * P].rearrange("p (b f) -> p b f", b=2)
        g_pre = sb("g_pre", [P, P])
        y_all = attn_all

        names = """x_first_loaded vec_loaded x_loaded edge_added bout_made feat_ready bq_made w_loaded wrest_loaded
            small_loaded ones_made ident_made ident_bf_made masks_made
            head_mask_a chunk_mask_a batch_mask_a keep_made mask_neg_made bias_made ada_ready ada_done qvec_ready bank6_read
            k_rows_in q_stack_in k_stacked stack_ones_in v_fixed_in
            ln1_stats ln1_mv ln1_eps ln1_rstd xn_ready xT_ready nT_ready q_ready k_ready v_ready qk_copied v_done
            keep_col split_hi split_r split_mid split_done
            s_ready max_done neg_zeroed neg_hi neg_r neg_mid neg_done neg_turned neg_copied st_ready exp_done pv_done
            o_zeroed o_copied o_turned den_done norm_done
            attn_g_ready attn_turned attnT_ready wo_ready x_bo_ready x1_ready ln2_stats ln2_mv ln2_eps ln2_rstd
            xn2_ready x1_turned xn2_turned x1T_ready n2T_ready h_ready gelu_ready y_ready x2T_ready rowsum_ready
            nonzero_ready sf_ready
            adj0_loaded adj1_loaded adj_cast edge_prod edge_keep_done edge_neg_done edge_mb_done
            gq_ready gqT_done kblk_done aff_ready aff_masked aff_biased aff_maxed aff_centred gw_ready
            gw_turned gwT_done feat_copied key_feat_copied vb_ready vblk_done gpv_ready fT_ready gden_done
            gnorm_done gsum_done gpre_done y_done""".split()
        s = {n: sem(n) for n in names}
        negmax_in = [sem(f"negmax_in{j}") for j in range(GB)]
        out_done = [sem(f"out_done{j}") for j in range(GB)]

        def W(name, n=P, at=0):
            return w[:, W_AT[name] + at:W_AT[name] + at + n]

        def V(name, n=1, at=0):
            return vec[:, V_AT[name] + at:V_AT[name] + at + n]

        def bank(k):
            return psum[:, k, :]

        def group(t, g):
            return t[:, bass.ts(g, GT)]

        def known(b):
            return isinstance(b, int)

        def reuse(eng, semaphore, value, b, first):
            if not known(b) or b >= first:
                eng.wait_ge(semaphore, value)

        block = ctx.enter_context(nc.Block())

        @block.sync
        def _(sp):
            sp.dma_start(x_all[:, 0:GB, :], x[0:GB].rearrange("b t d -> t b d")).then_inc(s["x_first_loaded"], 16)
            sp.dma_start(w[:, 0:W_FIRST], wall[:, 0:W_FIRST]).then_inc(s["w_loaded"], 16)
            sp.dma_start(x_all[:, GB:, :], x[GB:].rearrange("b t d -> t b d")).then_inc(s["x_loaded"], 16)
            sp.wait_ge(s["ones_made"], 1)
            sp.dma_start(q_all[ROW_MASK:ROW_MASK + 1].rearrange("r (a t) -> r a t", t=B * P),
                         ones_bf[0:1].unsqueeze(1).to_broadcast([1, QSIDE // (B * P), B * P])).then_inc(s["stack_ones_in"], 16)
            sp.dma_start(k_rows[ROW_NEGMAX:ROWS_ST].rearrange("r (a t) -> r a t", t=B * P),
                         ones_bf.unsqueeze(1).to_broadcast([6, NP * GT // (B * P), B * P])).then_inc(s["stack_ones_in"], 16)
            sp.dma_start(adj_int[:], adj[0]).then_inc(s["adj0_loaded"], 16)
            sp.dma_start(w[:, W_FIRST:], wall[:, W_FIRST:]).then_inc(s["wrest_loaded"], 16)
            sp.wait_ge(s["mask_neg_made"], 1)

            def stack_keys(g):
                if g >= 1:
                    sp.wait_ge(s["k_stacked"], 2 * g)
                for n, part in enumerate(K_PARTS):
                    sp.dma_start(k_rows[2 * n * HD:2 * (n + 1) * HD, :].rearrange("r (p t) -> r p t", p=NP),
                                 parts[:, part, 1, bass.ts(g, GT)]).then_inc(s["k_rows_in"], 16)
                sp.dma_start(k_rows[ROW_MASK:ROW_MASK + 1, :].rearrange("r (p t) -> r p t", p=NP),
                             group(mask_neg, g).unsqueeze(1).to_broadcast([1, NP, GT])).then_inc(s["k_rows_in"], 16)

            def stack_queries(g, slots):
                if slots.start == 0:
                    if g >= 1:
                        sp.wait_ge(s["q_stack_in"], 16 * N_STACK_Q * g)
                    if g >= 2:
                        sp.wait_ge(s["st_ready"], 4 * GB * (g - 1))
                for n in slots:
                    sp.dma_start(q_stack[2 * n * HD:2 * (n + 1) * HD, g % 2].rearrange("r p j t -> r p (j t)"),
                                 parts[:, Q_PARTS[n], 0, bass.ts(g, GT)]).then_inc(s["q_stack_in"], 16)

            def negmax(g, j):
                sp.wait_ge(s["neg_copied"], GB * g + j + 1)
                sp.dma_start(q_stack[ROW_NEGMAX:ROWS_ST, g % 2, :, j, :], neg_rows[:, j % 2, :]).then_inc(negmax_in[j], 16)

            for g in range(2):
                sp.wait_ge(s["split_done"], g + 1)
                stack_keys(g)
                stack_queries(g, range(N_STACK_Q))
            sp.wait_ge(s["split_done"], NG)
            for g in range(NG):
                ahead = 1 <= g < NG - 1
                if ahead:
                    stack_keys(g + 1)
                negmax(g, 0)
                if ahead:
                    stack_queries(g + 1, range(0, 2))
                negmax(g, 1)
                if ahead:
                    stack_queries(g + 1, range(2, N_STACK_Q))
                negmax(g, 2)
                negmax(g, 3)

            with sp.Fori(0, NG) as g:
                for j in range(GB):
                    b = GB * g + j
                    sp.wait_ge(s["y_done"], b + 1)
                    sp.dma_start(out[bass.ds(b, 1)].rearrange("b t d -> t b d"), y_all[:, bass.ds(b, 1), :]).then_inc(out_done[j], 16)
            for j in range(GB):
                sp.wait_ge(out_done[j], 16 * NG)

        @block.gpsimd
        def _(pool):
            nc.gpsimd.memset(minus_half[:], -0.5).then_inc(s["masks_made"], 1)
            nc.gpsimd.memset(ident[:], 0.0).then_inc(s["ident_made"], 1)
            pool.wait_ge(s["ident_made"], 1)
            nc.gpsimd.affine_select(out=ident[:], in_=ident[:], compare_op=ALU.not_equal, fill=1.0, base=0,
                                    pattern=[[-1, P]], channel_multiplier=1).then_inc(s["ident_made"], 1)
            pool.wait_ge(s["ident_made"], 2)
            nc.gpsimd.tensor_copy(ident_bf[:], ident[:]).then_inc(s["ident_bf_made"], 1)
            nc.gpsimd.memset(ones_bf, 1.0).then_inc(s["ones_made"], 1)
            nc.gpsimd.memset(neg_all[:], 0.0).then_inc(s["neg_zeroed"], 1)
            pool.wait_ge(s["masks_made"], 1)

            def rstd_of(eps_sem, rstd_sem, g, first=0, end=GB):
                if g is not None:
                    pool.wait_ge(eps_sem, g + 1)
                nc.gpsimd.tensor_tensor(rstd[:, first:end], var_eps[:, first:end], minus_half[:, first:end],
                                        ALU.pow).then_inc(rstd_sem, 1)

            def split_low(g):
                mid, lo = (parts[:, n, :, bass.ts(g, GT)] for n in (1, 2))
                pool.wait_ge(s["split_mid"], g + 1)
                nc.gpsimd.tensor_tensor(lo, rest, mid, ALU.subtract).then_inc(s["split_done"], 1)

            rstd_of(s["ln1_eps"], s["ln1_rstd"], 0)
            pool.wait_ge(s["ln1_eps"], 2)
            for g in range(1, NG):
                rstd_of(s["ln1_eps"], s["ln1_rstd"], None, g * GB, (g + 1) * GB)
            with pool.Fori(0, NG) as g:
                split_low(g)

            pool.wait_ge(s["keep_made"], 1)
            nc.gpsimd.tensor_copy(v_aug[:, :, :, HD], keep[:].unsqueeze(2).to_broadcast([P, B, NH])).then_inc(
                s["keep_col"], 1)

            nc.gpsimd.memset(head_mask[:], 1.0).then_inc(s["head_mask_a"], 1)
            nc.gpsimd.memset(chunk_mask[:], 1.0).then_inc(s["chunk_mask_a"], 1)
            pool.wait_ge(s["stack_ones_in"], 16 * 2)
            nc.gpsimd.memset(batch_mask[:], 1.0).then_inc(s["batch_mask_a"], 1)
            nc.gpsimd.memset(ones_col[:], 1.0).then_inc(s["masks_made"], 1)

            def band(t, sem_a, width, pattern):
                pool.wait_ge(sem_a, 1)
                lo = [[-width * n if n else 0, c] for n, c in pattern]
                nc.gpsimd.affine_select(out=t, in_=t, compare_op=ALU.is_ge, fill=0.0, base=0,
                                        pattern=lo, channel_multiplier=1).then_inc(sem_a, 1)
                pool.wait_ge(sem_a, 2)
                hi = [[width * n if n else 0, c] for n, c in pattern]
                nc.gpsimd.affine_select(out=t, in_=t, compare_op=ALU.is_ge, fill=0.0, base=width - 1,
                                        pattern=hi, channel_multiplier=-1).then_inc(s["masks_made"], 1)

            band(head_mask[:], s["head_mask_a"], HD, [[1, NH]])
            band(chunk_mask[:].rearrange("p (h d) -> p h d", h=HC), s["chunk_mask_a"], M, [[1, HC], [0, HD]])
            band(batch_mask[:].rearrange("p (b t) -> p b t", b=B), s["batch_mask_a"], 1, [[1, B], [0, P]])
            pool.wait_ge(s["masks_made"], 5)
            for j in range(2):
                nc.gpsimd.tensor_copy(
                    v_blocks[:, j, :, :, HD],
                    chunk_mask[:].rearrange("p (h d) -> p h d", h=HC)[:, :, 0].unsqueeze(1).to_broadcast([ROWS, 6, HC])
                ).then_inc(s["masks_made"], 1)

            labels = adj_int[:].bitcast(F32).rearrange("p (e l) -> p e l", l=L)
            terms = adj_f[:].rearrange("p (e l) -> p e l", l=L)
            added = 0

            def add_labels(out, a, b):
                nonlocal added
                if added:
                    pool.wait_ge(s["edge_added"], added)
                nc.gpsimd.tensor_tensor(out, a, b, ALU.add).then_inc(s["edge_added"], 1)
                added += 1

            def add_tree(first, source, total):
                add_labels(terms[:, :, 0:5], first[:, :, 0:5], first[:, :, 5:10])
                add_labels(terms[:, :, 0:2], terms[:, :, 0:2], terms[:, :, 2:4])
                add_labels(terms[:, :, 0], terms[:, :, 0], terms[:, :, 1])
                add_labels(terms[:, :, 4], terms[:, :, 4], source[:, :, 10])
                add_labels(total, terms[:, :, 0], terms[:, :, 4])

            for d in range(2):
                if d:
                    n = B * M * L // 4
                    for i in range(4):
                        pool.dma_start(adj_int[:, i * n:(i + 1) * n], adj[d][:, i * n:(i + 1) * n]).then_inc(s["adj1_loaded"], 16)
                    pool.wait_ge(s["adj1_loaded"], 16 * 4)
                    nc.gpsimd.tensor_copy(adj_int[:].bitcast(F32), adj_int[:]).then_inc(s["adj_cast"], 1)
                pool.wait_ge(s["adj_cast"], d + 1)
                nc.gpsimd.tensor_tensor(terms, labels, edge_all[:, 0:L].unsqueeze(1).to_broadcast([P, B * M, L]),
                                        ALU.mult).then_inc(s["edge_prod"], 1)
                pool.wait_ge(s["edge_prod"], d + 1)
                add_tree(terms, terms, edge_bias[:, d, :])
                add_tree(labels, labels, edge_sum[:, d, :])
                pool.wait_ge(s["edge_added"], added)

            def copy_attn(g):
                pool.wait_ge(s["norm_done"], GB * g + GB)
                reuse(pool, s["attn_turned"], g, g, 1)
                nc.gpsimd.tensor_copy(attn_g, attn_all[:, bass.ts(g, GB), :]).then_inc(s["attn_g_ready"], 1)

            def add_bo(g):
                reuse(pool, s["x1_ready"], g, g, 1)
                nc.gpsimd.tensor_tensor(x_bo, x_all[:, bass.ts(g, GB), :],
                                        bo_all[:].unsqueeze(1).to_broadcast([P, GB, P]), ALU.add).then_inc(s["x_bo_ready"], 1)

            def add_bout(g):
                pool.wait_ge(s["bank6_read"], g + 2)
                nc.gpsimd.tensor_tensor(feat_all[:, 1, bass.ts(g, GT)], group(sfT_all, g), bout_sum[:].to_broadcast([P, GT]),
                                        ALU.add).then_inc(s["feat_ready"], 1)

            pool.wait_ge(s["bout_made"], 1)
            copy_attn(0)
            add_bo(0)
            copy_attn(1)
            rstd_of(s["ln2_eps"], s["ln2_rstd"], 0)
            add_bo(1)
            with pool.Fori(0, NG - 2) as g:
                copy_attn(g + 2)
                rstd_of(s["ln2_eps"], s["ln2_rstd"], g + 1)
                add_bo(g + 2)
                add_bout(g)
            rstd_of(s["ln2_eps"], s["ln2_rstd"], NG - 1)
            add_bout(NG - 2)
            add_bout(NG - 1)

            def add_bias(b, j):
                pool.wait_ge(s["aff_masked"], b + 1)
                reuse(pool, s["aff_centred"], b - 1, b, 2)
                mb = edge_bias[:, :, bass.ds(b * M, M)]
                for d in range(2):
                    nc.gpsimd.tensor_tensor(
                        aff_b[:, j % 2, d, :].rearrange("p (h m) -> p h m", h=NH), aff[:, j % 2, d, :].rearrange("p (h m) -> p h m", h=NH),
                        mb[:, d, :].unsqueeze(1).to_broadcast([P, NH, M]), ALU.add).then_inc(s["aff_biased"], 1)

            def centre(b, j):
                pool.wait_ge(s["aff_maxed"], b + 1)
                reuse(pool, s["gw_ready"], b - 1, b, 2)
                nc.gpsimd.tensor_tensor(
                    aff_c[:, j % 2].rearrange("p d (h m) -> p (d h) m", h=NH), aff_b[:, j % 2].rearrange("p d (h m) -> p (d h) m", h=NH),
                    aff_max[:, j % 2].rearrange("p d h -> p (d h)").unsqueeze(2).to_broadcast([P, 2 * NH, M]),
                    ALU.subtract).then_inc(s["aff_centred"], 1)

            def sum_directions(b, j):
                pool.wait_ge(s["gnorm_done"], b + 1)
                reuse(pool, s["gpre_done"], b - 1, b, 2)
                nc.gpsimd.tensor_tensor(gout_sum[:, j % 2], gout_d[:, j % 2, 0], gout_d[:, j % 2, 1], ALU.add).then_inc(s["gsum_done"], 1)

            def pool_step(g, j):
                b = GB * g + j
                if not known(g) or 2 <= b < B + 2:
                    centre(b - 2, (j - 2) % GB)
                if not known(g) or 1 <= b <= B:
                    add_bias(b - 1, (j - 1) % GB)
                if not known(g) or 4 <= b < B + 4:
                    sum_directions(b - 4, j)

            pool.wait_ge(s["edge_mb_done"], 1)
            for j in range(2 * GB):
                pool_step(j // GB, j % GB)
            with pool.Fori(2, NG) as g:
                for j in range(GB):
                    pool_step(g, j)
            for j in range(GB):
                pool_step(NG, j)

        @block.scalar
        def _(act):
            act.dma_start(vec[:], vecs).then_inc(s["vec_loaded"], 16)
            act.dma_start(head_rows[:], row_of_head).then_inc(s["small_loaded"], 16)
            act.dma_start(mask_c[:], mask_cols).then_inc(s["small_loaded"], 16)
            act.dma_start(mask_r[:], mask_row).then_inc(s["small_loaded"], 16)
            act.dma_start(bo_all[:], bo_row.to_broadcast([P, P])).then_inc(s["small_loaded"], 16)
            act.dma_start(edge_all[:], edge_w.to_broadcast([P, L + 1])).then_inc(s["small_loaded"], 16)
            act.wait_ge(s["vec_loaded"], 16)
            nc.scalar.activation(bq_scaled[:], V("bq"), ACT.Copy, scale=QK_SCALE).then_inc(s["bq_made"], 1)
            act.wait_ge(s["bq_made"], 1)
            act.wait_ge(s["ada_done"], 4)
            act.wait_ge(s["keep_made"], 1)

            def modulate_in(g):
                act.wait_ge(s["xT_ready"], g + 1)
                for j in range(GB):
                    nc.scalar.activation(nT[:, bass.ts(j, P)], psum[:, 0, bass.ts(j, P)], ACT.Identity,
                                         scale=ada[:, 0, bass.ds(g * GB + j, 1)],
                                         bias=ada[:, 1, bass.ds(g * GB + j, 1)]).then_inc(s["nT_ready"], 1)

            def copy_qk(g):
                act.wait_ge(s["q_ready"], g + 1)
                reuse(act, s["split_r"], g, g, 1)
                nc.scalar.activation(qk32[:, 0, :], bank(1), ACT.Identity, scale=QK_SCALE, bias=bq_scaled[:]).then_inc(s["qk_copied"], 1)
                act.wait_ge(s["k_ready"], g + 1)
                nc.scalar.activation(qk32[:, 1, :], bank(2), ACT.Identity, bias=V("bk")).then_inc(s["qk_copied"], 1)

            def copy_v(g):
                act.wait_ge(s["v_ready"], g + 1)
                for j in range(GB):
                    b = g * GB + j
                    nc.scalar.activation(
                        v_aug[:, bass.ds(b, 1), :, 0:HD].rearrange("p b h d -> p (b h) d"),
                        psum[:, 3, bass.ts(j, P)].rearrange("p (h d) -> p h d", h=NH), ACT.Copy,
                        scale=keep[:, bass.ds(b, 1)]).then_inc(s["v_done"], 1)

            modulate_in(0)
            copy_qk(0)
            with act.Fori(0, NG - 1) as g:
                modulate_in(g + 1)
                copy_v(g)
                copy_qk(g + 1)
            copy_v(NG - 1)

            act.wait_ge(s["adj0_loaded"], 16)
            nc.scalar.copy(adj_int[:].bitcast(F32), adj_int[:]).then_inc(s["adj_cast"], 1)

            def fix_values(b, j):
                reuse(act, s["pv_done"], 4 * (b - GB) + 4, b, GB)
                act.wait_ge(s["v_done"], B)
                act.wait_ge(s["keep_col"], 1)
                nc.scalar.copy(v_fixed[:, j], v_aug[:, bass.ds(b, 1)].rearrange("p b h d -> p (b h) d")).then_inc(
                    s["v_fixed_in"], 1)

            def exp(b, c):
                quad = 4 * b + c
                act.wait_ge(s["st_ready"], quad + 1)
                reuse(act, s["pv_done"], quad - 3, b, 1)
                nc.scalar.activation(probsT[:, c, :], bank(6 + c % 2), ACT.Exp).then_inc(s["exp_done"], 1)

            def copy_negmax(g, j):
                b = GB * g + j
                act.wait_ge(s["neg_turned"], b + 1)
                if not known(g) or b >= 2:
                    act.wait_ge(negmax_in[(j - 2) % GB], 16 * (g + (j >= 2)))
                nc.scalar.copy(neg_rows[:, j % 2, :], bank(1)[0:3 * NH, 0:P // 2].bitcast(BF16)).then_inc(s["neg_copied"], 1)

            def copy_values(b, j):
                act.wait_ge(s["pv_done"], 4 * b + 4)
                reuse(act, s["o_turned"], b - 1, b, 2)
                nc.scalar.copy(o_rows[:, j % 2, :], bank(3 * (j % 2))).then_inc(s["o_copied"], 1)

            def act_step(g, j):
                b = GB * g + j
                if not known(g) or 2 <= b < B + 2:
                    exp(b - 2, 0)
                if not known(g) or 1 <= b <= B:
                    copy_negmax(g - (j == 0), (j - 1) % GB)
                if not known(g) or 2 <= b < B + 2:
                    exp(b - 2, 1)
                if not known(g) or 3 <= b < B + 3:
                    copy_values(b - 3, (j - 3) % GB)
                if not known(g) or 1 <= b <= B:
                    fix_values(b - 1, (j - 1) % GB)
                if not known(g) or 2 <= b < B + 2:
                    exp(b - 2, 2)
                    exp(b - 2, 3)

            for j in range(GB):
                act_step(0, j)
            with act.Fori(1, NG) as g:
                for j in range(GB):
                    act_step(g, j)
            for j in range(3):
                act_step(NG, j)

            def modulate(g, at=3):
                act.wait_ge(s["xn2_turned"], g + 1)
                reuse(act, s["h_ready"], MC * g, g, 1)
                for j in range(GB):
                    nc.scalar.activation(n2T[:, bass.ts(j, P)], psum[:, at, bass.ts(j, P)], ACT.Identity,
                                         scale=ada[:, 2, bass.ds(g * GB + j, 1)],
                                         bias=ada[:, 3, bass.ds(g * GB + j, 1)]).then_inc(s["n2T_ready"], 1)

            def gelu(g, c):
                act.wait_ge(s["h_ready"], MC * g + c + 1)
                nc.scalar.activation(hT[:, c, :], bank(4 + c % 2), ACT.Gelu, bias=V("b1", 1, c)).then_inc(s["gelu_ready"], 1)

            def self_features(g):
                act.wait_ge(s["sf_ready"], g + 1)
                nc.scalar.activation(group(sfT_all, g), bank(6), ACT.Identity, bias=V("bself")).then_inc(s["bank6_read"], 1)

            modulate(0, 5)
            with act.Fori(0, NG - 1) as g:
                for c in range(MC):
                    gelu(g, c)
                modulate(g + 1)
                self_features(g)
            for c in range(MC):
                gelu(NG - 1, c)
            self_features(NG - 1)

            def queries_and_keys(g, n):
                e = GB * g + n
                first, d = GB * g + n // 2 * 2, n % 2
                at = n // 2 * 2 % GB
                act.wait_ge(s["gq_ready"], e + 1)
                reuse(act, s["aff_ready"], first - 2, first, GB)
                nc.scalar.activation(gqT[:, at:at + 2, d, :], bank(0)[:, 0:2 * P].rearrange("p (b t) -> p b t", b=2),
                                     ACT.Identity, scale=QK_SCALE, bias=gbq_scaled[:, d:d + 1]).then_inc(s["gqT_done"], 1)
                nc.scalar.activation(gkT[:, at:at + 2, d, :], bank(0)[:, 2 * P:2 * P + 2 * M].rearrange("p (b m) -> p b m", b=2),
                                     ACT.Identity, bias=V("gbk", 1, d)).then_inc(s["gqT_done"], 1)

            def copies(b, j):
                reuse(act, s["fT_ready"], b - GB + 1, b, GB)
                nc.scalar.copy(feat[:, j], feat_all[:, :, bass.ts(b, P)]).then_inc(s["feat_copied"], 1)
                reuse(act, s["vb_ready"], b - GB + 1, b, GB)
                nc.scalar.copy(key_feat[:, j], sfT_all[:, bass.ds(b * P, M)].unsqueeze(1).to_broadcast([P, HC, M])
                                      ).then_inc(s["key_feat_copied"], 1)

            def graph_exp(b, j):
                act.wait_ge(s["aff_centred"], b + 1)
                reuse(act, s["gw_turned"], b - 1, b, 2)
                nc.scalar.activation(gw[:, j % 2], aff_c[:, j % 2], ACT.Exp).then_inc(s["gw_ready"], 1)

            def graph_weights(b, j):
                act.wait_ge(s["gw_turned"], b + 1)
                reuse(act, s["gpv_ready"], b, b, 1)
                nc.scalar.copy(gwT.rearrange("p (d t) -> p d t", d=2),
                               psum[0:ROWS, 3:5, 0:3 * P]).then_inc(s["gwT_done"], 1)

            def graph_act_step(g, j):
                b = GB * g + j
                if not known(g) or 2 <= b < B + 2:
                    graph_exp(b - 2, (j - 2) % GB)
                if not known(g) or b + 3 < B:
                    queries_and_keys(g, j + 3)
                if not known(g) or b < B:
                    copies(b, j)
                if not known(g) or 2 <= b < B + 2:
                    graph_weights(b - 2, (j - 2) % GB)

            act.wait_ge(s["bank6_read"], NG + 1)
            act.wait_ge(s["bias_made"], 1)
            for n in range(3):
                queries_and_keys(0, n)
            act.wait_ge(s["feat_ready"], NG)
            for j in range(GB):
                graph_act_step(0, j)
            with act.Fori(1, NG - 1) as g:
                for j in range(GB):
                    graph_act_step(g, j)
            for j in range(2 * GB):
                graph_act_step(NG - 1 + j // GB, j % GB)

        @block.vector
        def _(dve):

            def layer_stats(src, stats_sem, mv_sem, eps_sem, g):
                for j in range(GB):
                    nc.vector.bn_stats(stats[:, j, :], src(j)).then_inc(stats_sem, 1)
                dve.wait_ge(stats_sem, GB * g + GB)
                nc.vector.memset(carrier[:], 0.0)
                for j in range(GB):
                    nc.vector.bn_aggr(mean_var[:, j, :], stats[:, j, :]).then_inc(mv_sem, 1)
                dve.wait_ge(mv_sem, GB * g + GB)
                nc.vector.tensor_scalar(var_eps[:, 0:GB], mean_var[:, 0:GB, 1], EPS, None, ALU.add).then_inc(eps_sem, 1)

            def normalise(dst, src, ready_sem, first=0):
                for j in range(GB):
                    nc.vector.tensor_scalar(dst[:, j, :], src(j), mean_var[:, bass.ds(first + j, 1), 0], rstd[:, bass.ds(first + j, 1)],
                                            ALU.subtract, ALU.mult).then_inc(ready_sem, 1)

            def batch_of_x(g, j):
                return x_all[:, bass.ds(g * GB + j, 1), :].rearrange("p b d -> p (b d)")

            def ln1(g):
                dve.wait_ge(s["ln1_rstd"], g + 1)
                reuse(dve, s["xT_ready"], g, g, 1)
                normalise(xn, lambda j: batch_of_x(g, j), s["xn_ready"], g * GB)

            def split_high(g):
                dve.wait_ge(s["qk_copied"], 2 * g + 2)
                part = [parts[:, n, :, bass.ts(g, GT)] for n in range(3)]
                nc.vector.tensor_copy(part[0], qk32).then_inc(s["split_hi"], 1)
                dve.wait_ge(s["split_hi"], g + 1)
                reuse(dve, s["split_done"], g, g, 1)
                nc.vector.tensor_tensor(rest, qk32, part[0], ALU.subtract).then_inc(s["split_r"], 1)
                dve.wait_ge(s["split_r"], g + 1)
                nc.vector.tensor_copy(part[1], rest).then_inc(s["split_mid"], 1)

            def spread_keys(g, n):
                slot = (g & 1) if known(g) else dve.snap(g & 1)
                dve.wait_ge(s["k_rows_in"], 16 * N_STACK_K * (g + 1))
                reuse(dve, s["st_ready"], 4 * GB * (g - 1), g, 2)
                nc.vector.tensor_scalar(k_stack[0:ROWS_ST, bass.ds(slot, 1), :, n].rearrange("r g p j t -> r (g p) (j t)"),
                                        k_rows.rearrange("r (p t) -> r p t", p=NP), head_rows[0:ROWS_ST, n:n + 1],
                                        None, ALU.mult).then_inc(s["k_stacked"], 1)

            dve.wait_ge(s["x_first_loaded"], 16)
            layer_stats(lambda j: batch_of_x(0, j), s["ln1_stats"], s["ln1_mv"], s["ln1_eps"], 0)
            ln1(0)
            dve.wait_ge(s["vec_loaded"], 16)
            dve.wait_ge(s["ada_ready"], 4)
            for n, name in enumerate(("ba1", "ba1", "ba2", "ba2")):
                nc.vector.tensor_scalar(ada[:, n, :], bank(7)[:, n * B:(n + 1) * B], V(name, 1, n % 2), 1.0 - n % 2,
                                        ALU.add, ALU.add).then_inc(s["ada_done"], 1)
            dve.wait_ge(s["qvec_ready"], 1)
            nc.vector.tensor_copy(q_vec[:], psum[0:B, 6, 0:P]).then_inc(s["bank6_read"], 1)
            dve.wait_ge(s["small_loaded"], 16 * 5)
            nc.vector.tensor_scalar(keep[:], mask_c[:], -1.0, 1.0, ALU.mult, ALU.add).then_inc(s["keep_made"], 1)
            dve.wait_ge(s["x_loaded"], 16)
            for b in range(GB, B):
                nc.vector.bn_stats(stats[:, b, :], x_all[:, b, :]).then_inc(s["ln1_stats"], 1)
            dve.wait_ge(s["ln1_stats"], B)
            for b in range(GB, B):
                nc.vector.bn_aggr(mean_var[:, b, :], stats[:, b, :]).then_inc(s["ln1_mv"], 1)
            dve.wait_ge(s["ln1_mv"], B)
            nc.vector.tensor_scalar(var_eps[:, GB:], mean_var[:, GB:, 1], EPS, None, ALU.add).then_inc(s["ln1_eps"], 1)
            nc.vector.tensor_scalar(mask_neg[:], mask_r[:], MASKED, None, ALU.mult).then_inc(s["mask_neg_made"], 1)
            nc.vector.tensor_scalar(gbq_scaled[:], V("gbq", 2), QK_SCALE, None, ALU.mult).then_inc(s["bias_made"], 1)
            nc.vector.tensor_scalar(bout_sum[:], V("gbout", 1, 0), V("gbout", 1, 1), None, ALU.add).then_inc(s["bout_made"], 1)
            with dve.Fori(0, NG - 1) as g:
                ln1(g + 1)
                split_high(g)
            dve.wait_ge(s["stack_ones_in"], 16 * 2)
            spread_keys(0, 0)
            spread_keys(0, 1)
            split_high(NG - 1)

            def quad_max(b, c):
                dve.wait_ge(s["s_ready"], 4 * b + c + 1)
                nc.vector.tensor_reduce(row_max[:, 4 * c:4 * c + 4], bank(4 + c % 2).rearrange("p (h k) -> p h k", h=4),
                                        AX.X, ALU.max).then_inc(s["max_done"], 1)

            def split_negmax(b):
                dve.wait_ge(s["max_done"], 4 * b + 4)
                reuse(dve, s["neg_turned"], b, b, 1)
                nc.vector.tensor_scalar(neg_parts[:, 0], pair_max, -1.0, None, ALU.mult).then_inc(s["neg_hi"], 1)
                dve.wait_ge(s["neg_hi"], b + 1)
                nc.vector.scalar_tensor_tensor(pair_rest, pair_max, -1.0, neg_parts[:, 0], ALU.mult,
                                               ALU.subtract).then_inc(s["neg_r"], 1)
                dve.wait_ge(s["neg_r"], b + 1)
                nc.vector.tensor_copy(neg_parts[:, 1], pair_rest).then_inc(s["neg_mid"], 1)
                dve.wait_ge(s["neg_mid"], b + 1)
                nc.vector.tensor_tensor(neg_parts[:, 2], pair_rest, neg_parts[:, 1], ALU.subtract).then_inc(
                    s["neg_done"], 1)

            def attn_normalise(b):
                dve.wait_ge(s["o_turned"], b + 1)
                o = bank(2).rearrange("p (h d) -> p h d", h=NH)
                nc.vector.reciprocal(den_inv[:], o[:, :, HD]).then_inc(s["den_done"], 1)
                dve.wait_ge(s["den_done"], b + 1)
                nc.vector.tensor_tensor(attn_all[:, bass.ds(b, 1), :].rearrange("p b (h d) -> p (b h) d", h=NH), o[:, :, 0:HD],
                                        den_inv[:].unsqueeze(2).to_broadcast([P, NH, HD]), ALU.mult).then_inc(
                                            s["norm_done"], 1)

            def dve_step(g, j):
                b = GB * g + j
                for c in range(4):
                    if not known(g) or b < B:
                        quad_max(b, c)
                    if c == 1 and (not known(g) or 4 <= b < B + 4):
                        attn_normalise(b - 4)
                if not known(g) or b < B:
                    split_negmax(b)

            dve.wait_ge(s["v_done"], B)
            for k in (0, 3):
                nc.vector.memset(bank(k), 0.0).then_inc(s["o_zeroed"], 1)
            dve.wait_ge(s["neg_zeroed"], 1)
            for j in range(GB):
                dve_step(0, j)
                if j < 2:
                    spread_keys(1, j)
            with dve.Fori(1, NG - 1) as g:
                for j in range(GB):
                    dve_step(g, j)
                    if 1 <= j < 3:
                        spread_keys(g + 1, j - 1)
            def attn_out(g, at=0):
                dve.wait_ge(s["attn_turned"], g + 1)
                reuse(dve, s["wo_ready"], g, g, 1)
                nc.vector.tensor_scalar(attnT, bank(at), V("bv"), None, ALU.add).then_inc(s["attnT_ready"], 1)

            def x1_and_norm(g, at=1):
                dve.wait_ge(s["wo_ready"], g + 1)
                dve.wait_ge(s["x_bo_ready"], g + 1)
                reuse(dve, s["x1_turned"], g, g, 1)
                nc.vector.tensor_tensor(x1.rearrange("p b d -> p (b d)"), bank(at), x_bo.rearrange("p b d -> p (b d)"),
                                        ALU.add).then_inc(s["x1_ready"], 1)
                dve.wait_ge(s["x1_ready"], g + 1)
                layer_stats(lambda j: x1[:, j, :], s["ln2_stats"], s["ln2_mv"], s["ln2_eps"], g)
                dve.wait_ge(s["ln2_rstd"], g + 1)
                reuse(dve, s["xn2_turned"], g, g, 1)
                normalise(xn2, lambda j: x1[:, j, :], s["xn2_ready"])

            def copy_x1T(g, at=2):
                dve.wait_ge(s["x1_turned"], g + 1)
                nc.vector.tensor_scalar(group(x1T_all, g), bank(at), V("b2"), None, ALU.add).then_inc(s["x1T_ready"], 1)

            for j in range(GB):
                dve_step(NG - 1, j)
            attn_out(0, 4)
            dve_step(NG, 0)
            dve_step(NG, 1)
            x1_and_norm(0, 5)
            dve_step(NG, 2)
            dve_step(NG, 3)
            copy_x1T(0, 4)

            def x2(g):
                dve.wait_ge(s["y_ready"], g + 1)
                dve.wait_ge(s["x1T_ready"], g + 1)
                nc.vector.tensor_tensor(feat_all[:, 0, bass.ts(g, GT)], bank(6), group(x1T_all, g), ALU.add).then_inc(
                    s["x2T_ready"], 1)

            def nonzero_rows(g):
                dve.wait_ge(s["rowsum_ready"], g + 1)
                nc.vector.scalar_tensor_tensor(nonzero[:], psum[0:B, 7, :], 0.0, group(batch_mask, g), ALU.not_equal,
                                               ALU.mult).then_inc(s["nonzero_ready"], 1)

            with dve.Fori(0, NG - 1) as g:
                attn_out(g + 1)
                x1_and_norm(g + 1)
                x2(g)
                copy_x1T(g + 1)
                nonzero_rows(g)
            dve.wait_ge(s["edge_added"], 20)
            nc.vector.tensor_scalar(edge_keep[:], edge_sum[:], 0.0, None, ALU.is_gt).then_inc(s["edge_keep_done"], 1)
            dve.wait_ge(s["edge_keep_done"], 1)
            nc.vector.tensor_scalar(edge_sum[:], edge_keep[:], -NEG, NEG, ALU.mult, ALU.add).then_inc(s["edge_neg_done"], 1)
            dve.wait_ge(s["edge_neg_done"], 1)
            nc.vector.scalar_tensor_tensor(edge_bias[:], edge_bias[:], edge_all[:, L:L + 1], edge_sum[:], ALU.add,
                                           ALU.add).then_inc(s["edge_mb_done"], 1)

            x2(NG - 1)
            nonzero_rows(NG - 1)

            def key_blocks(g, j):
                b = GB * g + j
                dve.wait_ge(s["gqT_done"], 8 * g + 4 * (j // 2) + 4)
                reuse(dve, s["aff_ready"], b - GB + 1, b, GB)
                nc.vector.tensor_tensor(
                    k_blocks[:, j].rearrange("p d (h m) -> p d h m", h=NH),
                    gkT[:, j].unsqueeze(2).to_broadcast([P, 2, NH, M]),
                    head_mask[:].unsqueeze(1).unsqueeze(3).to_broadcast([P, 2, NH, M]), ALU.mult).then_inc(s["kblk_done"], 1)

            def mask_aff(b, j):
                dve.wait_ge(s["aff_ready"], b + 1)
                reuse(dve, s["aff_biased"], 2 * (b - 2) + 2, b, 2)
                nc.vector.tensor_tensor(
                    aff[:, j % 2].rearrange("p d (h m) -> p d h m", h=NH),
                    psum[:, 6:8, 0:NH * M].rearrange("p d (h m) -> p d h m", h=NH),
                    edge_keep[:, :, bass.ds(b * M, M)].unsqueeze(2).to_broadcast([P, 2, NH, M]), ALU.mult
                ).then_inc(s["aff_masked"], 1)

            def max_aff(b, j):
                dve.wait_ge(s["aff_biased"], 2 * b + 2)
                reuse(dve, s["aff_centred"], b - 1, b, 2)
                nc.vector.tensor_reduce(aff_max[:, j % 2].rearrange("p d h -> p (d h)"),
                                        aff_b[:, j % 2].rearrange("p d (h m) -> p (d h) m", h=NH), AX.X, ALU.max).then_inc(s["aff_maxed"], 1)

            def value_blocks(b, j):
                dve.wait_ge(s["vb_ready"], b + 1)
                reuse(dve, s["gpv_ready"], b - 1, b, 2)
                nc.vector.tensor_tensor(
                    v_blocks[:, j % 2, :, :, 0:HD], psum[0:ROWS, 2, 0:6 * HC * HD].rearrange("p (k h d) -> p k h d", k=6, h=HC),
                    chunk_mask[:].rearrange("p (h d) -> p h d", h=HC).unsqueeze(1).to_broadcast([ROWS, 6, HC, HD]), ALU.mult
                ).then_inc(s["vblk_done"], 1)

            def graph_normalise(b, j):
                dve.wait_ge(s["gpv_ready"], b + 1)
                o = bank(5)[:, 0:2 * NH * (HD + 1)].rearrange("p (h d) -> p h d", h=2 * NH)
                nc.vector.reciprocal(gden_inv[:], o[:, :, HD]).then_inc(s["gden_done"], 1)
                dve.wait_ge(s["gden_done"], b + 1)
                reuse(dve, s["gsum_done"], b - 1, b, 2)
                nc.vector.tensor_tensor(gout_d[:, j % 2].rearrange("p d (h e) -> p (d h) e", h=NH), o[:, :, 0:HD],
                                        gden_inv[:].unsqueeze(2).to_broadcast([P, 2 * NH, HD]), ALU.mult).then_inc(
                                            s["gnorm_done"], 1)

            def finish(b, j):
                dve.wait_ge(s["gsum_done"], b + 1)
                dve.wait_ge(s["fT_ready"], b + 1)
                nc.vector.tensor_tensor(g_pre[:], bank(1)[:, P:2 * P], gout_sum[:, j % 2], ALU.add).then_inc(s["gpre_done"], 1)
                dve.wait_ge(s["gpre_done"], b + 1)
                nc.vector.scalar_tensor_tensor(y_all[:, bass.ds(b, 1), :].rearrange("p b d -> p (b d)"), g_pre[:], 0.0, bank(1)[:, 0:P], ALU.max, ALU.add).then_inc(
                    s["y_done"], 1)

            def graph_dve_step(g, j):
                b = GB * g + j
                if not known(g) or 1 <= b <= B:
                    mask_aff(b - 1, (j - 1) % GB)
                if not known(g) or 4 <= b < B + 4:
                    graph_normalise(b - 4, j)
                if not known(g) or 2 <= b < B + 2:
                    value_blocks(b - 2, (j - 2) % GB)
                if not known(g) or b + 1 < B:
                    key_blocks(g + (j + 1) // GB, (j + 1) % GB)
                if not known(g) or 5 <= b < B + 5:
                    finish(b - 5, (j - 5) % GB)
                if not known(g) or 1 <= b <= B:
                    max_aff(b - 1, (j - 1) % GB)

            dve.wait_ge(s["masks_made"], 5 + 2)
            key_blocks(0, 0)
            for j in range(2 * GB):
                graph_dve_step(j // GB, j % GB)
            with dve.Fori(2, NG - 1) as g:
                for j in range(GB):
                    graph_dve_step(g, j)
            for j in range(2 * GB + 1):
                graph_dve_step(NG - 1 + j // GB, j % GB)

        @block.tensor
        def _(pe):
            def mm(dst, lhsT, rhs, start=True, stop=True):
                return nc.tensor.matmul(dst, lhsT, rhs, start=start, stop=stop)

            pe.wait_ge(s["w_loaded"], 16)
            for n in range(4):
                mm(bank(7)[:, n * B:(n + 1) * B], W(("wa1", "wa2")[n // 2], P, n % 2 * P), W("cond", B)).then_inc(s["ada_ready"], 1)
            mm(psum[0:B, 6, 0:P], W("cond", B), W("ws", P, P)).then_inc(s["qvec_ready"], 1)
            pe.wait_ge(s["ident_made"], 2)
            def project_in(g):
                pe.wait_ge(s["xn_ready"], GB * g + GB)
                for j in range(GB):
                    t = nc.tensor.transpose(bank(0)[:, j * P:(j + 1) * P], xn[:, j, :], ident[:])
                t.then_inc(s["xT_ready"], 1)
                pe.wait_ge(s["nT_ready"], GB * g + GB)
                reuse(pe, s["qk_copied"], 2 * g, g, 1)
                mm(bank(1), W("wq"), nT).then_inc(s["q_ready"], 1)
                mm(bank(2), W("wk"), nT).then_inc(s["k_ready"], 1)
                reuse(pe, s["v_done"], GB * g, g, 1)
                for j in range(GB):
                    t = mm(bank(3)[:, j * P:(j + 1) * P], nT[:, j * P:(j + 1) * P], W("wv"))
                t.then_inc(s["v_ready"], 1)

            project_in(0)
            with pe.Fori(1, NG) as g:
                project_in(g)

            def queries(rows, slot, j, pair):
                return q_stack[0:rows, bass.ds(slot, 1), pair, j, :].rearrange("r g t -> r (g t)")

            def scores(g, j, c):
                quad = 4 * (GB * g + j) + c
                if c == 0 and j == 0:
                    pe.wait_ge(s["q_stack_in"], 16 * N_STACK_Q * (g + 1))
                    pe.wait_ge(s["k_stacked"], 2 * (g + 1))
                reuse(pe, s["max_done"], quad - 1, quad, 2)
                for n in range(2):
                    keys = k_stack[0:ROWS_S, bass.ds(g & 1, 1), 2 * c + n, :, j, :].rearrange("r g s t -> r (g s) t")
                    t = mm(bank(4 + c % 2)[:, 2 * n * P:2 * (n + 1) * P].rearrange("q (s t) -> q s t", s=2),
                           queries(ROWS_S, g & 1, j, 2 * c + n), keys)
                t.then_inc(s["s_ready"], 1)

            def turn_negmax(b):
                pe.wait_ge(s["neg_done"], b + 1)
                reuse(pe, s["neg_copied"], b, b, 1)
                nc.tensor.transpose(bank(1)[:, 0:P // 2].bitcast(BF16), neg_all[:], ident_bf[:]).then_inc(s["neg_turned"], 1)

            def scores_T(g, j, c):
                quad = 4 * (GB * g + j) + c
                if c == 0:
                    pe.wait_ge(negmax_in[j], 16 * (g + 1))
                reuse(pe, s["exp_done"], quad - 1, quad, 2)
                for n in range(4):
                    pair = 2 * c + n // 2
                    keys = k_stack[0:ROWS_ST, bass.ds(g % 2, 1), pair, n % 2, j, :].rearrange("r g t -> r (g t)")
                    t = mm(bank(6 + c % 2)[:, n * P:(n + 1) * P], keys, queries(ROWS_ST, g % 2, j, pair))
                t.then_inc(s["st_ready"], 1)

            def weighted_values(b, j, c):
                pe.wait_ge(s["exp_done"], 4 * b + c + 1)
                if c == 0:
                    pe.wait_ge(s["v_fixed_in"], b + 1)
                    reuse(pe, s["o_copied"], b - 1, b, 2)
                for n in range(4):
                    t = mm(psum[32 * n:32 * n + HD + 1, 3 * (j % 2), c * P:(c + 1) * P], v_fixed[:, j, 4 * c + n, :],
                           probsT[:, c, n * P:(n + 1) * P])
                t.then_inc(s["pv_done"], 1)

            def turn_values(b, j):
                pe.wait_ge(s["o_copied"], b + 1)
                reuse(pe, s["norm_done"], b, b, 1)
                for c in range(4):
                    t = nc.tensor.transpose(bank(2)[:, c * P:(c + 1) * P], o_rows[:, j % 2, c * P:(c + 1) * P], ident[:])
                t.then_inc(s["o_turned"], 1)

            def pe_step(g, j):
                b = GB * g + j
                for c in range(4):
                    if not known(g) or b < B:
                        scores(g, j, c)
                    if not known(g) or 2 <= b < B + 2:
                        scores_T(g - (j < 2), (j - 2) % GB, c)
                    if c == 0:
                        if not known(g) or 3 <= b < B + 3:
                            weighted_values(b - 3, (j - 3) % GB, 3)
                        if not known(g) or 1 <= b <= B:
                            turn_negmax(b - 1)
                    elif not known(g) or 2 <= b < B + 2:
                        weighted_values(b - 2, (j - 2) % GB, c - 1)
                if not known(g) or 3 <= b < B + 3:
                    turn_values(b - 3, (j - 3) % GB)

            pe.wait_ge(s["stack_ones_in"], 16 * 2)
            pe.wait_ge(s["ident_bf_made"], 1)
            pe.wait_ge(s["o_zeroed"], 2)
            for j in range(GB):
                pe_step(0, j)
            with pe.Fori(1, NG) as g:
                for j in range(GB):
                    pe_step(g, j)
            def turn_attn(g, at=0):
                pe.wait_ge(s["attn_g_ready"], g + 1)
                reuse(pe, s["attnT_ready"], g, g, 1)
                for j in range(GB):
                    t = nc.tensor.transpose(bank(at)[:, j * P:(j + 1) * P], attn_g[:, j, :], ident[:])
                t.then_inc(s["attn_turned"], 1)

            def project(g, at=1):
                pe.wait_ge(s["attnT_ready"], g + 1)
                reuse(pe, s["x1_ready"], g, g, 1)
                for j in range(GB):
                    t = mm(bank(at)[:, j * P:(j + 1) * P], attnT[:, j * P:(j + 1) * P], W("wo"))
                t.then_inc(s["wo_ready"], 1)

            def turn_x1(g, at=2):
                pe.wait_ge(s["x1_ready"], g + 1)
                reuse(pe, s["x1T_ready"], g, g, 1)
                for j in range(GB):
                    t = nc.tensor.transpose(bank(at)[:, j * P:(j + 1) * P], x1[:, j, :], ident[:])
                t.then_inc(s["x1_turned"], 1)

            def turn_xn2(g, at=3):
                pe.wait_ge(s["xn2_ready"], GB * g + GB)
                reuse(pe, s["n2T_ready"], GB * g, g, 1)
                for j in range(GB):
                    t = nc.tensor.transpose(bank(at)[:, j * P:(j + 1) * P], xn2[:, j, :], ident[:])
                t.then_inc(s["xn2_turned"], 1)

            pe.wait_ge(s["wrest_loaded"], 16)
            pe.wait_ge(s["max_done"], 4 * B)
            turn_attn(0, 4)
            pe_step(NG, 0)
            project(0, 5)
            pe_step(NG, 1)
            pe_step(NG, 2)
            pe.wait_ge(s["attnT_ready"], 1)
            turn_x1(0, 4)
            turn_xn2(0, 5)

            pe.wait_ge(s["norm_done"], B)
            pe.wait_ge(s["neg_copied"], B)
            pe.wait_ge(s["x1T_ready"], 1)
            pe.wait_ge(s["exp_done"], 4 * B)
            pe.wait_ge(s["masks_made"], 5 + 2)

            def hidden(g, c):
                if c == 0:
                    pe.wait_ge(s["n2T_ready"], GB * g + GB)
                elif c >= 2:
                    pe.wait_ge(s["gelu_ready"], MC * g + c - 1)
                mm(bank(4 + c % 2), W("w1", P, c * P), n2T).then_inc(s["h_ready"], 1)

            def mlp_out(g):
                pe.wait_ge(s["bank6_read"], g + 1)
                for c in range(MC):
                    pe.wait_ge(s["gelu_ready"], MC * g + c + 1)
                    t = mm(bank(6), W("w2", P, c * P), hT[:, c, :], start=(c == 0), stop=(c == MC - 1))
                t.then_inc(s["y_ready"], 1)

            def self_features(g):
                pe.wait_ge(s["x2T_ready"], g + 1)
                mm(psum[0:B, 7, :], ones_col[:], feat_all[:, 0, bass.ts(g, GT)]).then_inc(s["rowsum_ready"], 1)
                mm(bank(6), W("ws"), feat_all[:, 0, bass.ts(g, GT)], stop=False)
                pe.wait_ge(s["nonzero_ready"], g + 1)
                mm(bank(6), q_vec[:], nonzero[:], start=False).then_inc(s["sf_ready"], 1)

            with pe.Fori(0, NG - 1) as g:
                turn_attn(g + 1)
                hidden(g, 0)
                hidden(g, 1)
                project(g + 1)
                hidden(g, 2)
                hidden(g, 3)
                mlp_out(g)
                turn_x1(g + 1)
                turn_xn2(g + 1)
                self_features(g)
            for c in range(MC):
                hidden(NG - 1, c)
            mlp_out(NG - 1)
            self_features(NG - 1)

            pe.wait_ge(s["attnT_ready"], NG)
            pe.wait_ge(s["x1_ready"], NG)
            pe.wait_ge(s["x1T_ready"], NG)
            pe.wait_ge(s["n2T_ready"], B)
            pe.wait_ge(s["gelu_ready"], MC * NG)
            pe.wait_ge(s["bank6_read"], NG + 1)
            pe.wait_ge(s["nonzero_ready"], NG)

            def queries_and_keys(g, n):
                e = GB * g + n
                first, d = GB * g + n // 2 * 2, n % 2
                reuse(pe, s["gqT_done"], 2 * e, e, 1)
                mm(bank(0)[:, 0:2 * P], W("gq", P, d * P), sfT_all[:, bass.ds(first * P, 2 * P)])
                mm(bank(0)[:, 2 * P:2 * P + 2 * M].rearrange("p (b m) -> p b m", b=2), W("gk", P, d * P),
                   sfT_all.rearrange("p (b t) -> p b t", b=B)[:, bass.ds(first, 2), 0:M]).then_inc(s["gq_ready"], 1)

            def turn_weights(b, j):
                pe.wait_ge(s["gw_ready"], b + 1)
                reuse(pe, s["gwT_done"], b, b, 1)
                for d in range(2):
                    for c in range(3):
                        h = CHUNK_HEAD[c]
                        t = nc.tensor.transpose(psum[0:ROWS, 3 + d, c * P:(c + 1) * P], gw[:, j % 2, d, h * M:h * M + ROWS], ident[:])
                t.then_inc(s["gw_turned"], 1)

            def graph_values(b, j):
                pe.wait_ge(s["gwT_done"], b + 1)
                pe.wait_ge(s["vblk_done"], b + 1)
                reuse(pe, s["gnorm_done"], b, b, 1)
                for d in range(2):
                    for c in range(3):
                        first = CHUNK_NEW[c]
                        at = (d * NH + CHUNK_HEAD[c] + first) * (HD + 1)
                        n = (HC - first) * (HD + 1)
                        t = mm(bank(5)[:, at:at + n], gwT[:, (d * 3 + c) * P:(d * 3 + c + 1) * P],
                               v_blocks[:, j % 2, 3 * d + c, first:, :].rearrange("p h d -> p (h d)"))
                t.then_inc(s["gpv_ready"], 1)

            def turn_features(b, j):
                pe.wait_ge(s["feat_copied"], b + 1)
                reuse(pe, s["y_done"], b, b, 1)
                for n in range(2):
                    t = nc.tensor.transpose(bank(1)[:, n * P:(n + 1) * P], feat[:, j, n, :], ident[:])
                t.then_inc(s["fT_ready"], 1)

            def affinities(g, j):
                b = GB * g + j
                pe.wait_ge(s["gqT_done"], 8 * g + 4 * (j // 2) + 4)
                pe.wait_ge(s["kblk_done"], b + 1)
                reuse(pe, s["aff_masked"], b, b, 1)
                for d in range(2):
                    t = mm(bank(6 + d)[:, 0:NH * M], gqT[:, j, d, :], k_blocks[:, j, d, :])
                t.then_inc(s["aff_ready"], 1)

            def value_projection(b, j):
                pe.wait_ge(s["key_feat_copied"], b + 1)
                reuse(pe, s["vblk_done"], b, b, 1)
                mm(psum[0:ROWS, 2, 0:6 * HC * HD], key_feat[:, j].rearrange("p h m -> p (h m)"),
                   W("gout", 6 * HC * HD)).then_inc(s["vb_ready"], 1)

            def graph_pe_step(g, j):
                b = GB * g + j
                if not known(g) or b < B:
                    affinities(g, j)
                if not known(g) or b + 3 < B:
                    queries_and_keys(g, j + 3)
                if not known(g) or 3 <= b < B + 3:
                    graph_values(b - 3, (j - 3) % GB)
                if not known(g) or 4 <= b < B + 4:
                    turn_features(b - 4, j)
                if not known(g) or 1 <= b <= B:
                    value_projection(b - 1, (j - 1) % GB)
                if not known(g) or 2 <= b < B + 2:
                    turn_weights(b - 2, (j - 2) % GB)

            for n in range(3):
                queries_and_keys(0, n)
            for j in range(GB):
                graph_pe_step(0, j)
            with pe.Fori(1, NG - 1) as g:
                for j in range(GB):
                    graph_pe_step(g, j)
            for j in range(2 * GB):
                graph_pe_step(NG - 1 + j // GB, j % GB)


def kernel(**inputs):
    import concourse.bacc as bacc
    from concourse.bass_utils import run_bass_kernel_spmd

    def a(name):
        return np.asarray(inputs[name])

    def dh(v):
        return np.moveaxis(v.reshape(NP, 2, HD, *v.shape[1:]), 0, 2).reshape(v.shape)

    adj = a("mask_BxSxSx11_ik0")
    row = np.arange(P)
    first = np.where(row < ROW_MASK, row // HD % 2 == 0, row < ROW_NEGMAX + 3)
    row_of_head = np.stack([first | (row == ROW_MASK), ~first | (row == ROW_MASK)], axis=1).astype(np.float32)
    columns = {
        "wq": dh(a("L0_cond_wq")).T, "wk": dh(a("L0_cond_wk")).T, "wv": a("L0_cond_wv").T,
        "wa1": a("L0_cond_w_adaln1").T, "cond": a("cond_1024").T, "wa2": a("L0_cond_w_adaln2").T,
        "ws": np.concatenate([a("L1_cond_W_self")[:, :P].T, a("L1_cond_W_self")[:, P:].T], axis=1),
        "wo": a("L0_cond_wo").T, "w1": a("L0_cond_w1").T,
        "w2": a("L0_cond_w2").T.reshape(MC, P, P).transpose(1, 0, 2).reshape(P, MC * P),
        "gq": np.concatenate([m.T for m in a("L1_cond_Wq")], axis=1),
        "gk": np.concatenate([m.T for m in a("L1_cond_Wk")], axis=1),
        "gout": np.concatenate([m[h:h + HC].reshape(HC * HD, P).T for m in a("L1_cond_Wout") for h in CHUNK_HEAD], axis=1),
    }
    vectors = {
        "bq": dh(a("L0_cond_bq"))[:, None], "bk": dh(a("L0_cond_bk"))[:, None], "bv": a("L0_cond_bv")[:, None],
        "ba1": a("L0_cond_b_adaln1").reshape(2, P).T, "ba2": a("L0_cond_b_adaln2").reshape(2, P).T,
        "bself": a("L1_cond_b_self")[:, None], "b1": a("L0_cond_b1").reshape(MC, P).T, "b2": a("L0_cond_b2")[:, None],
        "gbq": a("L1_cond_bq").T, "gbk": a("L1_cond_bk").T, "gbout": a("L1_cond_bout").T,
    }
    arrays = {
        "x": a("x"),
        "wall": np.concatenate([columns[n] for n, _ in W_NAMES], axis=1),
        "vecs": np.concatenate([vectors[n] for n, size in V_NAMES if size], axis=1),
        "bo_row": a("L0_cond_bo").reshape(1, P),
        "edge_w": np.concatenate([a("L1_cond_w_bias").reshape(1, L), a("L1_cond_b_bias").reshape(1, 1)], axis=1),
        "row_of_head": row_of_head,
        "mask_cols": np.ascontiguousarray(a("mask_BxS_bf0").T),
        "mask_row": np.ascontiguousarray(a("mask_BxS_bf0").reshape(1, B * P)),
        "adj": np.stack([adj[:, :, :M].transpose(1, 0, 2, 3).reshape(P, B * M * L),
                         adj[:, :M].transpose(2, 0, 1, 3).reshape(P, B * M * L)]),
    }
    nc = bacc.Bacc("TRN2", target_bir_lowering=False, num_devices=1)
    args = []
    for name in arrays:
        v = arrays[name] = np.ascontiguousarray(arrays[name])
        args.append(nc.dram_tensor(f"in_{name}", v.shape, mybir.dt.from_np(v.dtype), kind="ExternalInput").ap())
    out = nc.dram_tensor("out_y", (B, P, P), F32, kind="ExternalOutput").ap()
    build(nc, *args, out)
    r = run_bass_kernel_spmd(nc, [{f"in_{n}": v for n, v in arrays.items()}], core_ids=[0])
    return r.results[0]["out_y"]
```
